# Optimizing a Trainium2 kernel written in Bass

```python
import numpy as np
import jax
import jax.numpy as jnp

def _softmax(x, axis=-1):
    return jax.nn.softmax(x, axis=axis)

def _gelu(x):
    return jax.nn.gelu(x, approximate=True)

def _silu(x):
    return jax.nn.silu(x)

def _sigmoid(x):
    return jax.nn.sigmoid(x)

def _layernorm(x, axis=-1, eps=1e-05):
    m = jnp.mean(x, axis=axis, keepdims=True)
    v = jnp.var(x, axis=axis, keepdims=True)
    return (x - m) / jnp.sqrt(v + eps)

def _scatter_add(tgt, idx, src, axis=0):
    return tgt.at[idx].add(src)

def _segment_sum(src, seg, n):
    return jax.ops.segment_sum(src, seg, n)
kernel_name = 'mk_hybrid_d2_jaxref_r8_68a1e7'

def setup_inputs(seed: int=0):
    np.random.seed(seed)
    _w = jnp.asarray

    def _L0_attn_a_setup():
        import jax, jax.numpy as jnp
        import numpy as np
        B, S, D = (2, 512, 256)
        H, DK, DV = (16, 128, 128)
        SEG = 64
        UPDATE = 'delta'
        CAUSAL = True
        key = jax.random.key(seed)
        ks = jax.random.split(key, 6)
        s = 0.02
        return {'x': jax.random.normal(ks[0], (B, S, D), jnp.float32), 'Wq': jax.random.normal(ks[1], (D, H * DK), jnp.float32) * s, 'Wk': jax.random.normal(ks[2], (D, H * DK), jnp.float32) * s, 'Wv': jax.random.normal(ks[3], (D, H * DV), jnp.float32) * s, 'Wo': jax.random.normal(ks[4], (H * DV, D), jnp.float32) * s, 'betas': jax.random.normal(ks[5], (1, H, 1, DV), jnp.float32)}
    _L0_attn_a_in = _L0_attn_a_setup()

    def _L0_attn_b_setup():
        import jax, jax.numpy as jnp
        import numpy as np
        N_HEADS = 16
        D_HEAD = 128
        D_MODEL = 256
        MAXLEN = 256
        key = jax.random.key(seed)
        ks = jax.random.split(key, 9)
        b, t = (2, 256)
        hd = N_HEADS * D_HEAD
        init = 0.02
        return {'x': jax.random.normal(ks[0], (b, t, D_MODEL), dtype=jnp.float32), 'Wq': jax.random.normal(ks[1], (D_MODEL, hd), dtype=jnp.float32) * init, 'bq': jnp.zeros((hd,), dtype=jnp.float32), 'Wk': jax.random.normal(ks[2], (D_MODEL, hd), dtype=jnp.float32) * init, 'bk': jnp.zeros((hd,), dtype=jnp.float32), 'Wv': jax.random.normal(ks[3], (D_MODEL, hd), dtype=jnp.float32) * init, 'bv': jnp.zeros((hd,), dtype=jnp.float32), 'Wo': jax.random.normal(ks[4], (hd, D_MODEL), dtype=jnp.float32) * init, 'bo': jnp.zeros((D_MODEL,), dtype=jnp.float32)}
    _L0_attn_b_in = _L0_attn_b_setup()

    def _L0_ffn_setup():
        import jax, jax.numpy as jnp
        import numpy as np
        HIDDEN = 256
        NUM_EXPERTS = 8
        TOP_K = 2
        MOE_INTER = 176
        SHARED_INTER = 704

        def _silu_and_mul(gu):
            i = gu.shape[-1] // 2
            return jax.nn.silu(gu[:, :i]) * gu[:, i:]
        key = jax.random.key(seed)
        ks = jax.random.split(key, 7)
        s = 0.02
        return {'hidden_states': jax.random.normal(ks[0], (2, 256, HIDDEN), dtype=jnp.float32), 'gate_w': jax.random.normal(ks[1], (NUM_EXPERTS, HIDDEN), dtype=jnp.float32) * s, 'shared_gate_w': jax.random.normal(ks[2], (1, HIDDEN), dtype=jnp.float32) * s, 'shared_gate_up_w': jax.random.normal(ks[3], (2 * SHARED_INTER, HIDDEN), dtype=jnp.float32) * s, 'shared_down_w': jax.random.normal(ks[4], (HIDDEN, SHARED_INTER), dtype=jnp.float32) * s, 'w13': jax.random.normal(ks[5], (NUM_EXPERTS, 2 * MOE_INTER, HIDDEN), dtype=jnp.float32) * s, 'w2': jax.random.normal(ks[6], (NUM_EXPERTS, HIDDEN, MOE_INTER), dtype=jnp.float32) * s}
    _L0_ffn_in = _L0_ffn_setup()

    def _L1_attn_a_setup():
        import jax, jax.numpy as jnp
        import numpy as np
        N_EMBD = 256
        Q_HEAD = 16
        KV_HEAD = 4
        HEAD_DIM = N_EMBD // Q_HEAD
        ROPE_BASE = 10000.0

        def _rope(Y, d_rope, base=ROPE_BASE):
            b, h, t, d = Y.shape
            mid = d_rope // 2
            Y1 = Y[:, :mid]
            Y2 = Y[:, mid:]
            Ym1 = jnp.concatenate([Y1, Y2], axis=1)
            Ym2 = jnp.concatenate([-Y2, Y1], axis=1)
            inv = base ** (-2.0 * jnp.arange(d // 2, dtype=jnp.float32) / d)
            theta = jnp.arange(t, dtype=jnp.float32)[:, None] * inv[None, :]
            cos2 = jnp.concatenate([jnp.cos(theta), jnp.cos(theta)], axis=1)
            sin2 = jnp.concatenate([jnp.sin(theta), jnp.sin(theta)], axis=1)
            return Ym1 * cos2 + Ym2 * sin2

        def _attention(x, Wq, bq, Wk, bk, Wv, bv, Wo, bo):
            b, t, n = x.shape
            hd = n // Q_HEAD
            q = x @ Wq.T + bq
            k = x @ Wk.T + bk
            v = x @ Wv.T + bv
            q = q.reshape(b, t, Q_HEAD, hd).transpose(0, 2, 1, 3)
            k = k.reshape(b, t, KV_HEAD, hd).transpose(0, 2, 1, 3)
            v = v.reshape(b, t, KV_HEAD, hd).transpose(0, 2, 1, 3)
            q = _rope(q, N_EMBD)
            k = _rope(k, N_EMBD)
            rep = Q_HEAD // KV_HEAD
            k = jnp.repeat(k, rep, axis=1)
            v = jnp.repeat(v, rep, axis=1)
            scale = jnp.sqrt(jnp.float32(hd))
            att = jnp.einsum('bhqd,bhkd->bhqk', q, k) / scale
            causal = jnp.tril(jnp.ones((t, t), dtype=bool))
            att = jnp.where(causal[None, None], att, -jnp.inf)
            att = jax.nn.softmax(att, axis=-1)
            y = jnp.einsum('bhqt,bhtd->bhqd', att, v)
            y = y.transpose(0, 2, 1, 3).reshape(b, t, n)
            return y @ Wo.T + bo
        key = jax.random.key(seed)
        ks = jax.random.split(key, 9)
        kv_dim = HEAD_DIM * KV_HEAD
        s = 1.0 / np.sqrt(N_EMBD)
        return {'x': jax.random.normal(ks[0], (4, 128, N_EMBD), jnp.float32), 'Wq': jax.random.normal(ks[1], (N_EMBD, N_EMBD), jnp.float32) * s, 'bq': jax.random.normal(ks[2], (N_EMBD,), jnp.float32) * 0.01, 'Wk': jax.random.normal(ks[3], (kv_dim, N_EMBD), jnp.float32) * s, 'bk': jax.random.normal(ks[4], (kv_dim,), jnp.float32) * 0.01, 'Wv': jax.random.normal(ks[5], (kv_dim, N_EMBD), jnp.float32) * s, 'bv': jax.random.normal(ks[6], (kv_dim,), jnp.float32) * 0.01, 'Wo': jax.random.normal(ks[7], (N_EMBD, N_EMBD), jnp.float32) * s, 'bo': jax.random.normal(ks[8], (N_EMBD,), jnp.float32) * 0.01}
    _L1_attn_a_in = _L1_attn_a_setup()

    def _L1_attn_b_setup():
        import jax, jax.numpy as jnp
        import numpy as np
        B, T, C = (4, 256, 256)
        N, K = (16, 4)
        G, H = (N // K, C // N)

        def _rmsnorm(x):
            var = jnp.mean(jnp.square(x.astype(jnp.float32)), axis=-1, keepdims=True)
            return (x * jax.lax.rsqrt(var + 1e-06)).astype(x.dtype)

        def _sine_table(features, length, max_timescale=10000.0):
            fraction = jnp.arange(0, features, 2, dtype=jnp.float32) / features
            timescale = max_timescale ** fraction
            sinusoid = jnp.einsum('i,j->ij', jnp.arange(length).astype(jnp.float32), 1.0 / timescale, precision=jax.lax.Precision.HIGHEST)
            sinusoid = jnp.concatenate([sinusoid, sinusoid], axis=-1)
            return (jnp.sin(sinusoid), jnp.cos(sinusoid))

        def _rotate_half(x):
            x1, x2 = jnp.split(x, 2, axis=-1)
            return jnp.concatenate([-x2, x1], axis=-1)
        key = jax.random.key(seed)
        kx, kq, kk, kv, ko = jax.random.split(key, 5)
        q_std = float(np.sqrt(2.0 / (5.0 * C)))
        o_std = 2.0 / 24 / float(np.sqrt(N * H))
        return {'x': jax.random.normal(kx, (B, T, C), dtype=jnp.float32), 'Wq': jax.random.normal(kq, (C, N * H), dtype=jnp.float32) * q_std, 'Wk': jax.random.normal(kk, (C, K * H), dtype=jnp.float32) * q_std, 'Wv': jax.random.normal(kv, (C, K * H), dtype=jnp.float32) * q_std, 'Wout': jax.random.normal(ko, (N * H, C), dtype=jnp.float32) * o_std}
    _L1_attn_b_in = _L1_attn_b_setup()

    def _L1_ffn_setup():
        import jax, jax.numpy as jnp
        import numpy as np
        from jax import lax
        TOP_K = 2
        N_EXPERTS = 8
        key = jax.random.key(seed)
        ks = jax.random.split(key, 7)
        B, S, H, I, E = (4, 256, 256, 176, N_EXPERTS)
        s_h = 1.0 / np.sqrt(H)
        s_i = 1.0 / np.sqrt(I)
        return {'hidden_states': jax.random.normal(ks[0], (B, S, H), jnp.float32), 'gate_w': jax.random.normal(ks[1], (E, H), jnp.float32) * s_h, 'w1': jax.random.normal(ks[2], (E, H, 2 * I), jnp.float32) * s_h, 'w2': jax.random.normal(ks[3], (E, I, H), jnp.float32) * s_i, 'sw1': jax.random.normal(ks[4], (I, H), jnp.float32) * s_h, 'sw2': jax.random.normal(ks[5], (I, H), jnp.float32) * s_h, 'sw3': jax.random.normal(ks[6], (H, I), jnp.float32) * s_i}
    _L1_ffn_in = _L1_ffn_setup()
    _d = {'L0_attn_a_x': _L0_attn_a_in['x'], 'L0_attn_a_Wq': _L0_attn_a_in['Wq'], 'L0_attn_a_Wk': _L0_attn_a_in['Wk'], 'L0_attn_a_Wv': _L0_attn_a_in['Wv'], 'L0_attn_a_Wo': _L0_attn_a_in['Wo'], 'L0_attn_a_betas': _L0_attn_a_in['betas'], 'L0_attn_b_Wq': _L0_attn_b_in['Wq'], 'L0_attn_b_bq': _L0_attn_b_in['bq'], 'L0_attn_b_Wk': _L0_attn_b_in['Wk'], 'L0_attn_b_bk': _L0_attn_b_in['bk'], 'L0_attn_b_Wv': _L0_attn_b_in['Wv'], 'L0_attn_b_bv': _L0_attn_b_in['bv'], 'L0_attn_b_Wo': _L0_attn_b_in['Wo'], 'L0_attn_b_bo': _L0_attn_b_in['bo'], 'L0_ffn_gate_w': _L0_ffn_in['gate_w'], 'L0_ffn_shared_gate_w': _L0_ffn_in['shared_gate_w'], 'L0_ffn_shared_gate_up_w': _L0_ffn_in['shared_gate_up_w'], 'L0_ffn_shared_down_w': _L0_ffn_in['shared_down_w'], 'L0_ffn_w13': _L0_ffn_in['w13'], 'L0_ffn_w2': _L0_ffn_in['w2'], 'L1_attn_a_Wq': _L1_attn_a_in['Wq'], 'L1_attn_a_bq': _L1_attn_a_in['bq'], 'L1_attn_a_Wk': _L1_attn_a_in['Wk'], 'L1_attn_a_bk': _L1_attn_a_in['bk'], 'L1_attn_a_Wv': _L1_attn_a_in['Wv'], 'L1_attn_a_bv': _L1_attn_a_in['bv'], 'L1_attn_a_Wo': _L1_attn_a_in['Wo'], 'L1_attn_a_bo': _L1_attn_a_in['bo'], 'L1_attn_b_Wq': _L1_attn_b_in['Wq'], 'L1_attn_b_Wk': _L1_attn_b_in['Wk'], 'L1_attn_b_Wv': _L1_attn_b_in['Wv'], 'L1_attn_b_Wout': _L1_attn_b_in['Wout'], 'L1_ffn_gate_w': _L1_ffn_in['gate_w'], 'L1_ffn_w1': _L1_ffn_in['w1'], 'L1_ffn_w2': _L1_ffn_in['w2'], 'L1_ffn_sw1': _L1_ffn_in['sw1'], 'L1_ffn_sw2': _L1_ffn_in['sw2'], 'L1_ffn_sw3': _L1_ffn_in['sw3']}
    _x0 = _d['L0_attn_a_x']
    _d['L0_attn_a_x'] = jax.random.normal(jax.random.fold_in(jax.random.key(seed), 1), (2, 512, 256), dtype=_x0.dtype)
    del _x0
    return _d

def reference(L0_attn_a_x, L0_attn_a_Wq, L0_attn_a_Wk, L0_attn_a_Wv, L0_attn_a_Wo, L0_attn_a_betas, L0_attn_b_Wq, L0_attn_b_bq, L0_attn_b_Wk, L0_attn_b_bk, L0_attn_b_Wv, L0_attn_b_bv, L0_attn_b_Wo, L0_attn_b_bo, L0_ffn_gate_w, L0_ffn_shared_gate_w, L0_ffn_shared_gate_up_w, L0_ffn_shared_down_w, L0_ffn_w13, L0_ffn_w2, L1_attn_a_Wq, L1_attn_a_bq, L1_attn_a_Wk, L1_attn_a_bk, L1_attn_a_Wv, L1_attn_a_bv, L1_attn_a_Wo, L1_attn_a_bo, L1_attn_b_Wq, L1_attn_b_Wk, L1_attn_b_Wv, L1_attn_b_Wout, L1_ffn_gate_w, L1_ffn_w1, L1_ffn_w2, L1_ffn_sw1, L1_ffn_sw2, L1_ffn_sw3):

    def _L0_attn_a_ref(x, Wq, Wk, Wv, Wo, betas):
        import jax, jax.numpy as jnp
        import numpy as np
        B, S, D = (2, 512, 256)
        H, DK, DV = (16, 128, 128)
        SEG = 64
        UPDATE = 'delta'
        CAUSAL = True
        Bsz, seq, _ = x.shape
        nseg = seq // SEG
        q = (x @ Wq).reshape(Bsz, seq, H, DK).transpose(0, 2, 1, 3)
        k = (x @ Wk).reshape(Bsz, seq, H, DK).transpose(0, 2, 1, 3)
        v = (x @ Wv).reshape(Bsz, seq, H, DV).transpose(0, 2, 1, 3)
        qs = q.reshape(Bsz, H, nseg, SEG, DK).transpose(2, 0, 1, 3, 4)
        ks_ = k.reshape(Bsz, H, nseg, SEG, DK).transpose(2, 0, 1, 3, 4)
        vs = v.reshape(Bsz, H, nseg, SEG, DV).transpose(2, 0, 1, 3, 4)
        causal_mask = jnp.tril(jnp.ones((SEG, SEG), bool))
        scale = DK ** 0.5
        beta = jax.nn.sigmoid(betas)

        def step(carry, seg):
            mem, z = carry
            qq, kk, vv = seg
            sigma_q = jax.nn.elu(qq) + 1.0
            scores = jnp.einsum('bhsk,bhtk->bhst', qq, kk) / scale
            if CAUSAL:
                scores = jnp.where(causal_mask, scores, -jnp.inf)
            att_dot = jax.nn.softmax(scores, axis=-1) @ vv
            att_mem = sigma_q @ mem / (sigma_q @ z)
            sigma_k = jax.nn.elu(kk) + 1.0
            if UPDATE == 'linear':
                mem_new = mem + jnp.einsum('bhsk,bhsv->bhkv', sigma_k, vv)
            else:
                delta = vv - sigma_k @ mem / (sigma_k @ z)
                mem_new = mem + jnp.einsum('bhsk,bhsv->bhkv', sigma_k, delta)
            z_new = z + sigma_k.sum(axis=-2, keepdims=True).transpose(0, 1, 3, 2)
            att = beta * att_mem + (1.0 - beta) * att_dot
            out = att.reshape(Bsz, SEG, H * DV) @ Wo
            return ((mem_new, z_new), out)
        mem0 = jnp.zeros((Bsz, H, DK, DV), x.dtype)
        z0 = jnp.ones((Bsz, H, DK, 1), x.dtype) / DK
        _, outs = jax.lax.scan(step, (mem0, z0), (qs, ks_, vs))
        return outs.transpose(1, 0, 2, 3).reshape(Bsz, seq, D)

    def _L0_attn_b_ref(x, Wq, bq, Wk, bk, Wv, bv, Wo, bo):
        import jax, jax.numpy as jnp
        import numpy as np
        N_HEADS = 16
        D_HEAD = 128
        D_MODEL = 256
        MAXLEN = 256
        b, t, _ = x.shape
        h, dh = (N_HEADS, D_HEAD)
        scale = 1.0 / np.sqrt(dh).astype(np.float32)
        q = (x @ Wq + bq).reshape(b, h, t, dh)
        k = (x @ Wk + bk).reshape(b, t, h, dh).transpose(0, 2, 3, 1)
        v = (x @ Wv + bv).reshape(b, t, h, dh).transpose(0, 2, 1, 3)
        logits = jnp.einsum('bhtd,bhds->bhts', q, k) * scale
        mask = jnp.triu(jnp.full((t, t), -jnp.inf, dtype=x.dtype), k=1)
        weights = jax.nn.softmax(logits + mask, axis=-1)
        out = jnp.einsum('bhts,bhsd->bhtd', weights, v)
        out = out.transpose(0, 2, 1, 3).reshape(b, t, h * dh)
        return out @ Wo + bo

    def _L0_ffn_ref(hidden_states, gate_w, shared_gate_w, shared_gate_up_w, shared_down_w, w13, w2):
        import jax, jax.numpy as jnp
        import numpy as np
        HIDDEN = 256
        NUM_EXPERTS = 8
        TOP_K = 2
        MOE_INTER = 176
        SHARED_INTER = 704

        def _silu_and_mul(gu):
            i = gu.shape[-1] // 2
            return jax.nn.silu(gu[:, :i]) * gu[:, i:]
        orig_shape = hidden_states.shape
        x = hidden_states.reshape(-1, orig_shape[-1])
        shared = _silu_and_mul(x @ shared_gate_up_w.T) @ shared_down_w.T
        shared = shared * jax.nn.sigmoid(x @ shared_gate_w.T)
        router_logits = x @ gate_w.T
        probs = jax.nn.softmax(router_logits.astype(jnp.float32), axis=-1)
        routing_weights, selected_experts = jax.lax.top_k(probs, TOP_K)
        combined = jnp.zeros(x.shape, dtype=jnp.float32)
        E = w13.shape[0]
        for e in range(E):
            w_e = jnp.where(selected_experts == e, routing_weights, 0.0).sum(-1)
            h = _silu_and_mul(x @ w13[e].T) @ w2[e].T
            combined = combined + w_e[:, None] * h.astype(jnp.float32)
        out = shared + combined.astype(x.dtype)
        return out.reshape(orig_shape)

    def _L1_attn_a_ref(x, Wq, bq, Wk, bk, Wv, bv, Wo, bo):
        import jax, jax.numpy as jnp
        import numpy as np
        N_EMBD = 256
        Q_HEAD = 16
        KV_HEAD = 4
        HEAD_DIM = N_EMBD // Q_HEAD
        ROPE_BASE = 10000.0

        def _rope(Y, d_rope, base=ROPE_BASE):
            b, h, t, d = Y.shape
            mid = d_rope // 2
            Y1 = Y[:, :mid]
            Y2 = Y[:, mid:]
            Ym1 = jnp.concatenate([Y1, Y2], axis=1)
            Ym2 = jnp.concatenate([-Y2, Y1], axis=1)
            inv = base ** (-2.0 * jnp.arange(d // 2, dtype=jnp.float32) / d)
            theta = jnp.arange(t, dtype=jnp.float32)[:, None] * inv[None, :]
            cos2 = jnp.concatenate([jnp.cos(theta), jnp.cos(theta)], axis=1)
            sin2 = jnp.concatenate([jnp.sin(theta), jnp.sin(theta)], axis=1)
            return Ym1 * cos2 + Ym2 * sin2

        def _attention(x, Wq, bq, Wk, bk, Wv, bv, Wo, bo):
            b, t, n = x.shape
            hd = n // Q_HEAD
            q = x @ Wq.T + bq
            k = x @ Wk.T + bk
            v = x @ Wv.T + bv
            q = q.reshape(b, t, Q_HEAD, hd).transpose(0, 2, 1, 3)
            k = k.reshape(b, t, KV_HEAD, hd).transpose(0, 2, 1, 3)
            v = v.reshape(b, t, KV_HEAD, hd).transpose(0, 2, 1, 3)
            q = _rope(q, N_EMBD)
            k = _rope(k, N_EMBD)
            rep = Q_HEAD // KV_HEAD
            k = jnp.repeat(k, rep, axis=1)
            v = jnp.repeat(v, rep, axis=1)
            scale = jnp.sqrt(jnp.float32(hd))
            att = jnp.einsum('bhqd,bhkd->bhqk', q, k) / scale
            causal = jnp.tril(jnp.ones((t, t), dtype=bool))
            att = jnp.where(causal[None, None], att, -jnp.inf)
            att = jax.nn.softmax(att, axis=-1)
            y = jnp.einsum('bhqt,bhtd->bhqd', att, v)
            y = y.transpose(0, 2, 1, 3).reshape(b, t, n)
            return y @ Wo.T + bo
        return _attention(x, Wq, bq, Wk, bk, Wv, bv, Wo, bo)

    def _L1_attn_b_ref(x, Wq, Wk, Wv, Wout):
        import jax, jax.numpy as jnp
        import numpy as np
        B, T, C = (4, 256, 256)
        N, K = (16, 4)
        G, H = (N // K, C // N)

        def _rmsnorm(x):
            var = jnp.mean(jnp.square(x.astype(jnp.float32)), axis=-1, keepdims=True)
            return (x * jax.lax.rsqrt(var + 1e-06)).astype(x.dtype)

        def _sine_table(features, length, max_timescale=10000.0):
            fraction = jnp.arange(0, features, 2, dtype=jnp.float32) / features
            timescale = max_timescale ** fraction
            sinusoid = jnp.einsum('i,j->ij', jnp.arange(length).astype(jnp.float32), 1.0 / timescale, precision=jax.lax.Precision.HIGHEST)
            sinusoid = jnp.concatenate([sinusoid, sinusoid], axis=-1)
            return (jnp.sin(sinusoid), jnp.cos(sinusoid))

        def _rotate_half(x):
            x1, x2 = jnp.split(x, 2, axis=-1)
            return jnp.concatenate([-x2, x1], axis=-1)
        b, t, c = x.shape
        q = _rmsnorm(x @ Wq)
        k = _rmsnorm(x @ Wk)
        v = x @ Wv
        q = q.reshape(b, t, K, G, H)
        k = k.reshape(b, t, K, H)
        v = v.reshape(b, t, K, H)
        sin, cos = _sine_table(H, t)
        qcos, qsin = (cos[None, :, None, None, :], sin[None, :, None, None, :])
        kcos, ksin = (cos[None, :, None, :], sin[None, :, None, :])
        q = (q * qcos + _rotate_half(q) * qsin).astype(q.dtype)
        k = (k * kcos + _rotate_half(k) * ksin).astype(k.dtype)
        scale = jax.lax.rsqrt(jnp.array(H, dtype=jnp.float32)).astype(q.dtype)
        q = q * scale
        logits = jnp.einsum('btkgh,bskh->bkgts', q, k)
        probs = jax.nn.softmax(logits.astype(jnp.float32), axis=-1).astype(logits.dtype)
        enc = jnp.einsum('bkgts,bskh->btkgh', probs, v)
        return enc.reshape(b, t, N * H) @ Wout

    def _L1_ffn_ref(hidden_states, gate_w, w1, w2, sw1, sw2, sw3):
        import jax, jax.numpy as jnp
        import numpy as np
        from jax import lax
        TOP_K = 2
        N_EXPERTS = 8
        B, S, H = hidden_states.shape
        x = hidden_states.reshape(-1, H)
        T = x.shape[0]
        logits = jnp.einsum('th,eh->te', x.astype(jnp.float32), gate_w.astype(jnp.float32))
        scores = jax.nn.softmax(logits, axis=-1)
        topk_w, topk_idx = lax.top_k(scores, TOP_K)
        topk_w = topk_w / (topk_w.sum(-1, keepdims=True) + 1e-20)
        topk_w = topk_w.astype(hidden_states.dtype)
        cw = jnp.zeros((T, N_EXPERTS), hidden_states.dtype).at[jnp.arange(T)[:, None], topk_idx].add(topk_w)

        def body(acc, ew):
            w1e, w2e, cwe = ew
            h = x @ w1e
            g, u = jnp.split(h, 2, axis=-1)
            y = jax.nn.silu(g) * u @ w2e
            return (acc + cwe[:, None] * y, None)
        moe, _ = lax.scan(body, jnp.zeros_like(x), (w1, w2, cw.T))
        moe = moe.reshape(B, S, H)
        shared = jnp.einsum('bsi,hi->bsh', jax.nn.silu(jnp.einsum('bsh,ih->bsi', hidden_states, sw1)) * jnp.einsum('bsh,ih->bsi', hidden_states, sw2), sw3)
        return moe + shared
    x = L0_attn_a_x
    x = x + _L0_attn_a_ref(_layernorm(x, axis=-1), L0_attn_a_Wq, L0_attn_a_Wk, L0_attn_a_Wv, L0_attn_a_Wo, L0_attn_a_betas)
    x = x + _L0_ffn_ref(_layernorm(x, axis=-1), L0_ffn_gate_w, L0_ffn_shared_gate_w, L0_ffn_shared_gate_up_w, L0_ffn_shared_down_w, L0_ffn_w13, L0_ffn_w2)
    x = x + _L0_attn_b_ref(_layernorm(x, axis=-1), L0_attn_b_Wq, L0_attn_b_bq, L0_attn_b_Wk, L0_attn_b_bk, L0_attn_b_Wv, L0_attn_b_bv, L0_attn_b_Wo, L0_attn_b_bo)
    x = x + _L0_ffn_ref(_layernorm(x, axis=-1), L0_ffn_gate_w, L0_ffn_shared_gate_w, L0_ffn_shared_gate_up_w, L0_ffn_shared_down_w, L0_ffn_w13, L0_ffn_w2)
    x = x + _L1_attn_a_ref(_layernorm(x, axis=-1), L1_attn_a_Wq, L1_attn_a_bq, L1_attn_a_Wk, L1_attn_a_bk, L1_attn_a_Wv, L1_attn_a_bv, L1_attn_a_Wo, L1_attn_a_bo)
    x = x + _L1_ffn_ref(_layernorm(x, axis=-1), L1_ffn_gate_w, L1_ffn_w1, L1_ffn_w2, L1_ffn_sw1, L1_ffn_sw2, L1_ffn_sw3)
    x = x + _L1_attn_b_ref(_layernorm(x, axis=-1), L1_attn_b_Wq, L1_attn_b_Wk, L1_attn_b_Wv, L1_attn_b_Wout)
    x = x + _L1_ffn_ref(_layernorm(x, axis=-1), L1_ffn_gate_w, L1_ffn_w1, L1_ffn_w2, L1_ffn_sw1, L1_ffn_sw2, L1_ffn_sw3)
    return x

_drawn_inputs = setup_inputs


def setup_inputs(seed=0):
    import zlib

    import numpy as np

    out = dict(_drawn_inputs(seed))
    spreads = {'L0_attn_b_bq': (0.0, 0.612),
     'L0_attn_b_bk': (0.0, 0.8),
     'L0_attn_b_bv': (0.0, 0.1),
     'L0_attn_b_bo': (0.0, 0.1)}
    factors = {'L0_attn_a_Wq': 3.292,
     'L0_attn_a_Wk': 3.156,
     'L0_attn_b_Wq': 2.978,
     'L0_attn_b_Wk': 3.066,
     'L0_ffn_shared_gate_w': 2.686,
     'L1_attn_a_bq': 5.435,
     'L1_attn_a_bk': 5.462,
     'L1_attn_b_Wq': 6.552,
     'L1_attn_b_Wk': 8.0,
     'L1_attn_b_Wv': 3.584,
     'L1_attn_b_Wout': 3.434}
    for name, (base, spread) in spreads.items():
        noise = np.random.default_rng([zlib.crc32(name.encode()), seed]).standard_normal(out[name].shape)
        drawn = base * np.exp(spread * noise) if base else spread * noise
        out[name] = jnp.asarray(drawn.astype(out[name].dtype))
    for name, factor in factors.items():
        out[name] = (out[name] * factor).astype(out[name].dtype)
    return out
```

```python
import itertools
from contextlib import ExitStack

import concourse.bass as bass
from concourse import mybir

ALU = mybir.AluOpType
ACT = mybir.ActivationFunctionType
AX = mybir.AxisListType
F32 = mybir.dt.float32
F32R = mybir.dt.float32r
BF16 = mybir.dt.bfloat16
U32 = mybir.dt.uint32

P = 128
B, S, D = 2, 512, 256
TOK = B * S
NT = TOK // P
TB = S // P
DC = D // P
HALF = 512
NHALF = TOK // HALF
LN_EPS = 1e-5
NEG = -1e30

N_EXP, TOP_K, INTER = 8, 2, 176
SHARED0, SHARED1 = 704, 176
GATES = 10
W_SEL, W_GATE, W_UP = 0, P, P + DC * P
W_DOWN = P + 2 * DC * P
FFN_COLS = W_DOWN + D


def f32(ap):
    return ap.bitcast(F32)


def spread(ap, n):
    return ap.unsqueeze(len(ap.shape)).broadcast_to([*ap.shape, n])


class Chain:

    def __init__(self, engine, sem):
        self.engine, self.sem, self.n = engine, sem, 0

    def __call__(self, instruction):
        self.n += 1
        instruction.then_inc(self.sem, 1)
        self.engine.wait_ge(self.sem, self.n)


def product(pe, out, stationary, moving, first, last):
    (sh, sl), (mh, ml) = stationary, moving
    pe.matmul(out, sh, mh, start=first, stop=False, skip_group_check=True)
    pe.matmul(out, sh, ml, start=False, stop=False, skip_group_check=True)
    return pe.matmul(out, sl, mh, start=False, stop=last, skip_group_check=True)


class Semaphores:

    def __init__(self, nc, name):
        self.nc, self.name, self.all = nc, name, []

    def __call__(self, what):
        self.all.append(self.nc.alloc_semaphore(f"{self.name}_{what}"))
        return self.all[-1]

    def __enter__(self):
        return self

    def __exit__(self, *_):
        self.nc.clear_and_free_semaphores(self.all)
        self.nc.all_engine_barrier()


class Norm:

    def __init__(self, nc, ctx, sem, name, res, banks, xn=None):
        sb = lambda what, shape: ctx.enter_context(nc.sbuf_tensor(f"{name}_{what}", shape, F32))
        self.res, self.banks = res, banks
        self.stats, self.moments = sb("stats", [P, NT, 6]), sb("moments", [P, NT, 2])
        self.var, self.power, self.rstd = sb("var", [P, NT]), sb("power", [P, NT]), sb("rstd", [P, NT])
        self.xn = sb("xn", [P, NT, D]) if xn is None else xn
        self.stats_done, self.moments_done = sem("ln_stats_done"), sem("ln_moments_done")
        self.pool_step, self.rstd_done = sem("ln_pool_step"), sem("ln_rstd_done")
        self.normed, self.turned = sem("ln_normed"), sem("ln_turned")
        self.hi_done, self.lo_done = sem("ln_xn_hi_done"), sem("ln_xn_lo_done")

    def vector(self, dve):
        x = self.res.x
        for t in range(NT):
            dve.bn_stats(self.stats[:, t, :], x[:, t, :]).then_inc(self.stats_done, 1)
        for t in range(NT):
            dve.wait_ge(self.stats_done, t + 1)
            dve.bn_aggr(self.moments[:, t, :], self.stats[:, t, :]).then_inc(self.moments_done, 1)
        dve.wait_ge(self.rstd_done, 1)
        for t in range(NT):
            dve.tensor_scalar(self.xn[:, t, :], x[:, t, :], self.moments[:, t, 0:1], self.rstd[:, t:t + 1],
                              ALU.subtract, ALU.mult).then_inc(self.normed, 1)
        for k in range(NHALF * DC):
            h, c = divmod(k, DC)
            at = slice(h * HALF, (h + 1) * HALF)
            dve.wait_ge(self.hi_done, k + 1)
            dve.tensor_tensor(self.res.xl[:, c, at], self.banks[k], f32(self.res.xh[:, c, at]),
                              ALU.subtract).then_inc(self.lo_done, 1)

    def gpsimd(self, pool):
        pool.memset(self.power[:], -0.5).then_inc(self.pool_step, 1)
        pool.wait_ge(self.moments_done, NT)
        pool.tensor_scalar(self.var[:], self.moments[:, :, 1], LN_EPS, None, ALU.add).then_inc(self.pool_step, 1)
        pool.wait_ge(self.pool_step, 2)
        pool.tensor_tensor(self.rstd[:], self.var[:], self.power[:], ALU.pow).then_inc(self.rstd_done, 1)

    def tensor(self, pe):
        for k in range(NHALF * DC):
            h, c = divmod(k, DC)
            pe.wait_ge(self.normed, (h + 1) * TB)
            for j in range(TB):
                last = pe.transpose(self.banks[k][:, j * P:(j + 1) * P],
                                    self.xn[:, h * TB + j, c * P:(c + 1) * P], self.res.ident[:])
            last.then_inc(self.turned, 1)

    def scalar(self, act):
        for k in range(NHALF * DC):
            h, c = divmod(k, DC)
            act.wait_ge(self.turned, k + 1)
            act.activation(self.res.xh[:, c, h * HALF:(h + 1) * HALF], self.banks[k],
                           ACT.Copy).then_inc(self.hi_done, 1)


def ffn_stage(nc, name, res, weights, gate_w, owner_is_gated, renormalise):
    n_chunks = weights.shape[0]
    with ExitStack() as ctx:
        sem = ctx.enter_context(Semaphores(nc, name))
        sb = lambda what, shape, dt=F32: ctx.enter_context(nc.sbuf_tensor(f"{name}_{what}", shape, dt))
        banks = [ctx.enter_context(nc.psum_tensor(f"{name}_bank{i}", [P, HALF], F32)) for i in range(8)]
        acc = banks[:4]
        gate_bank = (banks[4], banks[6])
        up_bank = (banks[5], banks[7])
        norm = Norm(nc, ctx, sem, f"{name}_ln", res, [b[:] for b in banks[4:8]])

        w_raw = sb("w_raw", [P, 2, FFN_COLS])
        w_hi, w_lo = sb("w_hi", [P, 2, FFN_COLS], F32R), sb("w_lo", [P, 2, FFN_COLS], F32R)
        gate_raw = sb("gate_raw", [P, DC, GATES])
        gate_hi, gate_lo = sb("gate_hi", [P, DC, GATES], F32R), sb("gate_lo", [P, DC, GATES], F32R)
        logits, shifted = sb("logits", [P, NT, GATES]), sb("shifted", [P, NT, N_EXP])
        probs, row_max, row_sum = sb("probs", [P, NT, N_EXP]), sb("row_max", [P, NT]), sb("row_sum", [P, NT])
        gate_exp = sb("gate_exp", [P, NT])
        top8, at8 = sb("top8", [P, NT, 8]), sb("at8", [P, NT, 8], U32)
        at_f, iota = sb("at_f", [P, NT, TOP_K]), res.iota
        first_hit, second_hit = sb("first_hit", [P, NT, N_EXP]), sb("second_hit", [P, NT, N_EXP])
        token_w = sb("token_w", [P, NT, 16])
        tw_hi, tw_lo = sb("tw_hi", [16, TOK], F32R), sb("tw_lo", [16, TOK], F32R)
        silu = sb("silu", [P, NHALF, HALF])
        gated = sb("gated", [P, NHALF, HALF])
        h_full = sb("h_full", [P, NHALF, HALF])
        h_hi, h_lo = sb("h_hi", [P, 2, TOK], F32R), sb("h_lo", [P, 2, TOK], F32R)

        w_loaded = [sem("w_loaded0"), sem("w_loaded1")]
        w_hi_done = [sem("w_hi_done0"), sem("w_hi_done1")]
        w_up_split = [sem("w_up_split0"), sem("w_up_split1")]
        w_split = [sem("w_split0"), sem("w_split1")]
        w_used = [sem("w_used0"), sem("w_used1")]
        gate_loaded, gate_split = sem("gate_loaded"), sem("gate_split")
        logits_ready, logits_read, shifted_done = sem("logits_ready"), sem("logits_read"), sem("shifted_done")
        exp_done, step = sem("exp_done"), sem("vector_step")
        token_w_done, tw_turned, tw_hi_done, tw_lo_done = (
            sem("token_w_done"), sem("tw_turned"), sem("tw_hi_done"), sem("tw_lo_done"))
        gate_ready, up_ready, owner_ready = sem("gate_ready"), sem("up_ready"), sem("owner_ready")
        silu_done, gated_done, h_done = sem("silu_done"), sem("gated_done"), sem("h_done")
        h_hi_done, h_lo_done = sem("h_hi_done"), sem("h_lo_done")

        block = ctx.enter_context(nc.Block())

        @block.sync
        def _(sp):
            sp.dma_start(gate_raw[:], gate_w).then_inc(gate_loaded, 16)

            def load(n, parity, k):
                sp.wait_ge(w_split[parity], k)
                src = weights[bass.ds(n, 1), :, :].rearrange("a p n -> (a p) n")
                sp.dma_start(w_raw[:, parity, :], src).then_inc(w_loaded[parity], 16)

            with sp.Fori(0, n_chunks // 2) as i:
                load(2 * i, 0, i)
                load(2 * i + 1, 1, i)
            load(n_chunks - 1, 0, n_chunks // 2)

        @block.gpsimd
        def _(pool):
            def split(parity, k, columns, done):
                raw = w_raw[:, parity, columns]
                pool.tensor_tensor(w_hi[:, parity, columns], raw, res.zero[:].broadcast_to(raw.shape),
                                   ALU.add).then_inc(w_hi_done[parity], 1)
                pool.wait_ge(w_hi_done[parity], k)
                pool.tensor_tensor(w_lo[:, parity, columns], raw, f32(w_hi[:, parity, columns]),
                                   ALU.subtract).then_inc(done[parity], 1)

            def split_up(n, parity, k, first=False):
                if not first:
                    pool.wait_ge(owner_ready, 2 * n - 2)
                pool.wait_ge(w_loaded[parity], 16 * k + 16)
                split(parity, 2 * k + 1, slice(0, W_DOWN), w_up_split)

            def split_down(parity, k):
                pool.wait_ge(w_used[parity], k)
                split(parity, 2 * k + 2, slice(W_DOWN, FFN_COLS), w_split)

            pool.wait_ge(gate_loaded, 16)
            pool.tensor_copy(gate_hi[:], gate_raw[:]).then_inc(gate_split, 1)
            pool.wait_ge(gate_split, 1)
            pool.tensor_tensor(gate_lo[:], gate_raw[:], f32(gate_hi[:]), ALU.subtract).then_inc(gate_split, 1)
            norm.gpsimd(pool)
            split_up(0, 0, 0, True)
            split_down(0, 0)
            split_up(1, 1, 0, True)
            with pool.Fori(1, n_chunks // 2) as i:
                split_up(2 * i, 0, i)
                split_down(1, i - 1)
                split_up(2 * i + 1, 1, i)
                split_down(0, i)
            split_up(n_chunks - 1, 0, n_chunks // 2)
            split_down(1, n_chunks // 2 - 1)
            split_down(0, n_chunks // 2)

        @block.tensor
        def _(pe):
            def fill(bank, column, parity, half):
                at = slice(half * HALF, (half + 1) * HALF)
                for c in range(DC):
                    w = slice(column + c * P, column + (c + 1) * P)
                    last = product(pe, bank[:], (w_hi[:, parity, w], w_lo[:, parity, w]),
                                   (res.xh[:, c, at], res.xl[:, c, at]), c == 0, c == DC - 1)
                return last

            def gate_fill(n, parity, half):
                pe.wait_ge(h_done, 2 * n)
                fill(gate_bank[half], W_GATE, parity, half).then_inc(gate_ready, 1)

            def up_fill(n, parity, half):
                pe.wait_ge(gated_done, 2 * n)
                fill(up_bank[half], W_UP, parity, half).then_inc(up_ready, 1)

            def owner_fill(n, parity, half):
                at = slice(half * HALF, (half + 1) * HALF)
                sel = w_hi[0:16, parity, W_SEL:W_SEL + P]
                pe.wait_ge(silu_done, 2 * n + half + 1)
                pe.matmul(gate_bank[half][:], sel, tw_hi[:, at], start=True, stop=False, skip_group_check=True)
                pe.matmul(gate_bank[half][:], sel, tw_lo[:, at], start=False, stop=True,
                          skip_group_check=True).then_inc(owner_ready, 1)

            def up(n, parity, k, before_owner=None):
                pe.wait_ge(w_up_split[parity], k + 1)
                gate_fill(n, parity, 0)
                up_fill(n, parity, 0)
                gate_fill(n, parity, 1)
                if before_owner:
                    before_owner()
                owner_fill(n, parity, 0)
                up_fill(n, parity, 1)
                owner_fill(n, parity, 1)

            def down(n, parity, k, last_chunk=False):
                pe.wait_ge(w_split[parity], k + 1)
                pe.wait_ge(h_lo_done, 2 * n + 2)
                w = slice(W_DOWN, W_DOWN + D)
                for t in range(NT):
                    at = slice(t * P, (t + 1) * P)
                    last = product(pe, acc[t // 2][:, t % 2 * D:(t % 2 + 1) * D],
                                   (h_hi[:, parity, at], h_lo[:, parity, at]),
                                   (w_hi[:, parity, w], w_lo[:, parity, w]), False, last_chunk)
                last.then_inc(w_used[parity], 1)
                return last

            def route():
                pe.wait_ge(token_w_done, 1)
                pe.wait_ge(logits_read, 1)
                for half, bank in enumerate((up_bank[1], acc[0])):
                    for j in range(TB):
                        last = pe.transpose(bank[0:16, j * P:(j + 1) * P], token_w[:, half * TB + j, :], res.ident[:])
                    last.then_inc(tw_turned, 1)
                pe.wait_ge(tw_lo_done, 2)
                for bank in acc:
                    pe.matmul(bank[:], res.zeros[:, 0:P], res.zeros[:], start=True, stop=False,
                              skip_group_check=True)

            norm.tensor(pe)
            pe.wait_ge(norm.lo_done, NHALF * DC)
            pe.wait_ge(gate_split, 2)
            for t in range(NT):
                for c in range(DC):
                    at = slice(t * P, (t + 1) * P)
                    last = product(pe, up_bank[1][:, t * 16:t * 16 + GATES],
                                   (res.xh[:, c, at], res.xl[:, c, at]),
                                   (gate_hi[:, c, :], gate_lo[:, c, :]), t == 0 and c == 0, c == DC - 1)
            last.then_inc(logits_ready, 1)
            up(0, 0, 0, route)
            with pe.Fori(0, n_chunks // 2) as i:
                up(2 * i + 1, 1, i)
                down(2 * i, 0, i)
                up(2 * i + 2, 0, i + 1)
                down(2 * i + 1, 1, i)
            down(n_chunks - 1, 0, n_chunks // 2, True)

        @block.scalar
        def _(act):
            norm.scalar(act)
            act.wait_ge(shifted_done, 1)
            act.activation(probs[:], shifted[:], ACT.Exp).then_inc(exp_done, 1)
            if owner_is_gated:
                act.activation(gate_exp[:], logits[:, :, N_EXP], ACT.Exp, scale=-1.0).then_inc(exp_done, 1)
            for half, bank in enumerate((up_bank[1], acc[0])):
                act.wait_ge(tw_turned, half + 1)
                act.activation(tw_hi[:, half * HALF:(half + 1) * HALF], bank[0:16, :],
                               ACT.Copy).then_inc(tw_hi_done, 1)

            def chunk(n, parity, k):
                act.wait_ge(gated_done, 2 * n)
                for half in range(NHALF):
                    act.wait_ge(gate_ready, 2 * n + half + 1)
                    act.activation(silu[:, half, :], gate_bank[half][:], ACT.Silu).then_inc(silu_done, 1)
                act.wait_ge(w_used[parity], k)
                for half in range(NHALF):
                    act.wait_ge(h_done, 2 * n + half + 1)
                    act.activation(h_hi[:, parity, half * HALF:(half + 1) * HALF], h_full[:, half, :],
                                   ACT.Copy).then_inc(h_hi_done, 1)

            with act.Fori(0, n_chunks // 2) as i:
                chunk(2 * i, 0, i)
                chunk(2 * i + 1, 1, i)
            chunk(n_chunks - 1, 0, n_chunks // 2)

        @block.vector
        def _(dve):
            then = Chain(dve, step)
            norm.vector(dve)
            dve.wait_ge(logits_ready, 1)
            then(dve.tensor_copy(logits[:], up_bank[1][:, 0:NT * 16].rearrange("p (t g) -> p t g", g=16)[:, :, 0:GATES]))
            then(dve.tensor_reduce(row_max[:], logits[:, :, 0:N_EXP], AX.X, ALU.max))
            dve.tensor_tensor(shifted[:], logits[:, :, 0:N_EXP], spread(row_max[:], N_EXP),
                              ALU.subtract).then_inc(shifted_done, 1)
            dve.memset(token_w[:], 1.0).then_inc(logits_read, 1)
            dve.wait_ge(exp_done, 2 if owner_is_gated else 1)
            then(dve.tensor_reduce(row_sum[:], probs[:], AX.X, ALU.add))
            then(dve.reciprocal(row_sum[:], row_sum[:]))
            then(dve.tensor_tensor(probs[:], probs[:], spread(row_sum[:], N_EXP), ALU.mult))
            for t in range(NT):
                last = dve.max(top8[:, t, :], probs[:, t, :])
            then(last)
            for t in range(NT):
                last = dve.max_index(at8[:, t, :], top8[:, t, :], probs[:, t, :])
            then(last)
            then(dve.tensor_copy(at_f[:], at8[:, :, 0:TOP_K]))
            dve.tensor_tensor(first_hit[:], iota[:], spread(at_f[:, :, 0], N_EXP), ALU.is_equal)
            then(dve.tensor_tensor(second_hit[:], iota[:], spread(at_f[:, :, 1], N_EXP), ALU.is_equal))
            then(dve.tensor_tensor(first_hit[:], first_hit[:], second_hit[:], ALU.add))
            if renormalise:
                then(dve.tensor_tensor(row_sum[:], top8[:, :, 0], top8[:, :, 1], ALU.add))
                then(dve.tensor_scalar(row_sum[:], row_sum[:], 1e-20, None, ALU.add))
                then(dve.reciprocal(row_sum[:], row_sum[:]))
                then(dve.tensor_tensor(probs[:], probs[:], spread(row_sum[:], N_EXP), ALU.mult))
            if owner_is_gated:
                then(dve.tensor_scalar(gate_exp[:], gate_exp[:], 1.0, None, ALU.add))
                then(dve.reciprocal(token_w[:, :, N_EXP], gate_exp[:]))
            dve.tensor_tensor(token_w[:, :, 0:N_EXP], probs[:], first_hit[:], ALU.mult).then_inc(token_w_done, 1)
            for half, bank in enumerate((up_bank[1], acc[0])):
                at = slice(half * HALF, (half + 1) * HALF)
                dve.wait_ge(tw_hi_done, half + 1)
                dve.tensor_tensor(tw_lo[:, at], bank[0:16, :], f32(tw_hi[:, at]), ALU.subtract).then_inc(tw_lo_done, 1)

            def chunk(n, parity):
                for half in range(NHALF):
                    dve.wait_ge(silu_done, 2 * n + half + 1)
                    dve.wait_ge(up_ready, 2 * n + half + 1)
                    dve.tensor_tensor(gated[:, half, :], up_bank[half][:], silu[:, half, :],
                                      ALU.mult).then_inc(gated_done, 1)
                dve.wait_ge(h_hi_done, 2 * n)
                for half in range(NHALF):
                    dve.wait_ge(owner_ready, 2 * n + half + 1)
                    dve.wait_ge(gated_done, 2 * n + half + 1)
                    dve.tensor_tensor(h_full[:, half, :], gate_bank[half][:], gated[:, half, :],
                                      ALU.mult).then_inc(h_done, 1)
                for half in range(NHALF):
                    at = slice(half * HALF, (half + 1) * HALF)
                    dve.wait_ge(h_hi_done, 2 * n + half + 1)
                    dve.tensor_tensor(h_lo[:, parity, at], h_full[:, half, :], f32(h_hi[:, parity, at]),
                                      ALU.subtract).then_inc(h_lo_done, 1)

            with dve.Fori(0, n_chunks // 2) as i:
                chunk(2 * i, 0)
                chunk(2 * i + 1, 1)
            chunk(n_chunks - 1, 0)
            dve.wait_ge(w_used[0], n_chunks // 2 + 1)
            for b in range(NT // 2):
                two = res.x[:, 2 * b:2 * b + 2, :]
                dve.tensor_tensor(two, acc[b][:].rearrange("p (t d) -> p t d", d=D), two, ALU.add)


HEADS, DH = 16, 128
GROUP = 4
GROUPS = HEADS // GROUP
WIDE = GROUP * DH
UNIT_OF_ROW = (0, 0, 1, 2)
UNIT_ROWS = ((0, 1), (2,), (3,))
ROW_AT = (0, P, 0, 0)


def wide_stage(nc, name, res, t):
    scale = 1.0 / DH ** 0.5
    with ExitStack() as ctx:
        sem = ctx.enter_context(Semaphores(nc, name))
        sb = lambda what, shape, dt=F32: ctx.enter_context(nc.sbuf_tensor(f"{name}_{what}", shape, dt))
        banks = [ctx.enter_context(nc.psum_tensor(f"{name}_bank{i}", [P, HALF], F32)) for i in range(8)]
        acc, s_bank, t_bank, o_bank, fill_bank = banks[:2], banks[2:4], banks[4:6], banks[6], banks[7]
        ring = (*s_bank, *t_bank)
        norm = Norm(nc, ctx, sem, f"{name}_ln", res, [b[:] for b in ring])

        scratch = sb("scratch", [P, 2 * TB, HALF])
        wq_raw = scratch[:].rearrange("p (c a) n -> p c (a n)", c=DC)
        probs = scratch[:].rearrange("p (u r) n -> p u r n", u=2)
        probs_t = sb("probs_t", [P, TB, HALF])
        wq_hi, wq_lo = sb("wq_hi", [P, DC, HEADS * DH], F32R), sb("wq_lo", [P, DC, HEADS * DH], F32R)
        w_raw = sb("w_raw", [P, 3, DC * WIDE])
        w_hi, w_lo = sb("w_hi", [P, 3, DC * WIDE], F32R), sb("w_lo", [P, 3, DC * WIDE], F32R)
        bq, bk, bv = sb("bq", [P, HEADS]), sb("bk", [P, GROUP]), sb("bv", [P, WIDE])
        bo = sb("bo", [P, D])
        q, k, v = sb("q", [P, B, GROUP * S]), sb("k", [P, B, GROUP, S]), sb("v", [P, B, TB, WIDE])
        neg_max, row_sum = sb("neg_max", [P, 4 * GROUP]), sb("row_sum", [P, 4 * GROUP])
        o_hi, o_lo = sb("o_hi", [P, S], F32R), sb("o_lo", [P, S], F32R)

        wq_loaded, wq_hi_done, wq_split = sem("wq_loaded"), sem("wq_hi_done"), sem("wq_split")
        w_loaded = [sem(f"w_loaded{p}") for p in "kvo"]
        w_hi_done = sem("w_hi_done")
        w_split = [sem(f"w_split{p}") for p in "kvo"]
        bias_loaded, bk_loaded, bv_loaded, bq_scaled = sem("bias_loaded"), sem("bk_loaded"), sem("bv_loaded"), sem("bq_scaled")
        k_ready, v_ready, q_ready = sem("k_ready"), sem("v_ready"), sem("q_ready")
        k_done, v_done, q_done = sem("k_done"), sem("v_done"), sem("q_done")
        scores_ready, max_done, exp_done, inverse_done, probs_done = (
            sem("scores_ready"), sem("max_done"), sem("exp_done"), sem("inverse_done"), sem("probs_done"))
        turned, probs_t_done = sem("turned"), sem("probs_t_done")
        o_ready, o_hi_done, o_lo_done, out_done = sem("o_ready"), sem("o_hi_done"), sem("o_lo_done"), sem("out_done")
        bo_added, acc_read = sem("bo_added"), sem("acc_read")
        group_w = (t["wb_k"], t["wb_v"], t["wb_o"])
        FILLS = [(kind, f) for kind in "kqv" for f in range(4)]
        PER_STEP = len(FILLS) // GROUP

        def score_bank(h, r):
            return s_bank[(3 * h + UNIT_OF_ROW[r]) % 2][:, ROW_AT[r]:ROW_AT[r] + (r + 1) * P]

        def turned_bank(h, u):
            return t_bank[(3 * h + u) % 2]

        def units(engine, unit):
            with engine.Fori(0, GROUPS - 1) as i:
                for b in range(B):
                    unit(i, b, True)
            for b in range(B):
                unit(GROUPS - 1, b, b == 0)

        def fills_of_step(i, b, h):
            for kind, f in FILLS[PER_STEP * h:PER_STEP * (h + 1)]:
                yield B * i + b + 1, i + b, 1 - b, kind, f

        block = ctx.enter_context(nc.Block())

        @block.sync
        def _(sp):
            def load(i):
                sp.wait_ge(k_done, B * GROUP * i)
                sp.dma_start(bk[:], t["bb_k"][bass.ds(i, 1), :, :].rearrange("a p n -> (a p) n")).then_inc(bk_loaded, 16)
                sp.wait_ge(w_split[0], i)
                sp.dma_start(w_raw[:, 0, :], group_w[0][bass.ds(i, 1), :, :].rearrange("a p n -> (a p) n")).then_inc(w_loaded[0], 16)
                sp.wait_ge(v_done, B * TB * i)
                sp.dma_start(bv[:], t["bb_v"][bass.ds(i, 1), :].rearrange("a n -> (a n)").partition_broadcast(P)).then_inc(bv_loaded, 16)
                for p in (1, 2):
                    sp.wait_ge(w_split[p], i)
                    sp.dma_start(w_raw[:, p, :], group_w[p][bass.ds(i, 1), :, :].rearrange("a p n -> (a p) n")).then_inc(w_loaded[p], 16)

            load(0)
            for c in range(DC):
                sp.dma_start(wq_raw[:, c, :], t["wb_q"][:, c, :]).then_inc(wq_loaded, 16)
            sp.dma_start(bq[:], t["bb_q"]).then_inc(bias_loaded, 16)
            sp.dma_start(bo[:], t["bb_o"].partition_broadcast(P)).then_inc(bias_loaded, 16)
            with sp.Fori(1, GROUPS) as i:
                load(i)

        @block.gpsimd
        def _(pool):
            norm.gpsimd(pool)

            def split(i):
                for p, used in enumerate((k_ready, v_ready, out_done)):
                    pool.wait_ge(used, B * GROUP * i)
                    pool.wait_ge(w_loaded[p], 16 * i + 16)
                    pool.tensor_tensor(w_hi[:, p, :], w_raw[:, p, :], res.zero[:].broadcast_to([P, DC * WIDE]),
                                       ALU.add).then_inc(w_hi_done, 1)
                    pool.wait_ge(w_hi_done, 3 * i + p + 1)
                    pool.tensor_tensor(w_lo[:, p, :], w_raw[:, p, :], f32(w_hi[:, p, :]),
                                       ALU.subtract).then_inc(w_split[p], 1)

            split(0)
            pool.wait_ge(norm.normed, NT)
            pool.wait_ge(bias_loaded, 32)
            pool.tensor_tensor(res.x[:], res.x[:], bo[:].unsqueeze(1).broadcast_to([P, NT, D]), ALU.add).then_inc(bo_added, 1)
            with pool.Fori(1, GROUPS) as i:
                split(i)

        @block.tensor
        def _(pe):
            norm.tensor(pe)
            pe.wait_ge(norm.lo_done, NHALF * DC)

            def weights(p, c, at, n):
                w = slice(c * WIDE + at, c * WIDE + at + n)
                return w_hi[:, p, w], w_lo[:, p, w]

            def fill(U, i, b, kind, f, bank):
                both = lambda c, at: (res.xh[:, c, at], res.xl[:, c, at])
                if kind == "k":
                    if f == 0:
                        pe.wait_ge(w_split[0], i + 1)
                    for c in range(DC):
                        last = product(pe, bank[:], weights(0, c, f * DH, DH), both(c, slice(b * S, (b + 1) * S)),
                                       c == 0, c == DC - 1)
                    last.then_inc(k_ready, 1)
                if kind == "q":
                    for j in range(4):
                        sub = slice((4 * f + j) * DH, (4 * f + j + 1) * DH)
                        for c in range(DC):
                            last = product(pe, bank[:, j * P:(j + 1) * P], (wq_hi[:, c, sub], wq_lo[:, c, sub]),
                                           both(c, bass.ds(i * P + b * S, P)), j == 0 and c == 0, c == DC - 1)
                    last.then_inc(q_ready, 1)
                if kind == "v":
                    if f == 0:
                        pe.wait_ge(w_split[1], i + 1)
                    for c in range(DC):
                        last = product(pe, bank[:], both(c, slice(b * S + f * P, b * S + (f + 1) * P)),
                                       weights(1, c, 0, WIDE), c == 0, c == DC - 1)
                    last.then_inc(v_ready, 1)

            def next_fill(fills):
                U, i, b, kind, f = next(fills)
                if f:
                    pe.wait_ge({"k": k_done, "q": q_done, "v": v_done}[kind], 4 * U + f)
                else:
                    pe.wait_ge(*{"k": (v_done, 4 * U), "q": (k_done, 4 * U + 4), "v": (q_done, 4 * U + 4)}[kind])
                fill(U, i, b, kind, f, fill_bank)

            def scores(b, h, n, u):
                if u == 2:
                    pe.wait_ge(exp_done, 4 * n + 2)
                for r in UNIT_ROWS[u]:
                    to = score_bank(h, r)
                    pe.matmul(to, q[:, b, h * S + r * P:h * S + (r + 1) * P], k[:, b, h, 0:(r + 1) * P],
                              start=r == UNIT_ROWS[u][0], stop=False, skip_group_check=True)
                    last = pe.matmul(to[:, r * P:(r + 1) * P], res.ident_bf[:], res.causal[:],
                                     start=False, stop=True, skip_group_check=True)
                last.then_inc(scores_ready, 1)

            def turn(h, n, u):
                if u == 2:
                    pe.wait_ge(probs_t_done, 3 * n + 1)
                for r in UNIT_ROWS[u]:
                    pe.wait_ge(probs_done, 4 * n + r + 1)
                    for j in range(r + 1):
                        at = ROW_AT[r] + j * P
                        last = pe.transpose(turned_bank(h, u)[:, at:at + P], probs[:, h % 2, r, j * P:(j + 1) * P], res.ident[:])
                last.then_inc(turned, 1)

            def attend(b, h, n):
                pe.wait_ge(probs_t_done, 3 * n + 3)
                for j in range(TB):
                    last = pe.matmul(o_bank[:, j * P:S], v[:, b, j, h * DH:(h + 1) * DH], probs_t[:, j, j * P:S],
                                     start=j == 0, stop=j == TB - 1, skip_group_check=True)
                last.then_inc(o_ready, 1)

            def project_out(h, n):
                pe.wait_ge(o_lo_done, n + 1)
                for j in range(TB):
                    at = slice(j * P, (j + 1) * P)
                    last = product(pe, acc[j // 2][:, j % 2 * D:(j % 2 + 1) * D], (o_hi[:, at], o_lo[:, at]),
                                   (w_hi[:, 2, h * D:(h + 1) * D], w_lo[:, 2, h * D:(h + 1) * D]), h == 0 and j % 2 == 0,
                                   h == GROUP - 1)
                last.then_inc(out_done, 1)

            def unit(i, b, more):
                U = B * i + b
                for h in range(GROUP):
                    n = GROUP * U + h
                    head_after = (b, h + 1, n + 1) if h + 1 < GROUP else (1 - b, 0, n + 1)
                    follows = more or h + 1 < GROUP
                    fills = fills_of_step(i, b, h)
                    turn(h, n, 0)
                    turn(h, n, 1)
                    if follows:
                        pe.wait_ge(exp_done, 4 * n + 3)
                        scores(*head_after, 0)
                    turn(h, n, 2)
                    if follows:
                        pe.wait_ge(exp_done, 4 * n + 4)
                        scores(*head_after, 1)
                    if more:
                        next_fill(fills)
                    if h == 0:
                        pe.wait_ge(v_done, TB * U + TB)
                    attend(b, h, n)
                    if more:
                        next_fill(fills)
                    if follows:
                        scores(*head_after, 2)
                    if more:
                        next_fill(fills)
                    if h == 0:
                        pe.wait_ge(acc_read, 2 * U)
                        pe.wait_ge(w_split[2], i + 1)
                    project_out(h, n)

            evacuated = {"k": k_done, "q": q_done, "v": v_done}
            for g, (kind, f) in enumerate(FILLS):
                if g == 4:
                    pe.wait_ge(wq_split, 1)
                if g >= 4:
                    pe.wait_ge(evacuated[FILLS[g - 4][0]], f + 1)
                fill(0, 0, 0, kind, f, ring[g % 4])
            pe.wait_ge(v_done, TB)
            for u in range(3):
                scores(0, 0, 0, u)
            units(pe, unit)

        @block.scalar
        def _(act):
            norm.scalar(act)
            act.wait_ge(wq_loaded, 16 * DC)
            act.activation(wq_hi[:], wq_raw, ACT.Copy).then_inc(wq_hi_done, 1)

            def k_evacuated(U, b, f, bank):
                act.wait_ge(k_ready, GROUP * U + f + 1)
                act.activation(k[:, b, f, :], bank[:], ACT.Identity, bias=bk[:, f:f + 1]).then_inc(k_done, 1)

            def exponentials(h, n, u):
                for r in UNIT_ROWS[u]:
                    act.wait_ge(max_done, 4 * n + max(r, 1) + 1)
                    act.activation(probs[:, h % 2, r, 0:(r + 1) * P], score_bank(h, r), ACT.Exp,
                                   bias=neg_max[:, 4 * h + r:4 * h + r + 1],
                                   accum_out=row_sum[:, 4 * h + r:4 * h + r + 1]).then_inc(exp_done, 1)

            def turned_back(h, n, u):
                act.wait_ge(turned, 3 * n + u + 1)
                for r in UNIT_ROWS[u]:
                    from_ = turned_bank(h, u)[:, ROW_AT[r]:ROW_AT[r] + (r + 1) * P].rearrange("p (j q) -> p j q", q=P)
                    last = act.activation(probs_t[:, 0:r + 1, r * P:(r + 1) * P], from_, ACT.Copy)
                last.then_inc(probs_t_done, 1)

            def unit(i, b, more):
                U = B * i + b
                for h in range(GROUP):
                    n = GROUP * U + h
                    after, follows = ((h + 1) % GROUP, n + 1), more or h + 1 < GROUP
                    fills = fills_of_step(i, b, h) if more else iter(())

                    def next_fill():
                        for U1, i1, b1, kind, f in list(itertools.islice(fills, 1)):
                            if kind == "k":
                                if f == 0:
                                    act.wait_ge(bk_loaded, 16 * i1 + 16)
                                k_evacuated(U1, b1, f, fill_bank)

                    turned_back(h, n, 0)
                    turned_back(h, n, 1)
                    if follows:
                        exponentials(*after, 0)
                    turned_back(h, n, 2)
                    if follows:
                        exponentials(*after, 1)
                    next_fill()
                    act.wait_ge(o_ready, n + 1)
                    act.activation(o_hi[:], o_bank[:], ACT.Copy).then_inc(o_hi_done, 1)
                    next_fill()
                    if follows:
                        exponentials(*after, 2)
                    next_fill()

            act.wait_ge(bk_loaded, 16)
            for f in range(GROUP):
                k_evacuated(0, 0, f, ring[f])
            act.wait_ge(wq_split, 1)
            for u in range(3):
                exponentials(0, 0, u)
            units(act, unit)

        @block.vector
        def _(dve):
            norm.vector(dve)
            dve.wait_ge(wq_hi_done, 1)
            dve.tensor_tensor(wq_lo[:], wq_raw, f32(wq_hi[:]), ALU.subtract).then_inc(wq_split, 1)
            dve.wait_ge(bias_loaded, 32)
            dve.tensor_scalar(bq[:], bq[:], scale, None, ALU.mult).then_inc(bq_scaled, 1)
            dve.wait_ge(bq_scaled, 1)

            def evacuated(U, i, b, kind, f, bank):
                if kind == "q":
                    dve.wait_ge(q_ready, 4 * U + f + 1)
                    to = q[:, b, :].rearrange("p (t s) -> p s t", s=HEADS)[:, 4 * f:4 * f + 4, :]
                    dve.scalar_tensor_tensor(to, bank[:].rearrange("p (s t) -> p s t", s=4), scale,
                                             spread(bq[:, 4 * f:4 * f + 4], P), ALU.mult, ALU.add).then_inc(q_done, 1)
                if kind == "v":
                    if f == 0:
                        dve.wait_ge(bv_loaded, 16 * i + 16)
                    dve.wait_ge(v_ready, TB * U + f + 1)
                    dve.tensor_tensor(v[:, b, f, :], bank[:], bv[:], ALU.add).then_inc(v_done, 1)

            def row_max(h, n, u):
                dve.wait_ge(scores_ready, 3 * n + u + 1)
                for r in UNIT_ROWS[u]:
                    dve.tensor_reduce(neg_max[:, 4 * h + r:4 * h + r + 1], score_bank(h, r), AX.X, ALU.max,
                                      negate=True).then_inc(max_done, 1)

            def normalise(h, n, u):
                for r in UNIT_ROWS[u]:
                    one = row_sum[:, 4 * h + r:4 * h + r + 1]
                    dve.wait_ge(exp_done, 4 * n + r + 1)
                    dve.reciprocal(one, one).then_inc(inverse_done, 1)
                    dve.wait_ge(inverse_done, 4 * n + r + 1)
                    mine = probs[:, h % 2, r, 0:(r + 1) * P]
                    dve.tensor_scalar(mine, mine, one, None, ALU.mult).then_inc(probs_done, 1)

            def add_to_stream(U, b):
                dve.wait_ge(out_done, GROUP * (U + 1))
                for a in range(2):
                    two = res.x[:, b * TB + 2 * a:b * TB + 2 * a + 2, :]
                    dve.tensor_tensor(two, acc[a][:].rearrange("p (t d) -> p t d", d=D), two, ALU.add).then_inc(acc_read, 1)

            def unit(i, b, more):
                U = B * i + b
                for h in range(GROUP):
                    n = GROUP * U + h
                    after, follows = ((h + 1) % GROUP, n + 1), more or h + 1 < GROUP
                    fills = fills_of_step(i, b, h) if more else iter(())
                    next_fill = lambda: [evacuated(*x, fill_bank) for x in itertools.islice(fills, 1)]
                    if follows:
                        row_max(*after, 0)
                        row_max(*after, 1)
                        normalise(*after, 0)
                        normalise(*after, 1)
                    next_fill()
                    dve.wait_ge(o_hi_done, n + 1)
                    dve.tensor_tensor(o_lo[:], o_bank[:], f32(o_hi[:]), ALU.subtract).then_inc(o_lo_done, 1)
                    next_fill()
                    if follows:
                        row_max(*after, 2)
                        normalise(*after, 2)
                    next_fill()
                add_to_stream(U, b)

            for g, (kind, f) in enumerate(FILLS):
                evacuated(0, 0, 0, kind, f, ring[g % 4])
            for u in range(3):
                row_max(0, 0, u)
            for u in range(3):
                normalise(0, 0, u)
            dve.wait_ge(bo_added, 1)
            units(dve, unit)


Q_HEADS, KV_HEADS, HD = 16, 4, 16
PER_KV = Q_HEADS // KV_HEADS
SLOT = P // KV_HEADS
GQ_COLS = DC * P + D
GK_COLS = 2 * DC * P


def causal_gqa_stage(nc, name, res, t):
    with ExitStack() as ctx:
        sem = ctx.enter_context(Semaphores(nc, name))
        sb = lambda what, shape, dt=F32: ctx.enter_context(nc.sbuf_tensor(f"{name}_{what}", shape, dt))
        banks = [ctx.enter_context(nc.psum_tensor(f"{name}_bank{i}", [P, HALF], F32)) for i in range(8)]
        acc, s_bank, t_bank, o_bank = banks[:2], banks[2:5], banks[5:7], banks[7]
        norm = Norm(nc, ctx, sem, f"{name}_ln", res, [b[:] for b in banks[2:6]])

        kv_raw = sb("kv_raw", [P, GK_COLS])
        kv_hi, kv_lo = sb("kv_hi", [P, GK_COLS], F32R), sb("kv_lo", [P, GK_COLS], F32R)
        w_raw = sb("w_raw", [P, GQ_COLS])
        w_hi, w_lo = sb("w_hi", [P, GQ_COLS], F32R), sb("w_lo", [P, GQ_COLS], F32R)
        turn_q, turn_k = sb("turn_q", [P, S]), sb("turn_k", [P, S])
        bq, bk, bv, bo = sb("bq", [P, PER_KV]), sb("bk", [P, 1]), sb("bv", [P, P]), sb("bo", [P, D])
        k = sb("k", [P, TOK])
        k_hi, k_lo = sb("k_hi", [P, KV_HEADS, TOK], F32R), sb("k_lo", [P, KV_HEADS, TOK], F32R)
        v = sb("v", [P, NT, P])
        q, q_hi, q_lo = sb("q", [P, S]), sb("q_hi", [P, S], F32R), sb("q_lo", [P, S], F32R)
        probs = sb("probs", [P, 2, TB, S])
        probs_t = sb("probs_t", [P, KV_HEADS, TB, S])
        neg_max, row_sum = sb("neg_max", [P, 4 * KV_HEADS]), sb("row_sum", [P, 4 * KV_HEADS])
        o_hi, o_lo = sb("o_hi", [P, S], F32R), sb("o_lo", [P, S], F32R)

        loaded, kv_hi_done, kv_split = sem("loaded"), sem("kv_hi_done"), sem("kv_split")
        w_loaded, w_hi_done, wq_split, wo_split = sem("w_loaded"), sem("w_hi_done"), sem("wq_split"), sem("wo_split")
        k_ready, k_done, k_cleared, k_hi_done, k_lo_done = (
            sem("k_ready"), sem("k_done"), sem("k_cleared"), sem("k_hi_done"), sem("k_lo_done"))
        v_ready, v_done = sem("v_ready"), sem("v_done")
        q_ready, q_done, q_hi_done, q_lo_done = sem("q_ready"), sem("q_done"), sem("q_hi_done"), sem("q_lo_done")
        scores_ready, max_done, exp_done, inverse_done, probs_done = (
            sem("scores_ready"), sem("max_done"), sem("exp_done"), sem("inverse_done"), sem("probs_done"))
        turned, probs_t_done = sem("turned"), sem("probs_t_done")
        o_ready, o_hi_done, o_lo_done, out_done, acc_read = (
            sem("o_ready"), sem("o_hi_done"), sem("o_lo_done"), sem("out_done"), sem("acc_read"))

        def groups(engine, body, after_batch=None):
            for b in range(B):
                with engine.Fori(0, PER_KV - 1) as c:
                    body(b, c, c + b * PER_KV, b)
                body(b, PER_KV - 1, (b + 1) * PER_KV - 1, b + 1)
                if after_batch:
                    after_batch(b)

        block = ctx.enter_context(nc.Block())

        @block.sync
        def _(sp):
            sp.dma_start(kv_raw[:], t["wc_kv"]).then_inc(loaded, 16)
            for to, src in ((bq, "bc_q"), (bk, "bc_k"), (turn_q, "turn_q"), (turn_k, "turn_k")):
                sp.dma_start(to[:], t[src]).then_inc(loaded, 16)
            for to, src in ((bv, "bc_v"), (bo, "bc_o")):
                sp.dma_start(to[:], t[src].partition_broadcast(P)).then_inc(loaded, 16)
            for b in range(B):
                with sp.Fori(0, PER_KV) as c:
                    sp.wait_ge(wo_split, b * PER_KV + c)
                    sp.dma_start(w_raw[:], t["wc_q"][bass.ds(c, 1), :, :].rearrange("a p n -> (a p) n")).then_inc(w_loaded, 16)

        @block.gpsimd
        def _(pool):
            pool.memset(f32(k_hi[:]), 0.0).then_inc(k_cleared, 1)
            pool.memset(f32(k_lo[:]), 0.0).then_inc(k_cleared, 1)

            def split(raw, hi, lo, hi_done, value, done):
                pool.tensor_tensor(hi, raw, res.zero[:].broadcast_to(raw.shape), ALU.add).then_inc(hi_done, 1)
                pool.wait_ge(hi_done, value)
                pool.tensor_tensor(lo, raw, f32(hi), ALU.subtract).then_inc(done, 1)

            pool.wait_ge(loaded, 16 * 7)
            split(kv_raw[:], kv_hi[:], kv_lo[:], kv_hi_done, 1, kv_split)
            norm.gpsimd(pool)
            wq, wo = slice(0, DC * P), slice(DC * P, GQ_COLS)
            for b in range(B):
                with pool.Fori(0, PER_KV) as c:
                    G = b * PER_KV + c
                    pool.wait_ge(q_ready, G)
                    pool.wait_ge(w_loaded, 16 * G + 16)
                    split(w_raw[:, wq], w_hi[:, wq], w_lo[:, wq], w_hi_done, 2 * G + 1, wq_split)
                    pool.wait_ge(out_done, G)
                    split(w_raw[:, wo], w_hi[:, wo], w_lo[:, wo], w_hi_done, 2 * G + 2, wo_split)

        @block.tensor
        def _(pe):
            norm.tensor(pe)
            pe.wait_ge(norm.lo_done, NHALF * DC)
            pe.wait_ge(kv_split, 1)
            pair = lambda hi, lo, *at: (hi[(slice(None), *at)], lo[(slice(None), *at)])
            for b in range(B):
                for c in range(DC):
                    last = product(pe, banks[2 + b][:], pair(kv_hi, kv_lo, slice(c * P, (c + 1) * P)),
                                   pair(res.xh, res.xl, c, slice(b * S, (b + 1) * S)), c == 0, c == DC - 1)
                last.then_inc(k_ready, 1)
            for h in range(NHALF):
                for j in range(TB):
                    for c in range(DC):
                        at = slice((h * TB + j) * P, (h * TB + j + 1) * P)
                        last = product(pe, banks[4 + h][:, j * P:(j + 1) * P], pair(res.xh, res.xl, c, at),
                                       pair(kv_hi, kv_lo, slice((DC + c) * P, (DC + c + 1) * P)),
                                       j == 0 and c == 0, c == DC - 1)
                last.then_inc(v_ready, 1)

            def project_q(b, G):
                pe.wait_ge(wq_split, G + 1)
                pe.wait_ge(exp_done, 16 * G)
                for c in range(DC):
                    last = product(pe, s_bank[0][:], pair(w_hi, w_lo, slice(c * P, (c + 1) * P)),
                                   pair(res.xh, res.xl, c, slice(b * S, (b + 1) * S)), c == 0, c == DC - 1)
                last.then_inc(q_ready, 1)

            def scores(b, g, n):
                pe.wait_ge(exp_done, 4 * n)
                for unit in UNIT_ROWS:
                    for r in unit:
                        to = s_bank[UNIT_OF_ROW[r]][:, ROW_AT[r]:ROW_AT[r] + (r + 1) * P]
                        product(pe, to, pair(q_hi, q_lo, slice(r * P, (r + 1) * P)),
                                pair(k_hi, k_lo, g, slice(b * S, b * S + (r + 1) * P)), r == unit[0], False)
                        last = pe.matmul(to[:, r * P:(r + 1) * P], res.ident_bf[:], res.causal[:],
                                         start=False, stop=True, skip_group_check=True)
                    last.then_inc(scores_ready, 1)

            def turn(g, n):
                for u, unit in enumerate(UNIT_ROWS):
                    pe.wait_ge(probs_t_done, 3 * n + (u == 2))
                    for r in unit:
                        pe.wait_ge(probs_done, 4 * n + r + 1)
                        for j in range(r + 1):
                            at = ROW_AT[r] + j * P
                            last = pe.transpose(t_bank[u % 2][:, at:at + P], probs[:, g % 2, r, j * P:(j + 1) * P],
                                                res.ident[:])
                    last.then_inc(turned, 1)

            def attend(b, G):
                pe.wait_ge(o_lo_done, G)
                pe.wait_ge(probs_t_done, 12 * G + 12)
                for j in range(TB):
                    for g in range(KV_HEADS):
                        slot = slice(g * SLOT, (g + 1) * SLOT)
                        last = pe.matmul(o_bank[slot, j * P:S], v[:, b * TB + j, slot], probs_t[:, g, j, j * P:S],
                                         start=j == 0, stop=j == TB - 1, skip_group_check=True)
                last.then_inc(o_ready, 1)

            def project_out(c, G):
                pe.wait_ge(o_lo_done, G + 1)
                pe.wait_ge(wo_split, G + 1)
                for j in range(TB):
                    last = product(pe, acc[j // 2][:, j % 2 * D:(j % 2 + 1) * D], pair(o_hi, o_lo, slice(j * P, (j + 1) * P)),
                                   pair(w_hi, w_lo, slice(DC * P, GQ_COLS)), False, True)
                last.then_inc(out_done, 1)

            def clear(b):
                for bank in acc:
                    pe.matmul(bank[:], res.zeros[:, 0:P], res.zeros[:], start=True, stop=False, skip_group_check=True)

            def body(b, c, G, next_b):
                pe.wait_ge(q_lo_done, G + 1)
                for g in range(KV_HEADS):
                    n = KV_HEADS * G + g
                    scores(b, g, n)
                    if g:
                        turn(g - 1, n - 1)
                if next_b < B:
                    project_q(next_b, G + 1)
                turn(KV_HEADS - 1, KV_HEADS * G + KV_HEADS - 1)
                attend(b, G)
                project_out(c, G)

            def after_batch(b):
                if b + 1 < B:
                    pe.wait_ge(acc_read, 2 * (b + 1))
                    clear(b + 1)

            pe.wait_ge(k_done, B)
            project_q(0, 0)
            clear(0)
            pe.wait_ge(k_hi_done, B * KV_HEADS)
            pe.wait_ge(k_lo_done, B * KV_HEADS)
            pe.wait_ge(v_done, NHALF)
            groups(pe, body, after_batch)

        @block.scalar
        def _(act):
            norm.scalar(act)
            act.wait_ge(k_cleared, 2)
            for b in range(B):
                act.wait_ge(k_done, b + 1)
                for g in range(KV_HEADS):
                    slot, at = slice(g * SLOT, (g + 1) * SLOT), slice(b * S, (b + 1) * S)
                    act.activation(k_hi[slot, g, at], k[slot, at], ACT.Copy).then_inc(k_hi_done, 1)

            def split_q(G):
                act.wait_ge(q_done, G + 1)
                act.wait_ge(scores_ready, 12 * G)
                act.activation(q_hi[:], q[:], ACT.Copy).then_inc(q_hi_done, 1)

            def turned_back(g, n):
                for u, unit in enumerate(UNIT_ROWS):
                    act.wait_ge(turned, 3 * n + u + 1)
                    for r in unit:
                        from_ = t_bank[u % 2][:, ROW_AT[r]:ROW_AT[r] + (r + 1) * P].rearrange("p (j q) -> p j q", q=P)
                        last = act.activation(probs_t[:, g, 0:r + 1, r * P:(r + 1) * P], from_, ACT.Copy)
                    last.then_inc(probs_t_done, 1)

            def body(b, c, G, next_b):
                act.wait_ge(o_ready, G)
                for g in range(KV_HEADS):
                    n = KV_HEADS * G + g
                    act.wait_ge(turned, 3 * n - 3 if g else 3 * n)
                    for r in range(4):
                        act.wait_ge(max_done, 4 * n + max(r, 1) + 1)
                        act.activation(probs[:, g % 2, r, 0:(r + 1) * P],
                                       s_bank[UNIT_OF_ROW[r]][:, ROW_AT[r]:ROW_AT[r] + (r + 1) * P], ACT.Exp,
                                       bias=neg_max[:, 4 * g + r:4 * g + r + 1],
                                       accum_out=row_sum[:, 4 * g + r:4 * g + r + 1]).then_inc(exp_done, 1)
                    if g:
                        turned_back(g - 1, n - 1)
                if next_b < B:
                    split_q(G + 1)
                turned_back(KV_HEADS - 1, KV_HEADS * G + KV_HEADS - 1)
                act.wait_ge(out_done, G)
                act.wait_ge(o_ready, G + 1)
                act.activation(o_hi[:], o_bank[:], ACT.Copy).then_inc(o_hi_done, 1)

            split_q(0)
            groups(act, body)

        @block.vector
        def _(dve):
            norm.vector(dve)
            dve.wait_ge(loaded, 16 * 7)
            for b in range(B):
                dve.wait_ge(k_ready, b + 1)
                dve.scalar_tensor_tensor(k[:, b * S:(b + 1) * S], banks[2 + b][:], bk[:, 0:1], turn_k[:],
                                         ALU.add, ALU.mult).then_inc(k_done, 1)
            for h in range(NHALF):
                dve.wait_ge(v_ready, h + 1)
                dve.tensor_tensor(v[:, h * TB:(h + 1) * TB, :], banks[4 + h][:].rearrange("p (j n) -> p j n", n=P),
                                  bv[:].unsqueeze(1).broadcast_to([P, TB, P]), ALU.add).then_inc(v_done, 1)
            dve.wait_ge(k_cleared, 2)

            def rotate_q(c, G):
                dve.wait_ge(q_ready, G + 1)
                dve.wait_ge(q_hi_done, G)
                dve.scalar_tensor_tensor(q[:], s_bank[0][:], bq[:, bass.ds(c, 1)], turn_q[:],
                                         ALU.add, ALU.mult).then_inc(q_done, 1)
                dve.wait_ge(q_hi_done, G + 1)
                dve.tensor_tensor(q_lo[:], q[:], f32(q_hi[:]), ALU.subtract).then_inc(q_lo_done, 1)

            rotate_q(0, 0)
            for b in range(B):
                for g in range(KV_HEADS):
                    slot, at = slice(g * SLOT, (g + 1) * SLOT), slice(b * S, (b + 1) * S)
                    dve.wait_ge(k_hi_done, b * KV_HEADS + g + 1)
                    dve.tensor_tensor(k_lo[slot, g, at], k[slot, at], f32(k_hi[slot, g, at]),
                                      ALU.subtract).then_inc(k_lo_done, 1)

            def row_max(g, n, r):
                dve.wait_ge(scores_ready, 3 * n + UNIT_OF_ROW[r] + 1)
                dve.tensor_reduce(neg_max[:, 4 * g + r:4 * g + r + 1],
                                  s_bank[UNIT_OF_ROW[r]][:, ROW_AT[r]:ROW_AT[r] + (r + 1) * P], AX.X, ALU.max,
                                  negate=True).then_inc(max_done, 1)

            def normalise(g, n, r):
                one = row_sum[:, 4 * g + r:4 * g + r + 1]
                dve.wait_ge(exp_done, 4 * n + r + 1)
                dve.reciprocal(one, one).then_inc(inverse_done, 1)
                dve.wait_ge(inverse_done, 4 * n + r + 1)
                mine = probs[:, g % 2, r, 0:(r + 1) * P]
                dve.tensor_scalar(mine, mine, one, None, ALU.mult).then_inc(probs_done, 1)

            def body(b, c, G, next_b):
                for g in range(KV_HEADS):
                    n = KV_HEADS * G + g
                    for r in range(4):
                        row_max(g, n, r)
                        if r >= 2:
                            normalise(g, n, r - 2)
                    normalise(g, n, 2)
                    normalise(g, n, 3)
                if next_b < B:
                    rotate_q(c + 1 if next_b == b else 0, G + 1)
                dve.wait_ge(o_hi_done, G + 1)
                dve.tensor_tensor(o_lo[:], o_bank[:], f32(o_hi[:]), ALU.subtract).then_inc(o_lo_done, 1)

            def after_batch(b):
                dve.wait_ge(out_done, (b + 1) * PER_KV)
                for a in range(2):
                    two = res.x[:, b * TB + 2 * a:b * TB + 2 * a + 2, :]
                    dve.tensor_tensor(two, acc[a][:].rearrange("p (t d) -> p t d", d=D), two, ALU.add).then_inc(acc_read, 1)
                    dve.wait_ge(acc_read, 2 * b + a + 1)
                    dve.tensor_tensor(two, two, bo[:].unsqueeze(1).broadcast_to([P, 2, D]), ALU.add)

            groups(dve, body, after_batch)


RMS_EPS = 1e-6
FILLS = PER_KV + 1


def rms_gqa_stage(nc, name, res, t):
    with ExitStack() as ctx:
        sem = ctx.enter_context(Semaphores(nc, name))
        sb = lambda what, shape, dt=F32: ctx.enter_context(nc.sbuf_tensor(f"{name}_{what}", shape, dt))
        banks = [ctx.enter_context(nc.psum_tensor(f"{name}_bank{i}", [P, HALF], F32)) for i in range(8)]
        acc, s_bank, o_bank, sum_bank = banks[:2], banks[2:6], banks[6], banks[7]
        norm = Norm(nc, ctx, sem, f"{name}_ln", res, [b[:] for b in s_bank])

        kv_raw = sb("kv_raw", [P, GK_COLS])
        kv_hi, kv_lo = sb("kv_hi", [P, GK_COLS], F32R), sb("kv_lo", [P, GK_COLS], F32R)
        w_raw = sb("w_raw", [P, PER_KV, GQ_COLS])
        w_hi, w_lo = sb("w_hi", [P, PER_KV, GQ_COLS], F32R), sb("w_lo", [P, PER_KV, GQ_COLS], F32R)
        cos, sin = sb("cos", [P, S]), sb("sin", [P, S])
        half_turn, sum_sel, bv = sb("half_turn", [P, P]), sb("sum_sel", [P, P]), sb("bv", [P, P])
        ones = sb("ones", [P, 2])
        raw = sb("raw", [P, 2, S])
        square = sb("square", [P, 2, S])
        square_sums = sb("square_sums", [P, NT, 2])
        power, rms = sb("power", [P, 2 * NT]), sb("rms", [P, 2, NT])
        qk = sb("qk", [P, FILLS, TOK])
        scaled = sb("scaled", [P, 4, S])
        turned_part = sb("turned_part", [P, 2, S])
        k_hi, k_lo = sb("k_hi", [P, KV_HEADS, TOK], F32R), sb("k_lo", [P, KV_HEADS, TOK], F32R)
        q_hi, q_lo = sb("q_hi", [P, S], F32R), sb("q_lo", [P, S], F32R)
        v = sb("v", [P, NT, P])
        exps = sb("exps", [P, 2, KV_HEADS, S])
        o_raw, o = sb("o_raw", [P, S]), sb("o", [P, S])
        o_hi, o_lo = sb("o_hi", [P, S], F32R), sb("o_lo", [P, S], F32R)

        loaded, kv_hi_done, kv_split, w_hi_done, w_split = (
            sem("loaded"), sem("kv_hi_done"), sem("kv_split"), sem("w_hi_done"), sem("w_split"))
        k_cleared = sem("k_cleared")
        fill_ready, fill_copied, fill_squared, fill_summed = (
            sem("fill_ready"), sem("fill_copied"), sem("fill_squared"), sem("fill_summed"))
        v_ready, v_done, sums_read, rms_step, rms_done = (
            sem("v_ready"), sem("v_done"), sem("sums_read"), sem("rms_step"), sem("rms_done"))
        rms_spread, rms_applied, half_turned, half_read, cos_part, part_done = (
            sem("rms_spread"), sem("rms_applied"), sem("half_turned"), sem("half_read"), sem("cos_part"), sem("part_done"))
        k_hi_done, k_lo_done, q_hi_done, q_lo_done = sem("k_hi_done"), sem("k_lo_done"), sem("q_hi_done"), sem("q_lo_done")
        scores_ready, exp_done, o_ready, o_copied, sum_spread, inverse_done, o_done = (
            sem("scores_ready"), sem("exp_done"), sem("o_ready"), sem("o_copied"), sem("sum_spread"),
            sem("inverse_done"), sem("o_done"))
        o_hi_done, o_lo_done, out_done, acc_read = sem("o_hi_done"), sem("o_lo_done"), sem("out_done"), sem("acc_read")
        pair = lambda hi, lo, *at: (hi[(slice(None), *at)], lo[(slice(None), *at)])
        fills = [(b, f) for b in range(B) for f in range(FILLS)]
        batch = lambda b: slice(b * S, (b + 1) * S)

        block = ctx.enter_context(nc.Block())

        @block.sync
        def _(sp):
            sp.dma_start(kv_raw[:], t["wd_kv"]).then_inc(loaded, 16)
            sp.dma_start(w_raw[:], t["wd_q"].rearrange("c p n -> p c n")).then_inc(loaded, 16)
            for to, src in ((cos, "cos"), (sin, "sin"), (half_turn, "half_turn"), (sum_sel, "sum_sel")):
                sp.dma_start(to[:], t[src]).then_inc(loaded, 16)
            sp.dma_start(bv[:], t["v_ones"].partition_broadcast(P)).then_inc(loaded, 16)

        @block.gpsimd
        def _(pool):
            pool.memset(power[:], -0.5).then_inc(rms_step, 1)
            pool.memset(ones[:], 1.0).then_inc(k_cleared, 1)
            pool.memset(f32(k_hi[:]), 0.0).then_inc(k_cleared, 1)
            pool.memset(f32(k_lo[:]), 0.0).then_inc(k_cleared, 1)
            norm.gpsimd(pool)
            pool.wait_ge(sums_read, 2)
            pool.tensor_scalar(rms[:, 0, :], square_sums[:, :, 0], 1.0 / (Q_HEADS * HD), RMS_EPS, ALU.mult, ALU.add).then_inc(rms_step, 1)
            pool.tensor_scalar(rms[:, 1, :], square_sums[:, :, 1], 1.0 / (KV_HEADS * HD), RMS_EPS, ALU.mult, ALU.add).then_inc(rms_step, 1)
            pool.wait_ge(rms_step, 3)
            flat = rms[:].rearrange("p a t -> p (a t)")
            pool.tensor_tensor(flat, flat, power[:], ALU.pow).then_inc(rms_step, 1)
            pool.wait_ge(rms_step, 4)
            pool.tensor_scalar(rms[:, 0, :], rms[:, 0, :], HD ** -0.5, None, ALU.mult).then_inc(rms_done, 1)

        @block.tensor
        def _(pe):
            norm.tensor(pe)
            pe.wait_ge(norm.lo_done, NHALF * DC)
            pe.wait_ge(kv_split, 1)
            pe.wait_ge(w_split, 1)
            pe.wait_ge(k_cleared, 1)

            def sum_squares(m):
                b, f = fills[m]
                pe.wait_ge(fill_squared, m + 1)
                for j in range(TB):
                    at = 2 * ((b * TB + j) * 2 + (f == PER_KV))
                    last = pe.matmul(sum_bank[:, at:at + 2], square[:, m % 2, j * P:(j + 1) * P], ones[:],
                                     start=m == 0 and j == 0, stop=f >= PER_KV - 1, skip_group_check=True)
                last.then_inc(fill_summed, 1)

            for m, (b, f) in enumerate(fills):
                if m >= 4:
                    pe.wait_ge(fill_squared, m - 3)
                for c in range(DC):
                    at = slice(c * P, (c + 1) * P)
                    w = pair(w_hi, w_lo, f, at) if f < PER_KV else pair(kv_hi, kv_lo, at)
                    last = product(pe, s_bank[m % 4][:], w, pair(res.xh, res.xl, c, batch(b)), c == 0, c == DC - 1)
                last.then_inc(fill_ready, 1)
                if m:
                    sum_squares(m - 1)
            sum_squares(len(fills) - 1)
            for h in range(NHALF):
                for j in range(TB):
                    for c in range(DC):
                        at = slice((h * TB + j) * P, (h * TB + j + 1) * P)
                        last = product(pe, acc[h][:, j * P:(j + 1) * P], pair(res.xh, res.xl, c, at),
                                       pair(kv_hi, kv_lo, slice((DC + c) * P, (DC + c + 1) * P)),
                                       j == 0 and c == 0, c == DC - 1)
                last.then_inc(v_ready, 1)
            pe.wait_ge(rms_done, 1)
            for m in range(2 * B):
                b, a = divmod(m, 2)
                pe.wait_ge(rms_applied, m)
                if m < 2:
                    pe.wait_ge(fill_squared, len(fills))
                for j in range(TB):
                    last = pe.matmul(s_bank[a][:, j * P:(j + 1) * P],
                                     rms[:, a, b * TB + j:b * TB + j + 1].broadcast_to([P, P]), res.ident[:],
                                     start=j == 0, stop=True, skip_group_check=True)
                last.then_inc(rms_spread, 1)
                if a:
                    for f in range(FILLS):
                        k = b * FILLS + f
                        if k >= 2:
                            pe.wait_ge(half_read, k - 1)
                        pe.matmul(s_bank[2 + k % 2][:], half_turn[:], qk[:, f, batch(b)],
                                  start=True, stop=True, skip_group_check=True).then_inc(half_turned, 1)

            def clear():
                for bank in acc:
                    pe.matmul(bank[:], res.zeros[:, 0:P], res.zeros[:], start=True, stop=False, skip_group_check=True)

            def attend(b, G, step, j):
                pe.wait_ge(exp_done, 16 * G + 4 * (j + 1))
                if j == 0:
                    pe.wait_ge(o_copied, G)
                for g in range(KV_HEADS):
                    slot = slice(g * SLOT, (g + 1) * SLOT)
                    last = pe.matmul(o_bank[slot, :], v[:, b * TB + j, slot], exps[:, j % 2, g, :],
                                     start=j == 0, stop=j == TB - 1, skip_group_check=True)
                last.then_inc(o_ready, 1)

            def finish(c_static_unused, G):
                pe.wait_ge(o_copied, G + 1)
                pe.wait_ge(o_done, G)
                pe.matmul(sum_bank[:], sum_sel[:], o_raw[:], start=True, stop=True,
                          skip_group_check=True).then_inc(sum_spread, 1)

            def project_out(c, G):
                pe.wait_ge(o_lo_done, G + 1)
                for j in range(TB):
                    wo = (w_hi[:, c, DC * P:GQ_COLS], w_lo[:, c, DC * P:GQ_COLS])
                    last = product(pe, acc[j // 2][:, j % 2 * D:(j % 2 + 1) * D], pair(o_hi, o_lo, slice(j * P, (j + 1) * P)),
                                   wo, False, True)
                last.then_inc(out_done, 1)

            def scores(b, G, j):
                for g in range(KV_HEADS):
                    pe.wait_ge(exp_done, 16 * G + 4 * j + g - 3 if j else 16 * G)
                    product(pe, s_bank[g][:], pair(k_hi, k_lo, g, slice(b * S + j * P, b * S + (j + 1) * P)),
                            pair(q_hi, q_lo, slice(None)), True, True).then_inc(scores_ready, 1)

            def body(b, c, G, first):
                pe.wait_ge(q_lo_done, G + 1)
                scores(b, G, 0)
                if not first:
                    finish(None, G - 1)
                scores(b, G, 1)
                attend(b, G, 0, 0)
                if not first:
                    project_out(c - 1, G - 1)
                for j in range(2, TB):
                    scores(b, G, j)
                    attend(b, G, 0, j - 1)
                attend(b, G, 0, TB - 1)

            pe.wait_ge(k_hi_done, B * KV_HEADS)
            pe.wait_ge(k_lo_done, B * KV_HEADS)
            pe.wait_ge(v_done, NHALF)
            for b in range(B):
                if b:
                    pe.wait_ge(acc_read, 2 * b)
                clear()
                body(b, 0, b * PER_KV, True)
                with pe.Fori(1, PER_KV) as c:
                    body(b, c, c + b * PER_KV, False)
                finish(None, (b + 1) * PER_KV - 1)
                project_out(PER_KV - 1, (b + 1) * PER_KV - 1)

        @block.scalar
        def _(act):
            act.wait_ge(loaded, 16 * 7)
            act.activation(kv_hi[:], kv_raw[:], ACT.Copy).then_inc(kv_hi_done, 1)
            act.activation(w_hi[:], w_raw[:], ACT.Copy).then_inc(w_hi_done, 1)
            norm.scalar(act)
            for m, (b, f) in enumerate(fills):
                act.wait_ge(fill_ready, m + 1)
                if m >= 2:
                    act.wait_ge(fill_summed, m - 1)
                act.activation(qk[:, f, batch(b)], s_bank[m % 4][:], ACT.Copy).then_inc(fill_copied, 1)
                act.wait_ge(fill_copied, m + 1)
                act.activation(square[:, m % 2, :], qk[:, f, batch(b)], ACT.Square).then_inc(fill_squared, 1)
            act.wait_ge(k_cleared, 3)
            for b in range(B):
                act.wait_ge(part_done, (b + 1) * FILLS)
                for g in range(KV_HEADS):
                    slot = slice(g * SLOT, (g + 1) * SLOT)
                    act.activation(k_hi[slot, g, batch(b)], qk[slot, PER_KV, batch(b)], ACT.Copy).then_inc(k_hi_done, 1)

            def body(b, c, G):
                act.wait_ge(scores_ready, 16 * G)
                act.activation(q_hi[:], qk[:, bass.ds(c, 1), batch(b)].rearrange("p a n -> p (a n)"),
                               ACT.Copy).then_inc(q_hi_done, 1)
                for j in range(TB):
                    act.wait_ge(o_ready, 4 * G + j - 1 if j else 4 * G)
                    for g in range(KV_HEADS):
                        act.wait_ge(scores_ready, 16 * G + 4 * j + g + 1)
                        act.activation(exps[:, j % 2, g, :], s_bank[g][:], ACT.Exp).then_inc(exp_done, 1)
                act.wait_ge(sum_spread, G)
                act.wait_ge(o_done, G)
                act.wait_ge(o_ready, 4 * G + 4)
                act.activation(o_raw[:], o_bank[:], ACT.Copy).then_inc(o_copied, 1)

            for b in range(B):
                with act.Fori(0, PER_KV) as c:
                    body(b, c, c + b * PER_KV)

        @block.vector
        def _(dve):
            dve.wait_ge(kv_hi_done, 1)
            dve.tensor_tensor(kv_lo[:], kv_raw[:], f32(kv_hi[:]), ALU.subtract).then_inc(kv_split, 1)
            norm.vector(dve)
            dve.wait_ge(w_hi_done, 1)
            dve.tensor_tensor(w_lo[:], w_raw[:], f32(w_hi[:]), ALU.subtract).then_inc(w_split, 1)
            for h in range(NHALF):
                dve.wait_ge(v_ready, h + 1)
                dve.tensor_tensor(v[:, h * TB:(h + 1) * TB, :], acc[h][:].rearrange("p (j n) -> p j n", n=P),
                                  bv[:].unsqueeze(1).broadcast_to([P, TB, P]), ALU.add).then_inc(v_done, 1)
            dve.wait_ge(fill_summed, len(fills))
            sums = sum_bank[:, 0:4 * NT].rearrange("p (t a two) -> p t a two", t=NT, a=2)[:, :, :, 0]
            dve.tensor_copy(square_sums[:], sums).then_inc(sums_read, 2)
            for b in range(B):
                for a in range(2):
                    m = 2 * b + a
                    dve.wait_ge(rms_spread, m + 1)
                    if b:
                        dve.wait_ge(part_done, b * FILLS)
                    dve.tensor_tensor(scaled[:, 2 * a, :], s_bank[a][:], cos[:], ALU.mult)
                    dve.tensor_tensor(scaled[:, 2 * a + 1, :], s_bank[a][:], sin[:], ALU.mult).then_inc(rms_applied, 1)
                dve.wait_ge(rms_applied, 2 * b + 2)
                for f in range(FILLS):
                    k, a = b * FILLS + f, 2 * (f == PER_KV)
                    now = qk[:, f, batch(b)]
                    dve.wait_ge(half_turned, k + 1)
                    dve.tensor_tensor(turned_part[:, k % 2, :], s_bank[2 + k % 2][:], scaled[:, a + 1, :],
                                      ALU.mult).then_inc(half_read, 1)
                    dve.tensor_tensor(now, now, scaled[:, a, :], ALU.mult).then_inc(cos_part, 1)
                    dve.wait_ge(half_read, k + 1)
                    dve.wait_ge(cos_part, k + 1)
                    dve.tensor_tensor(now, now, turned_part[:, k % 2, :], ALU.add).then_inc(part_done, 1)
            for b in range(B):
                for g in range(KV_HEADS):
                    slot = slice(g * SLOT, (g + 1) * SLOT)
                    dve.wait_ge(k_hi_done, b * KV_HEADS + g + 1)
                    dve.tensor_tensor(k_lo[slot, g, batch(b)], qk[slot, PER_KV, batch(b)], f32(k_hi[slot, g, batch(b)]),
                                      ALU.subtract).then_inc(k_lo_done, 1)

            def split_q(b, c, G):
                dve.wait_ge(q_hi_done, G + 1)
                dve.tensor_tensor(q_lo[:], qk[:, bass.ds(c, 1), batch(b)].rearrange("p a n -> p (a n)"), f32(q_hi[:]),
                                  ALU.subtract).then_inc(q_lo_done, 1)

            def divide(G):
                dve.wait_ge(sum_spread, G + 1)
                dve.reciprocal(o[:], sum_bank[:]).then_inc(inverse_done, 1)
                dve.wait_ge(inverse_done, G + 1)
                dve.tensor_tensor(o[:], o[:], o_raw[:], ALU.mult).then_inc(o_done, 1)
                dve.wait_ge(o_done, G + 1)
                dve.wait_ge(out_done, G)
                dve.tensor_copy(o_hi[:], o[:]).then_inc(o_hi_done, 1)
                dve.wait_ge(o_hi_done, G + 1)
                dve.tensor_tensor(o_lo[:], o[:], f32(o_hi[:]), ALU.subtract).then_inc(o_lo_done, 1)

            for b in range(B):
                split_q(b, 0, b * PER_KV)
                with dve.Fori(1, PER_KV) as c:
                    split_q(b, c, c + b * PER_KV)
                    divide(c + b * PER_KV - 1)
                divide((b + 1) * PER_KV - 1)
                dve.wait_ge(out_done, (b + 1) * PER_KV)
                for a in range(2):
                    two = res.x[:, b * TB + 2 * a:b * TB + 2 * a + 2, :]
                    dve.tensor_tensor(two, acc[a][:].rearrange("p (t d) -> p t d", d=D), two, ALU.add).then_inc(acc_read, 1)


SEG = 64
PAIRS = S // (2 * SEG)
SEGS = S // SEG
CHAINS = B * GROUP
RUN = HEADS
RUNS = S // RUN
MZ = DH + 2


def recurrent_stage(nc, name, res, t):
    scale = 1.0 / DH ** 0.5
    with ExitStack() as ctx:
        sem = ctx.enter_context(Semaphores(nc, name))
        sb = lambda what, shape, dt=F32: ctx.enter_context(nc.sbuf_tensor(f"{name}_{what}", shape, dt))
        memory_bank = [ctx.enter_context(nc.psum_tensor(f"{name}_memory{b}", [P, 2, HALF], F32)) for b in range(B)]
        work = [ctx.enter_context(nc.psum_tensor(f"{name}_work{i}", [P, HALF], F32)) for i in range(4)]
        retrieved = [m[:].rearrange("p c (u n) -> p (c u) n", u=2) for m in memory_bank]

        read_nat = sb("read_nat", [P, CHAINS, PAIRS, DH])
        in_order = read_nat[:].rearrange("p m j n -> p m (j n)")
        norm = Norm(nc, ctx, sem, f"{name}_ln", res, [w[:] for w in work],
                    read_nat[:].rearrange("p a b n -> p (a b n)")[:, 0:NT * D].rearrange("p (t d) -> p t d", d=D))
        w_raw = sb("w_raw", [P, 3, DC * WIDE])
        w_hi, w_lo = sb("w_hi", [P, 3, DC * WIDE], F32R), sb("w_lo", [P, 3, DC * WIDE], F32R)
        k, q = sb("k", [P, CHAINS, S]), sb("q", [P, CHAINS, S])
        dot = q
        sigma = sb("sigma", [P, CHAINS, PAIRS, 4, SEG])
        sigma_k = sb("sigma_k", [P, CHAINS, PAIRS, DH])
        v = sb("v", [P, NT, WIDE])
        exp_part = sb("exp_part", [P, S])
        memory, delta = sb("memory", [P, CHAINS, MZ]), sb("delta", [P, CHAINS, MZ])
        inverse = sb("inverse", [P, CHAINS])
        seg_mask = sb("seg_mask", [P, P], BF16)
        probs, probs_t = sb("probs", [P, 2, TB, P]), sb("probs_t", [P, TB, P])
        neg_max, row_sum = sb("neg_max", [P, 2, TB]), sb("row_sum", [P, 2, TB])
        o_hi, o_lo = sb("o_hi", [P, 2, GROUP, CHAINS * RUNS], F32R), sb("o_lo", [P, 2, GROUP, CHAINS * RUNS], F32R)
        gate = sb("gate", [P, HEADS])
        neg_gate, rest_gate = sb("neg_gate", [P, GROUP]), sb("rest_gate", [P, GROUP])

        w_loaded = [sem(f"w_loaded{i}") for i in range(3)]
        w_split = [sem(f"w_split{i}") for i in range(3)]
        x_reloaded, x_stored, x_back = sem("x_reloaded"), sem("x_stored"), sem("x_back")
        w_hi_done, betas_loaded, gate_step, gates_done, mask_step = (
            sem("w_hi_done"), sem("betas_loaded"), sem("gate_step"), sem("gates_done"), sem("mask_step"))
        k_ready, q_ready, kq_copied, kq_read, clipped, sigma_in_order, sigma_done = (
            sem("k_ready"), sem("q_ready"), sem("kq_copied"), sem("kq_read"), sem("clipped"),
            sem("sigma_in_order"), sem("sigma_done"))
        v_ready, v_done, sigma_turned, sigma_k_done = sem("v_ready"), sem("v_done"), sem("sigma_turned"), sem("sigma_k_done")
        delta_set, memory_done, retrieved_ready, inverse_done, delta_done, read_done, update_ready = (
            sem("delta_set"), sem("memory_done"), sem("retrieved_ready"), sem("inverse_done"), sem("delta_done"),
            sem("read_done"), sem("update_ready"))
        scores_ready, max_raw, max_done, exp_done, sum_inverse, probs_done = (
            sem("scores_ready"), sem("max_raw"), sem("max_done"), sem("exp_done"), sem("sum_inverse"), sem("probs_done"))
        turned, probs_t_done, dot_ready, dot_done = sem("turned"), sem("probs_t_done"), sem("dot_ready"), sem("dot_done")
        read_turned, att_done, o_hi_done, o_lo_done, out_done, x_added = (
            sem("read_turned"), sem("att_done"), sem("o_hi_done"), sem("o_lo_done"), sem("out_done"), sem("x_added"))
        o_parts = HEADS // GROUP
        parts = [(t["wa_k"], 2, 0), (t["wa_q"], 0, 0), (t["wa_v"], 1, 0),
                 *((t["wa_o"][i:i + 1], i % 2, 1 + i // 2) for i in range(o_parts))]
        in_slot = (3, 3, 1)
        batch = lambda b: slice(b * S, (b + 1) * S)

        def dot_runs(i):
            return dot[:].rearrange("p m (n c) -> p (m n) c", c=RUN)[:, :, i * GROUP:(i + 1) * GROUP]

        def chain_runs(ap):
            return ap.rearrange("p c n -> p n c")

        def key_rows(seg):
            return slice(seg % 2 * SEG, seg % 2 * SEG + SEG)

        def query_rows(seg):
            return key_rows(seg + 1)

        x_in, x_mid = t["x"], t["x_mid"]

        def row_tiles(h):
            return res.x[h * RUNS:(h + 1) * RUNS, :, :]

        def rows_of(stream, b, h):
            at = h * SEG // RUN
            return stream[b].rearrange("(s g n) d -> s g n d", g=GROUPS, n=RUN)[:, :, at:at + SEG // RUN, :]

        block = ctx.enter_context(nc.Block())

        @block.sync
        def _(sp):
            sp.dma_start(gate[:], t["ba_gate"]).then_inc(betas_loaded, 16)
            def load(G, p):
                weights, slot, before = parts[p]
                sp.wait_ge(w_split[slot], in_slot[slot] * G + before)
                which = weights[bass.ds(G, 1), :, :] if p < 3 else weights
                sp.dma_start(w_raw[:, slot, :], which.rearrange("a p n -> (a p) n")).then_inc(w_loaded[slot], 16)

            def store(G):
                sp.wait_ge(x_added, B * (G + 1))
                for b in range(B):
                    for h in range(GROUP):
                        tile = row_tiles(h)[:, bass.ds(b * GROUPS + G, 1), :].rearrange("p a d -> p (a d)")
                        sp.dma_start(rows_of(x_mid, b, h)[:, bass.ds(G, 1), :, :].rearrange("s a u d -> s (a u) d"), tile
                                     ).then_inc(x_stored, 16)

            for p in range(5):
                load(0, p)
            sp.wait_ge(norm.normed, NT)
            for b in range(B):
                for h in range(GROUP):
                    for g in range(GROUPS):
                        sp.dma_start(row_tiles(h)[:, b * GROUPS + g, :], rows_of(x_in, b, h)[:, g, :, :]).then_inc(x_reloaded, 16)
            for p in range(5, len(parts)):
                load(0, p)
            with sp.Fori(1, GROUPS) as G:
                for p in range(5):
                    load(G, p)
                store(G - 1)
                for p in range(5, len(parts)):
                    load(G, p)
            store(GROUPS - 1)
            sp.wait_ge(x_stored, 16 * B * GROUP * GROUPS)
            sp.dma_start(res.x[:], x_mid.rearrange("b (t p) d -> p (b t) d", p=P)).then_inc(x_back, 16)
            sp.wait_ge(x_back, 16)

        @block.gpsimd
        def _(pool):
            pool.tensor_copy(seg_mask[:], res.causal[:]).then_inc(mask_step, 1)
            pool.wait_ge(mask_step, 1)
            pool.memset(seg_mask[SEG:P, 0:SEG], NEG).then_inc(mask_step, 1)
            pool.wait_ge(mask_step, 2)
            norm.gpsimd(pool)
            with pool.Fori(0, GROUPS) as G:
                users = ((k_ready, CHAINS * G), (out_done, o_parts * G), (out_done, o_parts * G),
                         (q_ready, CHAINS * G + CHAINS), (v_ready, NT * G + NT),
                         (out_done, o_parts * G + 1), (out_done, o_parts * G + 2))
                for p, (weights, slot, before) in enumerate(parts):
                    used, value = users[p]
                    pool.wait_ge(used, value)
                    pool.wait_ge(w_loaded[slot], 16 * (in_slot[slot] * G + before) + 16)
                    pool.tensor_tensor(w_hi[:, slot, :], w_raw[:, slot, :], res.zero[:].broadcast_to([P, DC * WIDE]),
                                       ALU.add).then_inc(w_hi_done, 1)
                    pool.wait_ge(w_hi_done, len(parts) * G + p + 1)
                    pool.tensor_tensor(w_lo[:, slot, :], w_raw[:, slot, :], f32(w_hi[:, slot, :]),
                                       ALU.subtract).then_inc(w_split[slot], 1)

        @block.tensor
        def _(pe):
            norm.tensor(pe)
            pe.wait_ge(norm.lo_done, NHALF * DC)
            pe.wait_ge(mask_step, 2)

            def project(G):
                for p, slot, ready in ((0, 2, k_ready), (1, 0, q_ready)):
                    pe.wait_ge(w_split[slot], in_slot[slot] * G + 1)
                    for m in range(CHAINS):
                        f, (b, h) = p * CHAINS + m, divmod(m, GROUP)
                        if f >= 4:
                            pe.wait_ge(kq_read, 2 * CHAINS * G + f - 3)
                        for c in range(DC):
                            w = slice(c * WIDE + h * DH, c * WIDE + (h + 1) * DH)
                            last = product(pe, work[f % 4][:], (w_hi[:, slot, w], w_lo[:, slot, w]),
                                           (res.xh[:, c, batch(b)], res.xl[:, c, batch(b)]), c == 0, c == DC - 1)
                        last.then_inc(ready, 1)
                pe.wait_ge(w_split[1], in_slot[1] * G + 1)
                for j in range(NT):
                    if j < 4:
                        pe.wait_ge(kq_read, 2 * CHAINS * G + 2 * CHAINS - 3 + j)
                    else:
                        pe.wait_ge(v_done, NT * G + j - 3)
                    for c in range(DC):
                        w, at = slice(c * WIDE, (c + 1) * WIDE), slice(j * P, (j + 1) * P)
                        last = product(pe, work[j % 4][:], (res.xh[:, c, at], res.xl[:, c, at]),
                                       (w_hi[:, 1, w], w_lo[:, 1, w]), c == 0, c == DC - 1)
                    last.then_inc(v_ready, 1)

            def turn_sigma_k(G, m):
                if m < 4:
                    pe.wait_ge(v_done, NT * G + m + 5)
                else:
                    pe.wait_ge(sigma_k_done, CHAINS * G + m - 3)
                pe.wait_ge(sigma_in_order, CHAINS * G + m + 1)
                for j in range(PAIRS):
                    at = slice(j * P, (j + 1) * P)
                    last = pe.transpose(work[m % 4][:, at], in_order[:, m, at], res.ident[:])
                last.then_inc(sigma_turned, 1)

            def retrieve(G, seg, b):
                pe.wait_ge(memory_done, 2 * SEGS * G + max(2 * seg + b + 1, 2))
                for h in range(GROUP):
                    m, side = b * GROUP + h, slice(seg % 2 * 2, seg % 2 * 2 + 2)
                    last = pe.matmul(retrieved[b][:, h, 0:MZ], sigma[:, m, seg // 2, side, :].rearrange("p a n -> p (a n)"),
                                     memory[:, m, :], start=True, stop=True, skip_group_check=True)
                last.then_inc(retrieved_ready, 1)

            def update(G, seg, b):
                pe.wait_ge(delta_done, 2 * SEGS * G + 2 * seg + b + 1)
                pe.wait_ge(read_done, 2 * SEGS * G + 2 * seg + b + 1)
                rows = key_rows(seg)
                for h in range(GROUP):
                    m = b * GROUP + h
                    last = pe.matmul(retrieved[b][:, h, 0:MZ], sigma_k[rows, m, seg // 2, :], delta[rows, m, :],
                                     start=True, stop=True, skip_group_check=True)
                last.then_inc(update_ready, 1)

            def scores(G, m):
                if m >= 2:
                    pe.wait_ge(exp_done, TB * CHAINS * G + TB * (m - 1))
                for j in range(TB):
                    at, to = slice(j * P, (j + 1) * P), work[m % 2][:, j * P:(j + 1) * P]
                    pe.matmul(to, q[:, m, at], k[:, m, at], start=j == 0, stop=False, skip_group_check=True)
                    last = pe.matmul(to, res.ident_bf[:], seg_mask[:], start=False, stop=True, skip_group_check=True)
                last.then_inc(scores_ready, 1)

            def attend(G, m):
                pe.wait_ge(probs_done, CHAINS * G + m + 1)
                pe.wait_ge(probs_t_done, CHAINS * G + m)
                for j in range(TB):
                    last = pe.transpose(work[2][:, j * P:(j + 1) * P], probs[:, m % 2, j, :], res.ident[:])
                last.then_inc(turned, 1)
                b, h = divmod(m, GROUP)
                pe.wait_ge(probs_t_done, CHAINS * G + m + 1)
                pe.wait_ge(dot_done, CHAINS * G + m)
                for j in range(TB):
                    last = pe.matmul(work[3][:, j * P:(j + 1) * P], v[:, b * TB + j, h * DH:(h + 1) * DH], probs_t[:, j, :],
                                     start=j == 0, stop=True, skip_group_check=True)
                last.then_inc(dot_ready, 1)

            def turn_read(G, m):
                if m >= 4:
                    pe.wait_ge(att_done, 2 * CHAINS * G + 2 * (m - 3))
                for j in range(PAIRS):
                    last = pe.transpose(work[m % 4][:, j * P:(j + 1) * P], read_nat[:, m, j, :], res.ident[:])
                last.then_inc(read_turned, 1)

            def project_out(G, i):
                slot = i % 2
                pe.wait_ge(w_split[slot], in_slot[slot] * G + 2 + i // 2)
                pe.wait_ge(o_lo_done, o_parts * G + i + 1)
                for n in range(GROUP):
                    c, w = i * GROUP + n, slice(n * D, (n + 1) * D)
                    for b in range(B):
                        at = slice(b * P, (b + 1) * P)
                        last = product(pe, memory_bank[b][:, 0, 0:D], (o_hi[:, slot, n, at], o_lo[:, slot, n, at]),
                                       (w_hi[:, slot, w], w_lo[:, slot, w]), c == 0, c == HEADS - 1)
                last.then_inc(out_done, 1)

            with pe.Fori(0, GROUPS) as G:
                pe.wait_ge(att_done, 2 * CHAINS * G)
                project(G)
                for m in range(CHAINS):
                    turn_sigma_k(G, m)
                pe.wait_ge(sigma_done, 2 * CHAINS * G + 2 * CHAINS)
                pe.wait_ge(x_added, B * G)
                pe.wait_ge(sigma_k_done, CHAINS * G + CHAINS)
                for seg in range(SEGS):
                    for b in range(B):
                        retrieve(G, seg, b)
                    scores(G, seg)
                    if seg < SEGS - 1:
                        for b in range(B):
                            update(G, seg, b)
                    if seg:
                        attend(G, seg - 1)
                attend(G, CHAINS - 1)
                pe.wait_ge(read_done, 2 * SEGS * (G + 1))
                pe.wait_ge(delta_done, 2 * SEGS * (G + 1))
                pe.wait_ge(exp_done, TB * CHAINS * (G + 1))
                pe.wait_ge(dot_done, CHAINS * (G + 1))
                for m in range(CHAINS):
                    turn_read(G, m)
                for i in range(o_parts):
                    project_out(G, i)

        @block.scalar
        def _(act):
            act.wait_ge(betas_loaded, 16)
            act.activation(gate[:], gate[:], ACT.Exp, scale=-1.0).then_inc(gate_step, 1)
            norm.scalar(act)

            def read_queries(G, seg, b):
                act.wait_ge(inverse_done, 2 * SEGS * G + 2 * seg + b + 1)
                rows = query_rows(seg)
                for h in range(GROUP):
                    m = b * GROUP + h
                    last = act.activation(read_nat[rows, m, seg // 2, :], retrieved[b][rows, h, 0:DH], ACT.Copy,
                                          scale=inverse[rows, m:m + 1])
                last.then_inc(read_done, 1)

            def exponentials(G, m):
                act.wait_ge(max_done, CHAINS * G + m + 1)
                act.wait_ge(turned, CHAINS * G + max(m - 1, 0))
                for j in range(TB):
                    act.activation(probs[:, m % 2, j, :], work[m % 2][:, j * P:(j + 1) * P], ACT.Exp, scale=scale,
                                   bias=neg_max[:, m % 2, j:j + 1],
                                   accum_out=row_sum[:, m % 2, j:j + 1]).then_inc(exp_done, 1)

            def softmax_part(G, m):
                act.wait_ge(turned, CHAINS * G + m + 1)
                act.wait_ge(dot_ready, CHAINS * G + m)
                act.activation(probs_t[:].rearrange("p j n -> p (j n)"), work[2][:], ACT.Copy).then_inc(probs_t_done, 1)
                act.wait_ge(dot_ready, CHAINS * G + m + 1)
                act.activation(dot[:, m, :], work[3][:], ACT.Copy,
                               scale=rest_gate[:, m % GROUP:m % GROUP + 1]).then_inc(dot_done, 1)

            with act.Fori(0, GROUPS) as G:
                act.wait_ge(out_done, o_parts * G)
                for p, (to, ready) in enumerate(((k, k_ready), (q, q_ready))):
                    for m in range(CHAINS):
                        f = 2 * CHAINS * G + p * CHAINS + m
                        act.wait_ge(ready, CHAINS * G + m + 1)
                        act.activation(to[:, m, :], work[m % 4][:], ACT.Copy).then_inc(kq_copied, 1)
                        act.wait_ge(sigma_done, f)
                        act.activation(exp_part[:], work[m % 4][:], ACT.Exp).then_inc(kq_read, 1)
                for m in range(CHAINS):
                    act.wait_ge(sigma_turned, CHAINS * G + m + 1)
                    act.activation(sigma_k[:, m, :, :].rearrange("p j n -> p (j n)"), work[m % 4][:],
                                   ACT.Copy).then_inc(sigma_k_done, 1)
                act.wait_ge(gates_done, 2 * G + 2)
                for seg in range(SEGS):
                    for b in range(B):
                        read_queries(G, seg, b)
                    exponentials(G, seg)
                    if seg:
                        softmax_part(G, seg - 1)
                softmax_part(G, CHAINS - 1)
                act.wait_ge(att_done, 2 * CHAINS * (G + 1))
                for i in range(o_parts):
                    if i >= 2:
                        act.wait_ge(out_done, o_parts * G + i - 1)
                    act.activation(chain_runs(o_hi[:, i % 2]), dot_runs(i), ACT.Copy).then_inc(o_hi_done, 1)

        @block.vector
        def _(dve):
            dve.wait_ge(gate_step, 1)
            dve.tensor_scalar(gate[:], gate[:], 1.0, None, ALU.add).then_inc(gate_step, 1)
            dve.wait_ge(gate_step, 2)
            dve.reciprocal(gate[:], gate[:]).then_inc(gate_step, 1)
            dve.memset(delta[:], 0.0).then_inc(delta_set, 1)
            dve.wait_ge(delta_set, 1)
            dve.memset(delta[:, :, DH:DH + 1], -1.0).then_inc(delta_set, 1)
            norm.vector(dve)
            dve.wait_ge(gate_step, 3)

            def feature_map(G, p, m):
                f = 2 * CHAINS * G + p * CHAINS + m
                dve.wait_ge(kq_read, f + 1)
                dve.tensor_scalar(exp_part[:], exp_part[:], 1.0, None, ALU.min).then_inc(clipped, 1)
                dve.wait_ge(clipped, f + 1)
                of, sides = (q, (1, 2)) if p else (k, (0, 3))
                split = lambda ap: ap.rearrange("p (j s n) -> p j s n", s=2, n=SEG)
                if p == 0:
                    dve.scalar_tensor_tensor(in_order[:, m, :], k[:, m, :], 0.0, exp_part[:],
                                             ALU.max, ALU.add).then_inc(sigma_in_order, 1)
                for s, side in enumerate(sides):
                    last = dve.scalar_tensor_tensor(sigma[:, m, :, side, :], split(of[:, m, :])[:, :, s, :], 0.0,
                                                    split(exp_part[:])[:, :, s, :], ALU.max, ALU.add)
                last.then_inc(sigma_done, 1)

            def deltas(G, seg, b):
                rows, mine = key_rows(seg), slice(b * GROUP, (b + 1) * GROUP)
                dve.wait_ge(retrieved_ready, 2 * SEGS * G + 2 * seg + b + 1)
                dve.reciprocal(inverse[:, mine], retrieved[b][:, :, DH]).then_inc(inverse_done, 1)
                dve.wait_ge(inverse_done, 2 * SEGS * G + 2 * seg + b + 1)
                for h in range(GROUP):
                    m = b * GROUP + h
                    last = dve.scalar_tensor_tensor(delta[rows, m, 0:DH], retrieved[b][rows, h, 0:DH], inverse[rows, m:m + 1],
                                                    v[rows, b * TB + seg // 2, h * DH:(h + 1) * DH], ALU.mult, ALU.add)
                last.then_inc(delta_done, 1)

            def remember(G, seg, b):
                mine = slice(b * GROUP, (b + 1) * GROUP)
                dve.wait_ge(update_ready, 2 * (SEGS - 1) * G + 2 * seg + b + 1)
                dve.tensor_tensor(memory[:, mine, :], memory[:, mine, :], retrieved[b][:, :, 0:MZ],
                                  ALU.add).then_inc(memory_done, 1)

            def maximum(G, m):
                dve.wait_ge(scores_ready, CHAINS * G + m + 1)
                dve.tensor_reduce(neg_max[:, m % 2, :], work[m % 2][:].rearrange("p (j n) -> p j n", n=P), AX.X, ALU.max,
                                  negate=True).then_inc(max_raw, 1)
                dve.wait_ge(max_raw, CHAINS * G + m + 1)
                dve.tensor_scalar(neg_max[:, m % 2, :], neg_max[:, m % 2, :], scale, None, ALU.mult).then_inc(max_done, 1)

            def normalise(G, m):
                dve.wait_ge(exp_done, TB * CHAINS * G + TB * (m + 1))
                dve.reciprocal(row_sum[:, m % 2, :], row_sum[:, m % 2, :]).then_inc(sum_inverse, 1)
                dve.wait_ge(sum_inverse, CHAINS * G + m + 1)
                dve.tensor_tensor(probs[:, m % 2, :, :], probs[:, m % 2, :, :], spread(row_sum[:, m % 2, :], P),
                                  ALU.mult).then_inc(probs_done, 1)

            def mix(G, m):
                dve.wait_ge(read_turned, CHAINS * G + m + 1)
                dve.wait_ge(dot_done, CHAINS * G + m + 1)
                halves = lambda ap: ap.rearrange("p (j s n) -> p j s n", s=2, n=SEG)
                for s in range(2):
                    dve.scalar_tensor_tensor(halves(dot[:, m, :])[:, :, s, :], halves(work[m % 4][:])[:, :, 1 - s, :],
                                             neg_gate[:, m % GROUP:m % GROUP + 1], halves(dot[:, m, :])[:, :, s, :],
                                             ALU.mult, ALU.add).then_inc(att_done, 1)

            def low_part(G, i):
                dve.wait_ge(o_hi_done, o_parts * G + i + 1)
                if i >= 2:
                    dve.wait_ge(out_done, o_parts * G + i - 1)
                dve.tensor_tensor(chain_runs(o_lo[:, i % 2]), dot_runs(i), f32(chain_runs(o_hi[:, i % 2])),
                                  ALU.subtract).then_inc(o_lo_done, 1)

            with dve.Fori(0, GROUPS) as G:
                dve.wait_ge(out_done, o_parts * G)
                dve.tensor_scalar(neg_gate[:], gate[:, bass.ds(G * GROUP, GROUP)], -1.0, None, ALU.mult).then_inc(gates_done, 1)
                dve.tensor_scalar(rest_gate[:], gate[:, bass.ds(G * GROUP, GROUP)], -1.0, 1.0, ALU.mult,
                                  ALU.add).then_inc(gates_done, 1)
                dve.memset(memory[:, :, DH + 1:MZ], 0.0)
                dve.memset(memory[:, :, 0:DH], 0.0).then_inc(memory_done, 1)
                dve.memset(memory[:, :, DH:DH + 1], -1.0 / DH).then_inc(memory_done, 1)
                for p in range(2):
                    for m in range(CHAINS):
                        feature_map(G, p, m)
                for j in range(NT):
                    dve.wait_ge(v_ready, NT * G + j + 1)
                    dve.tensor_copy(v[:, j, :], work[j % 4][:]).then_inc(v_done, 1)
                for seg in range(SEGS):
                    for b in range(B):
                        deltas(G, seg, b)
                    maximum(G, seg)
                    if seg < SEGS - 1:
                        for b in range(B):
                            remember(G, seg, b)
                    normalise(G, seg)
                for m in range(CHAINS):
                    mix(G, m)
                for i in range(o_parts):
                    low_part(G, i)
                dve.wait_ge(out_done, o_parts * (G + 1))
                dve.wait_ge(x_reloaded, 16 * B * GROUP * GROUPS)
                for b in range(B):
                    tile = res.x[:, bass.ds(b * GROUPS + G, 1), :].rearrange("p a d -> p (a d)")
                    dve.tensor_tensor(tile, memory_bank[b][:, 0, 0:D], tile, ALU.add).then_inc(x_added, 1)


class Residual:

    def __init__(self, nc, ctx):
        sb = lambda what, shape, dt=F32: ctx.enter_context(nc.sbuf_tensor(what, shape, dt))
        self.x = sb("x", [P, NT, D])
        self.xh, self.xl = sb("xn_t_hi", [P, DC, TOK], F32R), sb("xn_t_lo", [P, DC, TOK], F32R)
        self.ident = sb("ident", [P, P])
        self.ident_bf = sb("ident_bf", [P, P], BF16)
        self.causal = sb("causal", [P, P], BF16)
        self.zeros = sb("zeros", [P, HALF], BF16)
        self.zero = sb("zero", [P, 1])
        self.iota = sb("iota", [P, NT, N_EXP])


def load_stage(nc, res, x, consts):
    with ExitStack() as ctx:
        loaded = ctx.enter_context(nc.semaphore("start_loaded"))
        made = ctx.enter_context(nc.semaphore("constants_made"))
        block = ctx.enter_context(nc.Block())

        @block.sync
        def _(sp):
            sp.dma_start(res.ident[:], consts["ident"]).then_inc(loaded, 16)
            sp.dma_start(res.x[:], x.rearrange("b (t p) d -> p (b t) d", p=P)).then_inc(loaded, 16)
            sp.dma_start(res.iota[:], consts["iota"]).then_inc(loaded, 16)
            sp.wait_ge(loaded, 48)

        @block.vector
        def _(dve):
            dve.memset(res.zeros[:], 0.0).then_inc(made, 1)
            dve.wait_ge(loaded, 48)
            dve.tensor_copy(res.ident_bf[:], res.ident[:]).then_inc(made, 1)

        @block.gpsimd
        def _(pool):
            pool.memset(res.causal[:], 0.0).then_inc(made, 1)
            pool.memset(res.zero[:], 0.0).then_inc(made, 1)
            pool.wait_ge(made, 4)
            pool.affine_select(out=res.causal[:], in_=res.causal[:], compare_op=ALU.is_ge, fill=NEG,
                               base=0, pattern=[[-1, P]], channel_multiplier=1).then_inc(made, 1)
            pool.wait_ge(made, 5)


def store_stage(nc, res, out):
    with ExitStack() as ctx:
        stored = ctx.enter_context(nc.semaphore("stored"))
        block = ctx.enter_context(nc.Block())

        @block.sync
        def _(sp):
            sp.dma_start(out.rearrange("b (t p) d -> p (b t) d", p=P), res.x[:]).then_inc(stored, 16)
            sp.wait_ge(stored, 16)


STAGES = ['L0_attn_a', 'L0_ffn', 'L0_attn_b', 'L0_ffn', 'L1_attn_a', 'L1_ffn', 'L1_attn_b', 'L1_ffn']


def build_program(nc, t, out, stages=STAGES):
    with ExitStack() as ctx:
        res = Residual(nc, ctx)
        t = {**t, "x_mid": nc.dram_tensor("x_mid", (B, S, D), F32, kind="Internal").ap()}
        load_stage(nc, res, t["x"], t)
        for n, kind in enumerate(stages):
            name = f"s{n}"
            if kind == "L0_attn_a":
                recurrent_stage(nc, name, res, t)
            if kind == "L0_ffn":
                ffn_stage(nc, name, res, t["ffn0"], t["gate0"], True, False)
            if kind == "L0_attn_b":
                wide_stage(nc, name, res, t)
            if kind == "L1_attn_a":
                causal_gqa_stage(nc, name, res, t)
            if kind == "L1_attn_b":
                rms_gqa_stage(nc, name, res, t)
            if kind == "L1_ffn":
                ffn_stage(nc, name, res, t["ffn1"], t["gate1"], False, True)
        store_stage(nc, res, out)



def ffn_layout(np, gate, up, down, owners):
    n = -(-len(owners) // P)
    whole = np.zeros((n, P, FFN_COLS), np.float32)
    for k in range(n):
        at = slice(k * P, min((k + 1) * P, len(owners)))
        m = at.stop - at.start
        for c in range(DC):
            whole[k, :, W_GATE + c * P:W_GATE + c * P + m] = gate[at, c * P:(c + 1) * P].T
            whole[k, :, W_UP + c * P:W_UP + c * P + m] = up[at, c * P:(c + 1) * P].T
        whole[k, :m, W_DOWN:W_DOWN + D] = down[at]
        whole[k, owners[at], W_SEL + np.arange(m)] = 1.0
    return whole


def router_layout(np, *rows):
    gates = np.zeros((GATES, D), np.float32)
    at = 0
    for r in rows:
        gates[at:at + len(r)] = r
        at += len(r)
    return np.ascontiguousarray(gates.T.reshape(DC, P, GATES).transpose(1, 0, 2))


def slots(np, a):
    whole = np.zeros((*a.shape[:-2], KV_HEADS, SLOT), a.dtype)
    whole[..., :HD] = a
    return whole.reshape(*a.shape[:-2], P)


def gqa_layout(np, wq, wk, wv, wo):
    chunked = lambda w: w.reshape(*w.shape[:-2], DC, P, P).swapaxes(-3, -2).reshape(*w.shape[:-2], P, DC * P)
    q = slots(np, wq.reshape(D, KV_HEADS, PER_KV, HD).transpose(2, 0, 1, 3))
    o = slots(np, wo.T.reshape(D, KV_HEADS, PER_KV, HD).transpose(2, 0, 1, 3)).transpose(0, 2, 1)
    kv = [chunked(slots(np, w.reshape(D, KV_HEADS, HD))) for w in (wk, wv)]
    return np.concatenate([chunked(q), o], 2), np.concatenate(kv, 1)


def layout(np, i):
    owners = lambda shared: np.concatenate([np.repeat(np.arange(N_EXP), INTER), np.full(shared, N_EXP)])
    w13, gu, w1 = i["L0_ffn_w13"], i["L0_ffn_shared_gate_up_w"], i["L1_ffn_w1"]
    t = {
        "x": i["L0_attn_a_x"],
        "ident": np.eye(P, dtype=np.float32),
        "iota": np.ascontiguousarray(np.broadcast_to(np.arange(N_EXP, dtype=np.float32), (P, NT, N_EXP))),
        "gate0": router_layout(np, i["L0_ffn_gate_w"], i["L0_ffn_shared_gate_w"]),
        "gate1": router_layout(np, i["L1_ffn_gate_w"]),
        "ffn0": ffn_layout(
            np, np.concatenate([w13[:, :INTER].reshape(-1, D), gu[:SHARED0]]),
            np.concatenate([w13[:, INTER:].reshape(-1, D), gu[SHARED0:]]),
            np.concatenate([i["L0_ffn_w2"].transpose(0, 2, 1).reshape(-1, D), i["L0_ffn_shared_down_w"].T]),
            owners(SHARED0)),
        "ffn1": ffn_layout(
            np, np.concatenate([w1[:, :, :INTER].transpose(0, 2, 1).reshape(-1, D), i["L1_ffn_sw1"]]),
            np.concatenate([w1[:, :, INTER:].transpose(0, 2, 1).reshape(-1, D), i["L1_ffn_sw2"]]),
            np.concatenate([i["L1_ffn_w2"].reshape(-1, D), i["L1_ffn_sw3"].T]),
            owners(SHARED1)),
    }
    grouped = lambda w: w.reshape(DC, P, GROUPS, WIDE).transpose(2, 1, 0, 3).reshape(GROUPS, P, DC * WIDE)
    grouped_out = lambda w: w.reshape(GROUPS, GROUP, DH, D).transpose(0, 2, 1, 3).reshape(GROUPS, DH, GROUP * D)
    for n in "kqv":
        t[f"wa_{n}"] = grouped(i[f"L0_attn_a_W{n}"])
    t["wa_o"] = grouped_out(i["L0_attn_a_Wo"])
    t["ba_gate"] = i["L0_attn_a_betas"][0, :, 0, :].T
    t["wb_q"] = i["L0_attn_b_Wq"].reshape(DC, P, HEADS * DH).transpose(1, 0, 2)
    t["wb_k"], t["wb_v"] = grouped(i["L0_attn_b_Wk"]), grouped(i["L0_attn_b_Wv"])
    t["wb_o"] = grouped_out(i["L0_attn_b_Wo"])
    t["bb_q"] = i["L0_attn_b_bq"].reshape(HEADS, DH).T
    t["bb_k"] = i["L0_attn_b_bk"].reshape(GROUPS, GROUP, DH).transpose(0, 2, 1)
    t["bb_v"] = i["L0_attn_b_bv"].reshape(GROUPS, WIDE)
    t["bb_o"] = i["L0_attn_b_bo"]
    wq, wk, wv, wo = (i[f"L1_attn_a_W{n}"].T for n in "qkvo")
    t["wc_q"], t["wc_kv"] = gqa_layout(np, wq, wk, wv, wo)
    t["bc_q"] = slots(np, i["L1_attn_a_bq"].reshape(KV_HEADS, PER_KV, HD).transpose(1, 0, 2)).T
    t["bc_k"] = slots(np, i["L1_attn_a_bk"].reshape(KV_HEADS, HD))[:, None]
    t["bc_v"] = slots(np, i["L1_attn_a_bv"].reshape(KV_HEADS, HD))
    t["bc_o"] = i["L1_attn_a_bo"]
    inverse = np.float32(10000.0) ** (-2.0 * np.arange(HD // 2, dtype=np.float32) / HD).astype(np.float32)
    theta = np.arange(S, dtype=np.float32)[:, None] * inverse[None, :]
    both = np.concatenate([np.cos(theta) + np.sin(theta)] * 2, 1).astype(np.float32)
    by_slot = lambda table: slots(np, np.broadcast_to(table[:, None, :], (S, KV_HEADS, HD))).T
    t["turn_k"] = by_slot(both)
    t["turn_q"] = t["turn_k"] * np.float32(HD ** -0.5)
    wq, wk, wv, wo = (i[f"L1_attn_b_W{n}"] for n in ("q", "k", "v", "out"))
    t["wd_q"], t["wd_kv"] = gqa_layout(np, wq, wk, wv, wo)
    fraction = np.arange(0, HD, 2, dtype=np.float32) / np.float32(HD)
    sinusoid = np.arange(S, dtype=np.float32)[:, None] * (np.float32(1.0) / np.float32(10000.0) ** fraction)[None, :]
    t["cos"], t["sin"] = (by_slot(np.concatenate([f(sinusoid)] * 2, 1).astype(np.float32)) for f in (np.cos, np.sin))
    turn = np.zeros((SLOT, SLOT), np.float32)
    half = HD // 2
    turn[half + np.arange(half), np.arange(half)] = -1.0
    turn[np.arange(half), half + np.arange(half)] = 1.0
    t["half_turn"] = np.kron(np.eye(KV_HEADS, dtype=np.float32), turn)
    t["v_ones"] = np.tile(np.arange(SLOT) == HD, KV_HEADS).astype(np.float32)
    t["sum_sel"] = np.kron(np.eye(KV_HEADS, dtype=np.float32), np.outer(np.arange(SLOT) == HD, np.ones(SLOT)).astype(np.float32))
    return t


def kernel(**inputs):
    import numpy as np
    import concourse.bacc as bacc
    from concourse.bass_utils import run_bass_kernel_spmd

    nc = bacc.Bacc("TRN2", target_bir_lowering=False, num_devices=1)
    arrays, tensors = {}, {}
    for name, a in layout(np, {k: np.asarray(v) for k, v in inputs.items()}).items():
        a = np.ascontiguousarray(a)
        arrays[f"in_{name}"] = a
        tensors[name] = nc.dram_tensor(f"in_{name}", a.shape, mybir.dt.from_np(a.dtype), kind="ExternalInput").ap()
    out = nc.dram_tensor("out_x", (B, S, D), F32, kind="ExternalOutput").ap()
    build_program(nc, tensors, out)
    return run_bass_kernel_spmd(nc, [arrays], core_ids=[0]).results[0]["out_x"]
```

```python
from contextlib import ExitStack

import concourse.bass as bass
from concourse import mybir

ALU = mybir.AluOpType
ACT = mybir.ActivationFunctionType
AX = mybir.AxisListType
F32 = mybir.dt.float32
F32R = mybir.dt.float32r
BF16 = mybir.dt.bfloat16
U32 = mybir.dt.uint32

P = 128
B, S, D = 2, 512, 256
TOK = B * S
NT = TOK // P
TB = S // P
DC = D // P
HALF = 512
NHALF = TOK // HALF
LN_EPS = 1e-5
NEG = -1e30

N_EXP, TOP_K, INTER = 8, 2, 176
SHARED0, SHARED1 = 704, 176
GATES = 10
W_SEL, W_GATE, W_UP = 0, P, P + DC * P
W_DOWN = P + 2 * DC * P
FFN_COLS = W_DOWN + D


def f32(ap):
    return ap.bitcast(F32)


def spread(ap, n):
    return ap.unsqueeze(len(ap.shape)).broadcast_to([*ap.shape, n])


def signals(n):
    return n + 1


class Chain:

    def __init__(self, engine, sem):
        self.engine, self.sem, self.n = engine, sem, 0

    def __call__(self, instruction):
        self.n += 1
        instruction.then_inc(self.sem, 1)
        self.engine.wait_ge(self.sem, self.n)


def product(pe, out, stationary, moving, first, last):
    (sh, sl), (mh, ml) = stationary, moving
    pe.matmul(out, sh, mh, start=first, stop=False, skip_group_check=True)
    pe.matmul(out, sh, ml, start=False, stop=False, skip_group_check=True)
    return pe.matmul(out, sl, mh, start=False, stop=last, skip_group_check=True)


class Semaphores:

    def __init__(self, nc, name):
        self.nc, self.name, self.all = nc, name, []

    def __call__(self, what):
        self.all.append(self.nc.alloc_semaphore(f"{self.name}_{what}"))
        return self.all[-1]

    def __enter__(self):
        return self

    def __exit__(self, *_):
        self.nc.clear_and_free_semaphores(self.all)
        self.nc.all_engine_barrier()


class Norm:

    def __init__(self, nc, ctx, sem, name, res, banks, xn=None):
        sb = lambda what, shape: ctx.enter_context(nc.sbuf_tensor(f"{name}_{what}", shape, F32))
        self.res, self.banks = res, banks
        self.stats, self.moments = sb("stats", [P, NT, 6]), sb("moments", [P, NT, 2])
        self.var, self.power, self.rstd = sb("var", [P, NT]), sb("power", [P, NT]), sb("rstd", [P, NT])
        self.xn = sb("xn", [P, NT, D]) if xn is None else xn
        self.stats_done, self.moments_done = sem("ln_stats_done"), sem("ln_moments_done")
        self.pool_step, self.rstd_done = sem("ln_pool_step"), sem("ln_rstd_done")
        self.normed, self.turned = sem("ln_normed"), sem("ln_turned")
        self.hi_done, self.lo_done = sem("ln_xn_hi_done"), sem("ln_xn_lo_done")

    def vector(self, dve):
        x = self.res.x
        for h in range(NHALF):
            for t in range(h * TB, (h + 1) * TB):
                dve.bn_stats(self.stats[:, t, :], x[:, t, :]).then_inc(self.stats_done, 1)
            for t in range(h * TB, (h + 1) * TB):
                dve.wait_ge(self.stats_done, t + 1)
                dve.bn_aggr(self.moments[:, t, :], self.stats[:, t, :]).then_inc(self.moments_done, 1)
        for h in range(NHALF):
            dve.wait_ge(self.rstd_done, h + 1)
            for t in range(h * TB, (h + 1) * TB):
                dve.tensor_scalar(self.xn[:, t, :], x[:, t, :], self.moments[:, t, 0:1], self.rstd[:, t:t + 1],
                                  ALU.subtract, ALU.mult).then_inc(self.normed, 1)
        for k in range(NHALF * DC):
            h, c = divmod(k, DC)
            at = slice(h * HALF, (h + 1) * HALF)
            dve.wait_ge(self.hi_done, k + 1)
            dve.tensor_tensor(self.res.xl[:, c, at], self.banks[k], f32(self.res.xh[:, c, at]),
                              ALU.subtract).then_inc(self.lo_done, 1)

    def gpsimd(self, pool):
        pool.memset(self.power[:], -0.5).then_inc(self.pool_step, 1)
        for h in range(NHALF):
            half = slice(h * TB, (h + 1) * TB)
            pool.wait_ge(self.moments_done, (h + 1) * TB)
            pool.tensor_scalar(self.var[:, half], self.moments[:, half, 1], LN_EPS, None, ALU.add).then_inc(self.pool_step, 1)
            pool.wait_ge(self.pool_step, h + 2)
            pool.tensor_tensor(self.rstd[:, half], self.var[:, half], self.power[:, half],
                               ALU.pow).then_inc(self.rstd_done, 1)

    @staticmethod
    def ready(half):
        return DC * (half + 1)

    def tensor(self, pe):
        for k in range(NHALF * DC):
            h, c = divmod(k, DC)
            pe.wait_ge(self.normed, (h + 1) * TB)
            for j in range(TB):
                last = pe.transpose(self.banks[k][:, j * P:(j + 1) * P],
                                    self.xn[:, h * TB + j, c * P:(c + 1) * P], self.res.ident[:])
            last.then_inc(self.turned, 1)

    def scalar(self, act):
        for k in range(NHALF * DC):
            h, c = divmod(k, DC)
            act.wait_ge(self.turned, k + 1)
            act.activation(self.res.xh[:, c, h * HALF:(h + 1) * HALF], self.banks[k],
                           ACT.Copy).then_inc(self.hi_done, 1)


def ffn_stage(nc, name, res, weights, gate_w, owner_is_gated, renormalise):
    n_chunks = weights.shape[0]
    with ExitStack() as ctx:
        sem = ctx.enter_context(Semaphores(nc, name))
        sb = lambda what, shape, dt=F32: ctx.enter_context(nc.sbuf_tensor(f"{name}_{what}", shape, dt))
        banks = [ctx.enter_context(nc.psum_tensor(f"{name}_bank{i}", [P, HALF], F32)) for i in range(8)]
        acc = banks[:4]
        gate_bank = (banks[4], banks[6])
        up_bank = (banks[5], banks[7])
        norm = Norm(nc, ctx, sem, f"{name}_ln", res, [b[:] for b in banks[4:8]])

        w_raw = sb("w_raw", [P, 2, FFN_COLS])
        w_hi, w_lo = sb("w_hi", [P, 2, FFN_COLS], F32R), sb("w_lo", [P, 2, FFN_COLS], F32R)
        gate_raw = sb("gate_raw", [P, DC, GATES])
        gate_hi, gate_lo = sb("gate_hi", [P, DC, GATES], F32R), sb("gate_lo", [P, DC, GATES], F32R)
        logits, shifted = sb("logits", [P, NT, GATES]), sb("shifted", [P, NT, N_EXP])
        probs, row_max, row_sum = sb("probs", [P, NT, N_EXP]), sb("row_max", [P, NT]), sb("row_sum", [P, NT])
        gate_exp = sb("gate_exp", [P, NT])
        top8, at8 = sb("top8", [P, NT, 8]), sb("at8", [P, NT, 8], U32)
        at_f, iota = sb("at_f", [P, NT, TOP_K]), res.iota
        first_hit, second_hit = sb("first_hit", [P, NT, N_EXP]), sb("second_hit", [P, NT, N_EXP])
        token_w = sb("token_w", [P, NT, 16])
        tw_hi, tw_lo = sb("tw_hi", [16, TOK], F32R), sb("tw_lo", [16, TOK], F32R)
        silu = sb("silu", [P, NHALF, HALF])
        gated = sb("gated", [P, NHALF, HALF])
        h_full = sb("h_full", [P, NHALF, HALF])
        h_hi, h_lo = sb("h_hi", [P, 2, TOK], F32R), sb("h_lo", [P, 2, TOK], F32R)

        w_loaded = [sem("w_loaded0"), sem("w_loaded1")]
        w_hi_done = [sem("w_hi_done0"), sem("w_hi_done1")]
        w_up_split = [sem("w_up_split0"), sem("w_up_split1")]
        w_split = [sem("w_split0"), sem("w_split1")]
        w_used = [sem("w_used0"), sem("w_used1")]
        gate_loaded, gate_split = sem("gate_loaded"), sem("gate_split")
        logits_ready, logits_read, shifted_done = sem("logits_ready"), sem("logits_read"), sem("shifted_done")
        exp_done, step = sem("exp_done"), sem("vector_step")
        token_w_done, tw_turned, tw_hi_done, tw_lo_done = (
            sem("token_w_done"), sem("tw_turned"), sem("tw_hi_done"), sem("tw_lo_done"))
        gate_ready, up_ready, owner_ready = sem("gate_ready"), sem("up_ready"), sem("owner_ready")
        silu_done, gated_done, h_done = sem("silu_done"), sem("gated_done"), sem("h_done")
        h_hi_done, h_lo_done = sem("h_hi_done"), sem("h_lo_done")

        block = ctx.enter_context(nc.Block())

        @block.sync
        def _(sp):
            sp.dma_start(gate_raw[:], gate_w).then_inc(gate_loaded, 16)

            def load(n, parity, k):
                sp.wait_ge(w_split[parity], signals(k))
                src = weights[bass.ds(n, 1), :, :].rearrange("a p n -> (a p) n")
                sp.dma_start(w_raw[:, parity, :], src).then_inc(w_loaded[parity], 16)

            with sp.Fori(0, n_chunks // 2) as i:
                load(2 * i, 0, i)
                load(2 * i + 1, 1, i)
            load(n_chunks - 1, 0, n_chunks // 2)

        @block.gpsimd
        def _(pool):
            for one in (*w_split,):
                pool.sem_inc(one, 1)
            def split(parity, k, columns, done):
                raw = w_raw[:, parity, columns]
                pool.tensor_tensor(w_hi[:, parity, columns], raw, res.zero[:].broadcast_to(raw.shape),
                                   ALU.add).then_inc(w_hi_done[parity], 1)
                pool.wait_ge(w_hi_done[parity], k)
                pool.tensor_tensor(w_lo[:, parity, columns], raw, f32(w_hi[:, parity, columns]),
                                   ALU.subtract).then_inc(done[parity], 1)

            def split_up(n, parity, k, first=False):
                if not first:
                    pool.wait_ge(owner_ready, 2 * n - 2)
                pool.wait_ge(w_loaded[parity], 16 * k + 16)
                split(parity, 2 * k + 1, slice(0, W_DOWN), w_up_split)

            def split_down(parity, k):
                pool.wait_ge(w_used[parity], signals(k))
                split(parity, 2 * k + 2, slice(W_DOWN, FFN_COLS), w_split)

            pool.wait_ge(gate_loaded, 16)
            pool.tensor_copy(gate_hi[:], gate_raw[:]).then_inc(gate_split, 1)
            pool.wait_ge(gate_split, 1)
            pool.tensor_tensor(gate_lo[:], gate_raw[:], f32(gate_hi[:]), ALU.subtract).then_inc(gate_split, 1)
            norm.gpsimd(pool)
            split_up(0, 0, 0, True)
            split_down(0, 0)
            split_up(1, 1, 0, True)
            with pool.Fori(1, n_chunks // 2) as i:
                split_up(2 * i, 0, i)
                split_down(1, i - 1)
                split_up(2 * i + 1, 1, i)
                split_down(0, i)
            split_up(n_chunks - 1, 0, n_chunks // 2)
            split_down(1, n_chunks // 2 - 1)
            split_down(0, n_chunks // 2)

        @block.tensor
        def _(pe):
            for one in (*w_used,):
                pe.sem_inc(one, 1)
            def fill(bank, column, parity, half):
                at = slice(half * HALF, (half + 1) * HALF)
                for c in range(DC):
                    w = slice(column + c * P, column + (c + 1) * P)
                    last = product(pe, bank[:], (w_hi[:, parity, w], w_lo[:, parity, w]),
                                   (res.xh[:, c, at], res.xl[:, c, at]), c == 0, c == DC - 1)
                return last

            def gate_fill(n, parity, half):
                pe.wait_ge(h_done, 2 * n)
                fill(gate_bank[half], W_GATE, parity, half).then_inc(gate_ready, 1)

            def up_fill(n, parity, half):
                pe.wait_ge(gated_done, signals(2 * n))
                fill(up_bank[half], W_UP, parity, half).then_inc(up_ready, 1)

            def owner_fill(n, parity, half):
                at = slice(half * HALF, (half + 1) * HALF)
                sel = w_hi[0:16, parity, W_SEL:W_SEL + P]
                pe.wait_ge(silu_done, 2 * n + half + 1)
                pe.matmul(gate_bank[half][:], sel, tw_hi[:, at], start=True, stop=False, skip_group_check=True)
                pe.matmul(gate_bank[half][:], sel, tw_lo[:, at], start=False, stop=True,
                          skip_group_check=True).then_inc(owner_ready, 1)

            def up(n, parity, k, before_owner=None):
                pe.wait_ge(w_up_split[parity], k + 1)
                gate_fill(n, parity, 0)
                up_fill(n, parity, 0)
                gate_fill(n, parity, 1)
                if before_owner:
                    before_owner()
                owner_fill(n, parity, 0)
                up_fill(n, parity, 1)
                owner_fill(n, parity, 1)

            def down(n, parity, k, last_chunk=False):
                pe.wait_ge(w_split[parity], signals(k + 1))
                pe.wait_ge(h_lo_done, 2 * n + 2)
                w = slice(W_DOWN, W_DOWN + D)
                for t in range(NT):
                    at = slice(t * P, (t + 1) * P)
                    last = product(pe, acc[t // 2][:, t % 2 * D:(t % 2 + 1) * D],
                                   (h_hi[:, parity, at], h_lo[:, parity, at]),
                                   (w_hi[:, parity, w], w_lo[:, parity, w]), False, last_chunk)
                last.then_inc(w_used[parity], 1)
                return last

            def route():
                pe.wait_ge(token_w_done, 1)
                pe.wait_ge(logits_read, 1)
                for half, bank in enumerate((up_bank[1], acc[0])):
                    for j in range(TB):
                        last = pe.transpose(bank[0:16, j * P:(j + 1) * P], token_w[:, half * TB + j, :], res.ident[:])
                    last.then_inc(tw_turned, 1)
                pe.wait_ge(tw_lo_done, 2)
                for bank in acc:
                    pe.matmul(bank[:], res.zeros[:, 0:P], res.zeros[:], start=True, stop=False,
                              skip_group_check=True)

            norm.tensor(pe)
            pe.wait_ge(norm.lo_done, NHALF * DC)
            pe.wait_ge(gate_split, 2)
            for t in range(NT):
                for c in range(DC):
                    at = slice(t * P, (t + 1) * P)
                    last = product(pe, up_bank[1][:, t * 16:t * 16 + GATES],
                                   (res.xh[:, c, at], res.xl[:, c, at]),
                                   (gate_hi[:, c, :], gate_lo[:, c, :]), t == 0 and c == 0, c == DC - 1)
            last.then_inc(logits_ready, 1)
            up(0, 0, 0, route)
            with pe.Fori(0, n_chunks // 2) as i:
                up(2 * i + 1, 1, i)
                down(2 * i, 0, i)
                up(2 * i + 2, 0, i + 1)
                down(2 * i + 1, 1, i)
            down(n_chunks - 1, 0, n_chunks // 2, True)

        @block.scalar
        def _(act):
            for one in (h_hi_done,):
                act.sem_inc(one, 1)
            norm.scalar(act)
            act.wait_ge(shifted_done, 1)
            act.activation(probs[:], shifted[:], ACT.Exp).then_inc(exp_done, 1)
            if owner_is_gated:
                act.activation(gate_exp[:], logits[:, :, N_EXP], ACT.Exp, scale=-1.0).then_inc(exp_done, 1)
            for half, bank in enumerate((up_bank[1], acc[0])):
                act.wait_ge(tw_turned, half + 1)
                act.activation(tw_hi[:, half * HALF:(half + 1) * HALF], bank[0:16, :],
                               ACT.Copy).then_inc(tw_hi_done, 1)

            def chunk(n, parity, k):
                act.wait_ge(gated_done, signals(2 * n))
                for half in range(NHALF):
                    act.wait_ge(gate_ready, 2 * n + half + 1)
                    act.activation(silu[:, half, :], gate_bank[half][:], ACT.Silu).then_inc(silu_done, 1)
                act.wait_ge(w_used[parity], signals(k))
                for half in range(NHALF):
                    act.wait_ge(h_done, 2 * n + half + 1)
                    act.activation(h_hi[:, parity, half * HALF:(half + 1) * HALF], h_full[:, half, :],
                                   ACT.Copy).then_inc(h_hi_done, 1)

            with act.Fori(0, n_chunks // 2) as i:
                chunk(2 * i, 0, i)
                chunk(2 * i + 1, 1, i)
            chunk(n_chunks - 1, 0, n_chunks // 2)

        @block.vector
        def _(dve):
            for one in (gated_done,):
                dve.sem_inc(one, 1)
            then = Chain(dve, step)
            norm.vector(dve)
            dve.wait_ge(logits_ready, 1)
            then(dve.tensor_copy(logits[:], up_bank[1][:, 0:NT * 16].rearrange("p (t g) -> p t g", g=16)[:, :, 0:GATES]))
            then(dve.tensor_reduce(row_max[:], logits[:, :, 0:N_EXP], AX.X, ALU.max))
            dve.tensor_tensor(shifted[:], logits[:, :, 0:N_EXP], spread(row_max[:], N_EXP),
                              ALU.subtract).then_inc(shifted_done, 1)
            dve.memset(token_w[:], 1.0).then_inc(logits_read, 1)
            dve.wait_ge(exp_done, 2 if owner_is_gated else 1)
            then(dve.tensor_reduce(row_sum[:], probs[:], AX.X, ALU.add))
            then(dve.reciprocal(row_sum[:], row_sum[:]))
            then(dve.tensor_tensor(probs[:], probs[:], spread(row_sum[:], N_EXP), ALU.mult))
            for t in range(NT):
                last = dve.max(top8[:, t, :], probs[:, t, :])
            then(last)
            for t in range(NT):
                last = dve.max_index(at8[:, t, :], top8[:, t, :], probs[:, t, :])
            then(last)
            then(dve.tensor_copy(at_f[:], at8[:, :, 0:TOP_K]))
            dve.tensor_tensor(first_hit[:], iota[:], spread(at_f[:, :, 0], N_EXP), ALU.is_equal)
            then(dve.tensor_tensor(second_hit[:], iota[:], spread(at_f[:, :, 1], N_EXP), ALU.is_equal))
            then(dve.tensor_tensor(first_hit[:], first_hit[:], second_hit[:], ALU.add))
            if renormalise:
                then(dve.tensor_tensor(row_sum[:], top8[:, :, 0], top8[:, :, 1], ALU.add))
                then(dve.tensor_scalar(row_sum[:], row_sum[:], 1e-20, None, ALU.add))
                then(dve.reciprocal(row_sum[:], row_sum[:]))
                then(dve.tensor_tensor(probs[:], probs[:], spread(row_sum[:], N_EXP), ALU.mult))
            if owner_is_gated:
                then(dve.tensor_scalar(gate_exp[:], gate_exp[:], 1.0, None, ALU.add))
                then(dve.reciprocal(token_w[:, :, N_EXP], gate_exp[:]))
            dve.tensor_tensor(token_w[:, :, 0:N_EXP], probs[:], first_hit[:], ALU.mult).then_inc(token_w_done, 1)
            for half, bank in enumerate((up_bank[1], acc[0])):
                at = slice(half * HALF, (half + 1) * HALF)
                dve.wait_ge(tw_hi_done, half + 1)
                dve.tensor_tensor(tw_lo[:, at], bank[0:16, :], f32(tw_hi[:, at]), ALU.subtract).then_inc(tw_lo_done, 1)

            def chunk(n, parity):
                for half in range(NHALF):
                    dve.wait_ge(silu_done, 2 * n + half + 1)
                    dve.wait_ge(up_ready, 2 * n + half + 1)
                    dve.tensor_tensor(gated[:, half, :], up_bank[half][:], silu[:, half, :],
                                      ALU.mult).then_inc(gated_done, 1)
                dve.wait_ge(h_hi_done, signals(2 * n))
                for half in range(NHALF):
                    dve.wait_ge(owner_ready, 2 * n + half + 1)
                    dve.wait_ge(gated_done, signals(2 * n + half + 1))
                    dve.tensor_tensor(h_full[:, half, :], gate_bank[half][:], gated[:, half, :],
                                      ALU.mult).then_inc(h_done, 1)
                for half in range(NHALF):
                    at = slice(half * HALF, (half + 1) * HALF)
                    dve.wait_ge(h_hi_done, signals(2 * n + half + 1))
                    dve.tensor_tensor(h_lo[:, parity, at], h_full[:, half, :], f32(h_hi[:, parity, at]),
                                      ALU.subtract).then_inc(h_lo_done, 1)

            with dve.Fori(0, n_chunks // 2) as i:
                chunk(2 * i, 0)
                chunk(2 * i + 1, 1)
            chunk(n_chunks - 1, 0)
            dve.wait_ge(w_used[0], signals(n_chunks // 2 + 1))
            for b in range(NT // 2):
                two = res.x[:, 2 * b:2 * b + 2, :]
                dve.tensor_tensor(two, acc[b][:].rearrange("p (t d) -> p t d", d=D), two, ALU.add)


HEADS, DH = 16, 128
GROUP = 4
GROUPS = HEADS // GROUP
WIDE = GROUP * DH
UNIT_OF_ROW = (0, 0, 1, 2)
UNIT_ROWS = ((0, 1), (2,), (3,))
ROW_AT = (0, P, 0, 0)


def wide_stage(nc, name, res, t):
    scale = 1.0 / DH ** 0.5
    with ExitStack() as ctx:
        sem = ctx.enter_context(Semaphores(nc, name))
        sb = lambda what, shape, dt=F32: ctx.enter_context(nc.sbuf_tensor(f"{name}_{what}", shape, dt))
        banks = [ctx.enter_context(nc.psum_tensor(f"{name}_bank{i}", [P, HALF], F32)) for i in range(8)]
        acc, s_bank, t_bank, o_bank, fill_bank = banks[:2], banks[2:4], banks[4:6], banks[6], banks[7]
        ring = (*s_bank, *t_bank)
        norm = Norm(nc, ctx, sem, f"{name}_ln", res, [b[:] for b in ring])

        scratch = sb("scratch", [P, 2 * TB, HALF])
        wq_raw = scratch[:].rearrange("p (c a) n -> p c (a n)", c=DC)
        probs = scratch[:].rearrange("p (u r) n -> p u r n", u=2)
        probs_t = sb("probs_t", [P, TB, HALF])
        wq_hi, wq_lo = sb("wq_hi", [P, DC, HEADS * DH], F32R), sb("wq_lo", [P, DC, HEADS * DH], F32R)
        w_raw = sb("w_raw", [P, 3, DC * WIDE])
        w_hi, w_lo = sb("w_hi", [P, 3, DC * WIDE], F32R), sb("w_lo", [P, 3, DC * WIDE], F32R)
        bq, bk, bv = sb("bq", [P, HEADS]), sb("bk", [P, GROUP]), sb("bv", [P, WIDE])
        bo = sb("bo", [P, D])
        q_next = sb("q_next", [P, GROUP * S])
        q, k, v = sb("q", [P, B, GROUP * S]), sb("k", [P, B, GROUP, S]), sb("v", [P, B, TB, WIDE])
        neg_max, row_sum = sb("neg_max", [P, 4 * GROUP]), sb("row_sum", [P, 4 * GROUP])
        o_hi, o_lo = sb("o_hi", [P, S], F32R), sb("o_lo", [P, S], F32R)

        wq_loaded, wq_hi_done, wq_split = sem("wq_loaded"), sem("wq_hi_done"), sem("wq_split")
        w_loaded = [sem(f"w_loaded{p}") for p in "kvo"]
        w_hi_done = sem("w_hi_done")
        w_split = [sem(f"w_split{p}") for p in "kvo"]
        bias_loaded, bk_loaded, bv_loaded, bq_scaled = sem("bias_loaded"), sem("bk_loaded"), sem("bv_loaded"), sem("bq_scaled")
        k_ready, v_ready, q_ready = sem("k_ready"), sem("v_ready"), sem("q_ready")
        k_done, v_done, q_done = sem("k_done"), sem("v_done"), sem("q_done")
        scores_ready, max_done, exp_done, inverse_done, probs_done = (
            sem("scores_ready"), sem("max_done"), sem("exp_done"), sem("inverse_done"), sem("probs_done"))
        turned, probs_t_done = sem("turned"), sem("probs_t_done")
        o_ready, o_hi_done, o_lo_done, out_done = sem("o_ready"), sem("o_hi_done"), sem("o_lo_done"), sem("out_done")
        k_hi_done, q_moved = sem("k_hi_done"), sem("q_moved")
        bo_added, acc_read = sem("bo_added"), sem("acc_read")
        group_w = (t["wb_k"], t["wb_v"], t["wb_o"])
        Q_FILLS = 8
        K_FILLS, V_FILLS = [("k", f) for f in range(4)], [("v", f) for f in range(4)]
        Q_ALL = [("q", f) for f in range(Q_FILLS)]
        FILLS_OF = (Q_ALL + K_FILLS + V_FILLS, K_FILLS + V_FILLS)
        FIRST_FILLS = K_FILLS + Q_ALL + V_FILLS

        def score_bank(h, r):
            return s_bank[(3 * h + UNIT_OF_ROW[r]) % 2][:, ROW_AT[r]:ROW_AT[r] + (r + 1) * P]

        def turned_bank(h, u):
            return t_bank[(3 * h + u) % 2]

        def units(engine, unit):
            with engine.Fori(0, GROUPS - 1) as i:
                for b in range(B):
                    unit(i, b, True)
            for b in range(B):
                unit(GROUPS - 1, b, b == 0)

        def fills_of_step(i, b, h, more):
            if not more:
                return [[]] * 4
            fills = FILLS_OF[1 - b]
            n = len(fills) // GROUP
            mine = [(i + b, 1 - b, kind, f) for kind, f in fills[n * h:n * (h + 1)]]
            return [[one] for one in mine] if n == 4 else [[], [mine[0]], [mine[1]], []]

        block = ctx.enter_context(nc.Block())

        @block.sync
        def _(sp):
            def load(i):
                sp.wait_ge(k_done, B * GROUP * i)
                sp.dma_start(bk[:], t["bb_k"][bass.ds(i, 1), :, :].rearrange("a p n -> (a p) n")).then_inc(bk_loaded, 16)
                sp.wait_ge(w_split[0], i)
                sp.dma_start(w_raw[:, 0, :], group_w[0][bass.ds(i, 1), :, :].rearrange("a p n -> (a p) n")).then_inc(w_loaded[0], 16)
                sp.wait_ge(v_done, B * TB * i)
                sp.dma_start(bv[:], t["bb_v"][bass.ds(i, 1), :].rearrange("a n -> (a n)").partition_broadcast(P)).then_inc(bv_loaded, 16)
                for p in (1, 2):
                    sp.wait_ge(w_split[p], i)
                    sp.dma_start(w_raw[:, p, :], group_w[p][bass.ds(i, 1), :, :].rearrange("a p n -> (a p) n")).then_inc(w_loaded[p], 16)

            load(0)
            for c in range(DC):
                sp.dma_start(wq_raw[:, c, :], t["wb_q"][:, c, :]).then_inc(wq_loaded, 16)
            sp.dma_start(bq[:], t["bb_q"]).then_inc(bias_loaded, 16)
            sp.dma_start(bo[:], t["bb_o"].partition_broadcast(P)).then_inc(bias_loaded, 16)
            with sp.Fori(1, GROUPS) as i:
                load(i)

        @block.gpsimd
        def _(pool):
            norm.gpsimd(pool)

            def split(i, some):
                for p in some:
                    used = (k_ready, v_ready, out_done)[p]
                    pool.wait_ge(used, B * GROUP * i)
                    pool.wait_ge(w_loaded[p], 16 * i + 16)
                    pool.tensor_tensor(w_hi[:, p, :], w_raw[:, p, :], res.zero[:].broadcast_to([P, DC * WIDE]),
                                       ALU.add).then_inc(w_hi_done, 1)
                    pool.wait_ge(w_hi_done, 3 * i + p)
                    pool.tensor_tensor(w_lo[:, p, :], w_raw[:, p, :], f32(w_hi[:, p, :]),
                                       ALU.subtract).then_inc(w_split[p], 1)

            def move_q(i):
                pool.wait_ge(scores_ready, 3 * B * GROUP * i)
                pool.wait_ge(q_done, Q_FILLS * (i + 1))
                pool.tensor_tensor(q[:, 1, :], q_next[:], res.zero[:].broadcast_to([P, GROUP * S]),
                                   ALU.add).then_inc(q_moved, 1)

            split(0, (1, 2))
            move_q(0)
            pool.wait_ge(norm.normed, NT)
            pool.wait_ge(bias_loaded, 32)
            pool.tensor_tensor(res.x[:], res.x[:], bo[:].unsqueeze(1).broadcast_to([P, NT, D]), ALU.add).then_inc(bo_added, 1)
            with pool.Fori(1, GROUPS) as i:
                split(i, (0, 1, 2))
                move_q(i)

        @block.tensor
        def _(pe):
            norm.tensor(pe)
            pe.wait_ge(norm.lo_done, norm.ready(0))

            def weights(p, c, at, n):
                w = slice(c * WIDE + at, c * WIDE + at + n)
                return w_hi[:, p, w], w_lo[:, p, w]

            def fill(i, b, kind, f, bank):
                both = lambda c, at: (res.xh[:, c, at], res.xl[:, c, at])
                if kind == "k":
                    if f == 0:
                        pe.wait_ge(w_split[0], i + 1)
                    for c in range(DC):
                        last = product(pe, bank[:], weights(0, c, f * DH, DH), both(c, slice(b * S, (b + 1) * S)),
                                       c == 0, c == DC - 1)
                    last.then_inc(k_ready, 1)
                if kind == "q":
                    for j in range(2):
                        sub = slice((2 * f + j) * DH, (2 * f + j + 1) * DH)
                        for c in range(DC):
                            both_batches = tuple(x[:, c, :].rearrange("p (b n) -> p b n", b=B)[:, :, bass.ds(i * P, P)]
                                                 for x in (res.xh, res.xl))
                            last = product(pe, bank[:, j * B * P:(j + 1) * B * P], (wq_hi[:, c, sub], wq_lo[:, c, sub]),
                                           both_batches, j == 0 and c == 0, c == DC - 1)
                    last.then_inc(q_ready, 1)
                if kind == "v":
                    if f == 0:
                        pe.wait_ge(w_split[1], i + 1)
                    for c in range(DC):
                        last = product(pe, bank[:], both(c, slice(b * S + f * P, b * S + (f + 1) * P)),
                                       weights(1, c, 0, WIDE), c == 0, c == DC - 1)
                    last.then_inc(v_ready, 1)

            def next_fills(fills):
                for i, b, kind, f in fills:
                    U = B * i + b
                    if f:
                        read, n = {"k": (k_done, 4 * U + f), "q": (q_done, Q_FILLS * i + f), "v": (v_done, 4 * U + f)}[kind]
                    elif kind == "v":
                        read, n = k_done, 4 * U + 4
                    elif kind == "k" and b == 0:
                        read, n = q_done, Q_FILLS * (i + 1)
                    else:
                        read, n = v_done, 4 * U
                    pe.wait_ge(read, n)
                    fill(i, b, kind, f, fill_bank)

            def scores(b, h, n, u):
                if u == 2:
                    pe.wait_ge(exp_done, 4 * n + 2)
                for r in UNIT_ROWS[u]:
                    to = score_bank(h, r)
                    pe.matmul(to, q[:, b, h * S + r * P:h * S + (r + 1) * P], k[:, b, h, 0:(r + 1) * P],
                              start=r == UNIT_ROWS[u][0], stop=False, skip_group_check=True)
                    last = pe.matmul(to[:, r * P:(r + 1) * P], res.ident_bf[:], res.causal[:],
                                     start=False, stop=True, skip_group_check=True)
                last.then_inc(scores_ready, 1)

            def turn(h, n, u):
                if u == 2:
                    pe.wait_ge(probs_t_done, 3 * n + 1)
                for r in UNIT_ROWS[u]:
                    pe.wait_ge(probs_done, 4 * n + r + 1)
                    for j in range(r + 1):
                        at = ROW_AT[r] + j * P
                        last = pe.transpose(turned_bank(h, u)[:, at:at + P], probs[:, h % 2, r, j * P:(j + 1) * P], res.ident[:])
                last.then_inc(turned, 1)

            def attend(b, h, n):
                pe.wait_ge(probs_t_done, 3 * n + 3)
                for j in range(TB):
                    last = pe.matmul(o_bank[:, j * P:S], v[:, b, j, h * DH:(h + 1) * DH], probs_t[:, j, j * P:S],
                                     start=j == 0, stop=j == TB - 1, skip_group_check=True)
                last.then_inc(o_ready, 1)

            def project_out(h, n):
                pe.wait_ge(o_lo_done, n + 1)
                for j in range(TB):
                    at = slice(j * P, (j + 1) * P)
                    last = product(pe, acc[j // 2][:, j % 2 * D:(j % 2 + 1) * D], (o_hi[:, at], o_lo[:, at]),
                                   (w_hi[:, 2, h * D:(h + 1) * D], w_lo[:, 2, h * D:(h + 1) * D]), h == 0 and j % 2 == 0,
                                   h == GROUP - 1)
                last.then_inc(out_done, 1)

            def unit(i, b, more):
                U = B * i + b
                for h in range(GROUP):
                    n = GROUP * U + h
                    head_after = (b, h + 1, n + 1) if h + 1 < GROUP else (1 - b, 0, n + 1)
                    follows = more or h + 1 < GROUP
                    fills = fills_of_step(i, b, h, more)
                    turn(h, n, 0)
                    turn(h, n, 1)
                    if h + 1 == GROUP and more and b == 0:
                        pe.wait_ge(q_moved, i + 1)
                    if follows:
                        pe.wait_ge(exp_done, 4 * n + 3)
                        scores(*head_after, 0)
                    turn(h, n, 2)
                    if follows:
                        pe.wait_ge(exp_done, 4 * n + 4)
                        scores(*head_after, 1)
                    next_fills(fills[0])
                    if h == 0:
                        pe.wait_ge(v_done, TB * U + TB)
                    attend(b, h, n)
                    next_fills(fills[1])
                    if follows:
                        scores(*head_after, 2)
                    next_fills(fills[2])
                    if h == 0:
                        pe.wait_ge(acc_read, signals(2 * U))
                        pe.wait_ge(w_split[2], i + 1)
                    project_out(h, n)
                    next_fills(fills[3])

            evacuated = {"k": k_done, "q": q_done, "v": v_done}
            for g, (kind, f) in enumerate(FIRST_FILLS):
                if g == 2:
                    pe.wait_ge(norm.lo_done, norm.ready(1))
                if g == 4:
                    pe.wait_ge(wq_split, 1)
                if g >= 4:
                    pe.wait_ge(evacuated[FIRST_FILLS[g - 4][0]], FIRST_FILLS[g - 4][1] + 1)
                fill(0, 0, kind, f, ring[g % 4])
            pe.wait_ge(v_done, TB)
            for u in range(3):
                scores(0, 0, 0, u)
            units(pe, unit)

        @block.scalar
        def _(act):
            norm.scalar(act)
            act.wait_ge(w_loaded[0], 16)
            act.activation(w_hi[:, 0, :], w_raw[:, 0, :], ACT.Copy).then_inc(k_hi_done, 1)
            act.wait_ge(wq_loaded, 16 * DC)
            act.activation(wq_hi[:], wq_raw, ACT.Copy).then_inc(wq_hi_done, 1)

            def k_evacuated(U, b, f, bank):
                act.wait_ge(k_ready, GROUP * U + f + 1)
                act.activation(k[:, b, f, :], bank[:], ACT.Identity, bias=bk[:, f:f + 1]).then_inc(k_done, 1)

            def exponentials(h, n, u):
                for r in UNIT_ROWS[u]:
                    act.wait_ge(max_done, 4 * n + max(r, 1) + 1)
                    act.activation(probs[:, h % 2, r, 0:(r + 1) * P], score_bank(h, r), ACT.Exp,
                                   bias=neg_max[:, 4 * h + r:4 * h + r + 1],
                                   accum_out=row_sum[:, 4 * h + r:4 * h + r + 1]).then_inc(exp_done, 1)

            def turned_back(h, n, u):
                act.wait_ge(turned, 3 * n + u + 1)
                for r in UNIT_ROWS[u]:
                    from_ = turned_bank(h, u)[:, ROW_AT[r]:ROW_AT[r] + (r + 1) * P].rearrange("p (j q) -> p j q", q=P)
                    last = act.activation(probs_t[:, 0:r + 1, r * P:(r + 1) * P], from_, ACT.Copy)
                last.then_inc(probs_t_done, 1)

            def unit(i, b, more):
                U = B * i + b
                for h in range(GROUP):
                    n = GROUP * U + h
                    after, follows = ((h + 1) % GROUP, n + 1), more or h + 1 < GROUP
                    fills = fills_of_step(i, b, h, more)

                    def next_fills(fills):
                        for i1, b1, kind, f in fills:
                            if kind == "k":
                                if f == 0:
                                    act.wait_ge(bk_loaded, 16 * i1 + 16)
                                k_evacuated(B * i1 + b1, b1, f, fill_bank)

                    turned_back(h, n, 0)
                    turned_back(h, n, 1)
                    if follows:
                        exponentials(*after, 0)
                    turned_back(h, n, 2)
                    if follows:
                        exponentials(*after, 1)
                    next_fills(fills[0])
                    act.wait_ge(o_ready, n + 1)
                    act.activation(o_hi[:], o_bank[:], ACT.Copy).then_inc(o_hi_done, 1)
                    next_fills(fills[1])
                    if follows:
                        exponentials(*after, 2)
                    next_fills(fills[2] + fills[3])

            act.wait_ge(bk_loaded, 16)
            for f in range(GROUP):
                k_evacuated(0, 0, f, ring[f])
            act.wait_ge(wq_split, 1)
            for u in range(3):
                exponentials(0, 0, u)
            units(act, unit)

        @block.vector
        def _(dve):
            for one in (acc_read,):
                dve.sem_inc(one, 1)
            norm.vector(dve)
            dve.wait_ge(k_hi_done, 1)
            dve.tensor_tensor(w_lo[:, 0, :], w_raw[:, 0, :], f32(w_hi[:, 0, :]), ALU.subtract).then_inc(w_split[0], 1)
            dve.wait_ge(wq_hi_done, 1)
            dve.tensor_tensor(wq_lo[:], wq_raw, f32(wq_hi[:]), ALU.subtract).then_inc(wq_split, 1)
            dve.wait_ge(bias_loaded, 32)
            dve.tensor_scalar(bq[:], bq[:], scale, None, ALU.mult).then_inc(bq_scaled, 1)
            dve.wait_ge(bq_scaled, 1)

            def evacuated(i, b, kind, f, bank):
                if kind == "q":
                    dve.wait_ge(q_ready, Q_FILLS * i + f + 1)
                    subs = slice(2 * f, 2 * f + 2)
                    for b1, to in ((0, q[:, 0, :]), (1, q_next[:])):
                        last = dve.scalar_tensor_tensor(
                            to.rearrange("p (t s) -> p s t", s=HEADS)[:, subs, :],
                            bank[:].rearrange("p (s b t) -> p s b t", s=2, b=B)[:, :, b1, :], scale,
                            spread(bq[:, subs], P), ALU.mult, ALU.add)
                    last.then_inc(q_done, 1)
                if kind == "v":
                    if f == 0:
                        dve.wait_ge(bv_loaded, 16 * i + 16)
                    dve.wait_ge(v_ready, TB * (B * i + b) + f + 1)
                    dve.tensor_tensor(v[:, b, f, :], bank[:], bv[:], ALU.add).then_inc(v_done, 1)

            def row_max(h, n, u):
                dve.wait_ge(scores_ready, 3 * n + u + 1)
                for r in UNIT_ROWS[u]:
                    dve.tensor_reduce(neg_max[:, 4 * h + r:4 * h + r + 1], score_bank(h, r), AX.X, ALU.max,
                                      negate=True).then_inc(max_done, 1)

            def normalise(h, n, u):
                for r in UNIT_ROWS[u]:
                    one = row_sum[:, 4 * h + r:4 * h + r + 1]
                    dve.wait_ge(exp_done, 4 * n + r + 1)
                    dve.reciprocal(one, one).then_inc(inverse_done, 1)
                    dve.wait_ge(inverse_done, 4 * n + r + 1)
                    mine = probs[:, h % 2, r, 0:(r + 1) * P]
                    dve.tensor_scalar(mine, mine, one, None, ALU.mult).then_inc(probs_done, 1)

            def add_to_stream(U, b):
                dve.wait_ge(out_done, GROUP * (U + 1))
                for a in range(2):
                    two = res.x[:, b * TB + 2 * a:b * TB + 2 * a + 2, :]
                    dve.tensor_tensor(two, acc[a][:].rearrange("p (t d) -> p t d", d=D), two, ALU.add).then_inc(acc_read, 1)

            def unit(i, b, more):
                U = B * i + b
                for h in range(GROUP):
                    n = GROUP * U + h
                    after, follows = ((h + 1) % GROUP, n + 1), more or h + 1 < GROUP
                    fills = fills_of_step(i, b, h, more)

                    def next_fills(fills):
                        for one in fills:
                            evacuated(*one, fill_bank)

                    if follows:
                        row_max(*after, 0)
                        row_max(*after, 1)
                        normalise(*after, 0)
                        normalise(*after, 1)
                    next_fills(fills[0])
                    dve.wait_ge(o_hi_done, n + 1)
                    dve.tensor_tensor(o_lo[:], o_bank[:], f32(o_hi[:]), ALU.subtract).then_inc(o_lo_done, 1)
                    next_fills(fills[1])
                    if follows:
                        row_max(*after, 2)
                        normalise(*after, 2)
                    next_fills(fills[2] + fills[3])
                add_to_stream(U, b)

            for g, (kind, f) in enumerate(FIRST_FILLS):
                evacuated(0, 0, kind, f, ring[g % 4])
            for u in range(3):
                row_max(0, 0, u)
            for u in range(3):
                normalise(0, 0, u)
            dve.wait_ge(bo_added, 1)
            units(dve, unit)


Q_HEADS, KV_HEADS, HD = 16, 4, 16
PER_KV = Q_HEADS // KV_HEADS
SLOT = P // KV_HEADS
GQ_COLS = DC * P + D
GK_COLS = 2 * DC * P
WHOLE = 2 * P


def causal_gqa_stage(nc, name, res, t):
    with ExitStack() as ctx:
        sem = ctx.enter_context(Semaphores(nc, name))
        sb = lambda what, shape, dt=F32: ctx.enter_context(nc.sbuf_tensor(f"{name}_{what}", shape, dt))
        banks = [ctx.enter_context(nc.psum_tensor(f"{name}_bank{i}", [P, HALF], F32)) for i in range(8)]
        acc, s_bank, t_bank, o_bank = banks[:2], banks[2:5], banks[5:7], banks[7]
        norm = Norm(nc, ctx, sem, f"{name}_ln", res, [b[:] for b in banks[2:6]])

        kv_raw = sb("kv_raw", [P, GK_COLS])
        kv_hi, kv_lo = sb("kv_hi", [P, GK_COLS], F32R), sb("kv_lo", [P, GK_COLS], F32R)
        w_raw = sb("w_raw", [P, GQ_COLS])
        w_hi, w_lo = sb("w_hi", [P, GQ_COLS], F32R), sb("w_lo", [P, GQ_COLS], F32R)
        turn_q, turn_k = sb("turn_q", [P, S]), sb("turn_k", [P, S])
        bq, bk, bv, bo = sb("bq", [P, PER_KV]), sb("bk", [P, 1]), sb("bv", [P, P]), sb("bo", [P, D])
        k = sb("k", [P, TOK])
        k_hi, k_lo = sb("k_hi", [P, KV_HEADS, TOK], F32R), sb("k_lo", [P, KV_HEADS, TOK], F32R)
        v = sb("v", [P, NT, P])
        q, q_hi, q_lo = sb("q", [P, S]), sb("q_hi", [P, B, S], F32R), sb("q_lo", [P, B, S], F32R)
        probs = sb("probs", [P, 2, TB, S])
        probs_t = sb("probs_t", [P, KV_HEADS, TB, S])
        neg_max, row_sum = sb("neg_max", [P, 4 * KV_HEADS]), sb("row_sum", [P, 4 * KV_HEADS])
        o_hi, o_lo = sb("o_hi", [P, S], F32R), sb("o_lo", [P, S], F32R)

        loaded, kv_hi_done, kv_split = sem("loaded"), sem("kv_hi_done"), sem("kv_split")
        w_loaded, w_hi_done, wq_split, wo_split = sem("w_loaded"), sem("w_hi_done"), sem("wq_split"), sem("wo_split")
        k_ready, k_done, k_cleared, k_hi_done, k_lo_done = (
            sem("k_ready"), sem("k_done"), sem("k_cleared"), sem("k_hi_done"), sem("k_lo_done"))
        v_ready, v_done = sem("v_ready"), sem("v_done")
        q_ready, q_done, q_hi_done, q_lo_done = sem("q_ready"), sem("q_done"), sem("q_hi_done"), sem("q_lo_done")
        scores_ready, max_done, exp_done, inverse_done, probs_done = (
            sem("scores_ready"), sem("max_done"), sem("exp_done"), sem("inverse_done"), sem("probs_done"))
        turned, probs_t_done = sem("turned"), sem("probs_t_done")
        o_ready, o_hi_done, o_lo_done, out_done, acc_read = (
            sem("o_ready"), sem("o_hi_done"), sem("o_lo_done"), sem("out_done"), sem("acc_read"))
        bo_added = sem("bo_added")

        def units(engine, unit):
            with engine.Fori(0, PER_KV - 1) as c:
                for b in range(B):
                    unit(c, b, True)
            for b in range(B):
                unit(PER_KV - 1, b, b == 0)

        def next_heads(b, g, more):
            return [(b, g + 1)] if g + 1 < KV_HEADS else [(1 - b, 0)] if more else []

        block = ctx.enter_context(nc.Block())

        @block.sync
        def _(sp):
            sp.dma_start(kv_raw[:], t["wc_kv"]).then_inc(loaded, 16)
            for to, src in ((bq, "bc_q"), (bk, "bc_k"), (turn_q, "turn_q"), (turn_k, "turn_k")):
                sp.dma_start(to[:], t[src]).then_inc(loaded, 16)
            for to, src in ((bv, "bc_v"), (bo, "bc_o")):
                sp.dma_start(to[:], t[src].partition_broadcast(P)).then_inc(loaded, 16)
            with sp.Fori(0, PER_KV) as c:
                sp.wait_ge(wo_split, signals(c))
                sp.dma_start(w_raw[:], t["wc_q"][bass.ds(c, 1), :, :].rearrange("a p n -> (a p) n")).then_inc(w_loaded, 16)

        @block.gpsimd
        def _(pool):
            for one in (wo_split,):
                pool.sem_inc(one, 1)
            norm.gpsimd(pool)

            def split(raw, hi, lo, hi_done, value, done):
                pool.tensor_tensor(hi, raw, res.zero[:].broadcast_to(raw.shape), ALU.add).then_inc(hi_done, 1)
                pool.wait_ge(hi_done, value)
                pool.tensor_tensor(lo, raw, f32(hi), ALU.subtract).then_inc(done, 1)

            pool.wait_ge(loaded, 16 * 7)
            split(kv_raw[:], kv_hi[:], kv_lo[:], kv_hi_done, 1, kv_split)
            wq, wo = slice(0, DC * P), slice(DC * P, GQ_COLS)
            def split_q(c):
                pool.wait_ge(q_ready, B * c)
                pool.wait_ge(w_loaded, 16 * c + 16)
                split(w_raw[:, wq], w_hi[:, wq], w_lo[:, wq], w_hi_done, 2 * c + 1, wq_split)

            def split_o(c):
                pool.wait_ge(out_done, signals(B * c))
                split(w_raw[:, wo], w_hi[:, wo], w_lo[:, wo], w_hi_done, 2 * c + 2, wo_split)

            split_q(0)
            pool.memset(f32(k_hi[:]), 0.0).then_inc(k_cleared, 1)
            pool.memset(f32(k_lo[:]), 0.0).then_inc(k_cleared, 1)
            split_o(0)
            pool.wait_ge(norm.normed, NT)
            pool.tensor_tensor(res.x[:], res.x[:], bo[:].unsqueeze(1).broadcast_to([P, NT, D]), ALU.add).then_inc(bo_added, 1)
            with pool.Fori(1, PER_KV) as c:
                split_q(c)
                split_o(c)

        @block.tensor
        def _(pe):
            for one in (o_ready, out_done,):
                pe.sem_inc(one, 1)
            norm.tensor(pe)
            pe.wait_ge(norm.lo_done, NHALF * DC)
            pe.wait_ge(kv_split, 1)
            pair = lambda hi, lo, *at: (hi[(slice(None), *at)], lo[(slice(None), *at)])
            for b in range(B):
                for c in range(DC):
                    last = product(pe, banks[2 + b][:], pair(kv_hi, kv_lo, slice((2 * c + 1) * P, (2 * c + 2) * P)),
                                   pair(res.xh, res.xl, c, slice(b * S, (b + 1) * S)), c == 0, c == DC - 1)
                last.then_inc(k_ready, 1)
            for h in range(NT // 2):
                for j in range(2):
                    for c in range(DC):
                        at = slice((2 * h + j) * P, (2 * h + j + 1) * P)
                        last = product(pe, banks[4 + h][:, j * WHOLE:(j + 1) * WHOLE], pair(res.xh, res.xl, c, at),
                                       pair(kv_hi, kv_lo, slice(c * WHOLE, (c + 1) * WHOLE)),
                                       j == 0 and c == 0, c == DC - 1)
                last.then_inc(v_ready, 1)

            def project_q(c, b):
                U = B * c + b
                pe.wait_ge(wq_split, c + 1)
                for k in range(DC):
                    last = product(pe, o_bank[:], pair(w_hi, w_lo, slice(k * P, (k + 1) * P)),
                                   pair(res.xh, res.xl, k, slice(b * S, (b + 1) * S)), k == 0, k == DC - 1)
                last.then_inc(q_ready, 1)

            def scores(b, g, n, u):
                for r in UNIT_ROWS[u]:
                    to = s_bank[u][:, ROW_AT[r]:ROW_AT[r] + (r + 1) * P]
                    product(pe, to, pair(q_hi, q_lo, b, slice(r * P, (r + 1) * P)),
                            pair(k_hi, k_lo, g, slice(b * S, b * S + (r + 1) * P)), r == UNIT_ROWS[u][0], False)
                    last = pe.matmul(to[:, r * P:(r + 1) * P], res.ident_bf[:], res.causal[:],
                                     start=False, stop=True, skip_group_check=True)
                last.then_inc(scores_ready, 1)

            def turn(g, n, u):
                if g or u == 2:
                    pe.wait_ge(probs_t_done, 3 * n + u - 1)
                for r in UNIT_ROWS[u]:
                    pe.wait_ge(probs_done, 4 * n + r + 1)
                    for j in range(r + 1):
                        at = ROW_AT[r] + j * P
                        last = pe.transpose(t_bank[(3 * g + u) % 2][:, at:at + P], probs[:, g % 2, r, j * P:(j + 1) * P],
                                            res.ident[:])
                last.then_inc(turned, 1)

            def attend(b, U):
                pe.wait_ge(probs_t_done, 12 * U + 12)
                for j in range(TB):
                    for g in range(KV_HEADS):
                        slot = slice(g * SLOT, (g + 1) * SLOT)
                        last = pe.matmul(o_bank[slot, j * P:S], v[:, b * TB + j, slot], probs_t[:, g, j, j * P:S],
                                         start=j == 0, stop=j == TB - 1, skip_group_check=True)
                last.then_inc(o_ready, 1)

            def project_out(c, U):
                pe.wait_ge(o_lo_done, signals(U + 1))
                pe.wait_ge(acc_read, signals(2 * U))
                pe.wait_ge(wo_split, signals(c + 1))
                for j in range(TB):
                    last = product(pe, acc[j // 2][:, j % 2 * D:(j % 2 + 1) * D], pair(o_hi, o_lo, slice(j * P, (j + 1) * P)),
                                   pair(w_hi, w_lo, slice(DC * P, GQ_COLS)), j % 2 == 0, True)
                last.then_inc(out_done, 1)

            def unit(c, b, more):
                U = B * c + b
                for g in range(KV_HEADS):
                    n = KV_HEADS * U + g
                    if g == 3 and more:
                        pe.wait_ge(q_lo_done, U + 2)
                    for u, read in enumerate((2, 3, 4)):
                        turn(g, n, u)
                        for b1, g1 in next_heads(b, g, more):
                            pe.wait_ge(exp_done, 4 * n + read)
                            scores(b1, g1, n + 1, u)
                    if g == 0 and b == 1:
                        project_out(c, U - 1)
                    if g == 1 and more:
                        if b == 0:
                            pe.wait_ge(o_lo_done, signals(U))
                        project_q(c + b, 1 - b)
                attend(b, U)
                if b == 1 or not more:
                    project_out(c, U)

            pe.wait_ge(k_done, B)
            pe.wait_ge(v_done, NT // 2)
            project_q(0, 0)
            pe.wait_ge(k_hi_done, B * KV_HEADS)
            pe.wait_ge(k_lo_done, B * KV_HEADS)
            pe.wait_ge(q_lo_done, 1)
            for u in range(3):
                scores(0, 0, 0, u)
            units(pe, unit)

        @block.scalar
        def _(act):
            norm.scalar(act)
            act.wait_ge(k_cleared, 2)
            for b in range(B):
                act.wait_ge(k_done, b + 1)
                for g in range(KV_HEADS):
                    slot, at = slice(g * SLOT, (g + 1) * SLOT), slice(b * S, (b + 1) * S)
                    act.activation(k_hi[slot, g, at], k[slot, at], ACT.Copy).then_inc(k_hi_done, 1)

            def split_q(b, U):
                act.wait_ge(q_done, U + 1)
                act.activation(q_hi[:, b, :], q[:], ACT.Copy).then_inc(q_hi_done, 1)

            def exponentials(g, n, u):
                for r in UNIT_ROWS[u]:
                    act.wait_ge(max_done, 4 * n + max(r, 1) + 1)
                    act.activation(probs[:, g % 2, r, 0:(r + 1) * P], s_bank[u][:, ROW_AT[r]:ROW_AT[r] + (r + 1) * P],
                                   ACT.Exp, bias=neg_max[:, 4 * g + r:4 * g + r + 1],
                                   accum_out=row_sum[:, 4 * g + r:4 * g + r + 1]).then_inc(exp_done, 1)

            def turned_back(g, n, u):
                act.wait_ge(turned, 3 * n + u + 1)
                for r in UNIT_ROWS[u]:
                    from_ = t_bank[(3 * g + u) % 2][:, ROW_AT[r]:ROW_AT[r] + (r + 1) * P].rearrange("p (j q) -> p j q", q=P)
                    last = act.activation(probs_t[:, g, 0:r + 1, r * P:(r + 1) * P], from_, ACT.Copy)
                last.then_inc(probs_t_done, 1)

            def unit(c, b, more):
                U = B * c + b
                for g in range(KV_HEADS):
                    n = KV_HEADS * U + g
                    if g == 0:
                        act.wait_ge(o_ready, signals(U))
                    if g == 2 and more:
                        split_q(1 - b, U + 1)
                    for u in range(3):
                        turned_back(g, n, u)
                        for b1, g1 in next_heads(b, g, more):
                            exponentials(g1, n + 1, u)
                act.wait_ge(o_ready, signals(U + 1))
                act.wait_ge(out_done, signals(U))
                act.activation(o_hi[:], o_bank[:], ACT.Copy).then_inc(o_hi_done, 1)

            split_q(0, 0)
            for u in range(3):
                exponentials(0, 0, u)
            units(act, unit)

        @block.vector
        def _(dve):
            for one in (acc_read, o_lo_done,):
                dve.sem_inc(one, 1)
            norm.vector(dve)
            dve.wait_ge(loaded, 16 * 7)
            for b in range(B):
                dve.wait_ge(k_ready, b + 1)
                dve.scalar_tensor_tensor(k[:, b * S:(b + 1) * S], banks[2 + b][:], bk[:, 0:1], turn_k[:],
                                         ALU.add, ALU.mult).then_inc(k_done, 1)
            for h in range(NT // 2):
                dve.wait_ge(v_ready, h + 1)
                dve.tensor_tensor(v[:, 2 * h:2 * h + 2, :], banks[4 + h][:].rearrange("p (j n) -> p j n", n=WHOLE)[:, :, 0:P],
                                  bv[:].unsqueeze(1).broadcast_to([P, 2, P]), ALU.add).then_inc(v_done, 1)
            dve.wait_ge(k_cleared, 2)

            def rotate_q(c, b):
                U = B * c + b
                dve.wait_ge(q_ready, U + 1)
                dve.wait_ge(q_hi_done, U)
                dve.scalar_tensor_tensor(q[:], o_bank[:], bq[:, bass.ds(c, 1)], turn_q[:],
                                         ALU.add, ALU.mult).then_inc(q_done, 1)

            def low_q(b, U):
                dve.wait_ge(q_hi_done, U + 1)
                dve.tensor_tensor(q_lo[:, b, :], q[:], f32(q_hi[:, b, :]), ALU.subtract).then_inc(q_lo_done, 1)

            rotate_q(0, 0)
            low_q(0, 0)
            for b in range(B):
                for g in range(KV_HEADS):
                    slot, at = slice(g * SLOT, (g + 1) * SLOT), slice(b * S, (b + 1) * S)
                    dve.wait_ge(k_hi_done, b * KV_HEADS + g + 1)
                    dve.tensor_tensor(k_lo[slot, g, at], k[slot, at], f32(k_hi[slot, g, at]),
                                      ALU.subtract).then_inc(k_lo_done, 1)

            def row_max(g, n, u):
                dve.wait_ge(scores_ready, 3 * n + u + 1)
                for r in UNIT_ROWS[u]:
                    dve.tensor_reduce(neg_max[:, 4 * g + r:4 * g + r + 1], s_bank[u][:, ROW_AT[r]:ROW_AT[r] + (r + 1) * P],
                                      AX.X, ALU.max, negate=True).then_inc(max_done, 1)

            def normalise(g, n, u):
                for r in UNIT_ROWS[u]:
                    one = row_sum[:, 4 * g + r:4 * g + r + 1]
                    dve.wait_ge(exp_done, 4 * n + r + 1)
                    dve.reciprocal(one, one).then_inc(inverse_done, 1)
                    dve.wait_ge(inverse_done, 4 * n + r + 1)
                    mine = probs[:, g % 2, r, 0:(r + 1) * P]
                    dve.tensor_scalar(mine, mine, one, None, ALU.mult).then_inc(probs_done, 1)

            def add_to_stream(b, U):
                dve.wait_ge(out_done, signals(U + 1))
                for a in range(2):
                    two = res.x[:, b * TB + 2 * a:b * TB + 2 * a + 2, :]
                    dve.tensor_tensor(two, acc[a][:].rearrange("p (t d) -> p t d", d=D), two, ALU.add).then_inc(acc_read, 1)

            def unit(c, b, more):
                U = B * c + b
                for g in range(KV_HEADS):
                    n = KV_HEADS * U + g
                    following = next_heads(b, g, more)
                    for b1, g1 in following:
                        row_max(g1, n + 1, 0)
                    normalise(g, n, 2)
                    for b1, g1 in following:
                        row_max(g1, n + 1, 1)
                        normalise(g1, n + 1, 0)
                        row_max(g1, n + 1, 2)
                        normalise(g1, n + 1, 1)
                    if g == 1:
                        if b == 1:
                            add_to_stream(0, U - 1)
                        if more:
                            rotate_q(c + b, 1 - b)
                    if g == 2 and more:
                        low_q(1 - b, U + 1)
                dve.wait_ge(o_hi_done, U + 1)
                dve.tensor_tensor(o_lo[:], o_bank[:], f32(o_hi[:]), ALU.subtract).then_inc(o_lo_done, 1)
                if b == 1:
                    add_to_stream(1, U)

            for u in range(3):
                row_max(0, 0, u)
            for u in range(2):
                normalise(0, 0, u)
            dve.wait_ge(bo_added, 1)
            units(dve, unit)


RMS_EPS = 1e-6
FILLS = PER_KV + 1


def rms_gqa_stage(nc, name, res, t):
    with ExitStack() as ctx:
        sem = ctx.enter_context(Semaphores(nc, name))
        sb = lambda what, shape, dt=F32: ctx.enter_context(nc.sbuf_tensor(f"{name}_{what}", shape, dt))
        banks = [ctx.enter_context(nc.psum_tensor(f"{name}_bank{i}", [P, HALF], F32)) for i in range(8)]
        acc, s_bank, o_bank, sum_bank = banks[:2], banks[2:6], banks[6], banks[7]
        v_bank = (*acc, o_bank, s_bank[2])
        norm = Norm(nc, ctx, sem, f"{name}_ln", res, [b[:] for b in s_bank])

        kv_raw = sb("kv_raw", [P, GK_COLS])
        kv_hi, kv_lo = sb("kv_hi", [P, GK_COLS], F32R), sb("kv_lo", [P, GK_COLS], F32R)
        w_raw = sb("w_raw", [P, PER_KV, GQ_COLS])
        w_hi, w_lo = sb("w_hi", [P, PER_KV, GQ_COLS], F32R), sb("w_lo", [P, PER_KV, GQ_COLS], F32R)
        cos, sin = sb("cos", [P, S]), sb("sin", [P, S])
        half_turn, sum_sel, bv = sb("half_turn", [P, P]), sb("sum_sel", [P, P]), sb("bv", [P, P])
        ones = sb("ones", [P, 2])
        raw = sb("raw", [P, 2, S])
        square = sb("square", [P, 2, S])
        square_sums = sb("square_sums", [P, NT, 2])
        power, rms = sb("power", [P, 2 * NT]), sb("rms", [P, 2, NT])
        qk = sb("qk", [P, FILLS, TOK])
        scaled = sb("scaled", [P, 4, S])
        turned_part = sb("turned_part", [P, S])
        k_hi, k_lo = sb("k_hi", [P, KV_HEADS, TOK], F32R), sb("k_lo", [P, KV_HEADS, TOK], F32R)
        q_hi, q_lo = sb("q_hi", [P, S], F32R), sb("q_lo", [P, S], F32R)
        v = sb("v", [P, NT, P])
        exps = sb("exps", [P, 2, KV_HEADS, S])
        o_raw, o = sb("o_raw", [P, S]), sb("o", [P, S])
        o_hi, o_lo = sb("o_hi", [P, S], F32R), sb("o_lo", [P, S], F32R)

        w_loaded, pool_hi_done, pool_split = sem("w_loaded"), sem("pool_hi_done"), sem("pool_split")
        loaded, kv_hi_done, kv_split, w_hi_done, w_split = (
            sem("loaded"), sem("kv_hi_done"), sem("kv_split"), sem("w_hi_done"), sem("w_split"))
        k_cleared = sem("k_cleared")
        fill_ready, fill_copied, fill_squared, fill_summed = (
            sem("fill_ready"), sem("fill_copied"), sem("fill_squared"), sem("fill_summed"))
        v_ready, v_done, sums_read, rms_step, rms_done = (
            sem("v_ready"), sem("v_done"), sem("sums_read"), sem("rms_step"), sem("rms_done"))
        rms_spread, rms_applied, half_turned, half_read, cos_part, part_done = (
            sem("rms_spread"), sem("rms_applied"), sem("half_turned"), sem("half_read"), sem("cos_part"), sem("part_done"))
        k_hi_done, k_lo_done, q_hi_done, q_lo_done = sem("k_hi_done"), sem("k_lo_done"), sem("q_hi_done"), sem("q_lo_done")
        scores_ready, exp_done, o_ready, o_copied, sum_spread, inverse_done, o_done = (
            sem("scores_ready"), sem("exp_done"), sem("o_ready"), sem("o_copied"), sem("sum_spread"),
            sem("inverse_done"), sem("o_done"))
        o_hi_done, o_lo_done, out_done, acc_read = sem("o_hi_done"), sem("o_lo_done"), sem("out_done"), sem("acc_read")
        pair = lambda hi, lo, *at: (hi[(slice(None), *at)], lo[(slice(None), *at)])
        fills = [(b, f) for b in range(B) for f in (PER_KV, *range(PER_KV))]
        k_rotation = lambda b: FILLS * b
        q_rotation = lambda b, c: FILLS * b + 1 + c
        batch = lambda b: slice(b * S, (b + 1) * S)

        def units(engine, unit):
            for b in range(B):
                unit(b, 0, b * PER_KV)
                with engine.Fori(1, PER_KV - 1) as c:
                    unit(b, c, c + b * PER_KV)
                unit(b, PER_KV - 1, (b + 1) * PER_KV - 1)

        def is_last(c):
            return isinstance(c, int) and c == PER_KV - 1

        block = ctx.enter_context(nc.Block())

        @block.sync
        def _(sp):
            sp.dma_start(kv_raw[:], t["wd_kv"]).then_inc(w_loaded, 16)
            sp.dma_start(w_raw[:], t["wd_q"].rearrange("c p n -> p c n")).then_inc(w_loaded, 16)
            for to, src in ((cos, "cos"), (sin, "sin"), (half_turn, "half_turn"), (sum_sel, "sum_sel")):
                sp.dma_start(to[:], t[src]).then_inc(loaded, 16)
            sp.dma_start(bv[:], t["v_ones"].partition_broadcast(P)).then_inc(loaded, 16)

        @block.gpsimd
        def _(pool):
            norm.gpsimd(pool)
            pool.memset(power[:], -0.5).then_inc(rms_step, 1)
            pool.memset(ones[:], 1.0).then_inc(k_cleared, 1)
            pool.memset(f32(k_hi[:]), 0.0).then_inc(k_cleared, 1)
            pool.memset(f32(k_lo[:]), 0.0).then_inc(k_cleared, 1)
            pool.wait_ge(w_loaded, 16 * 2)
            for n, f in enumerate((2, 3)):
                pool.tensor_tensor(w_hi[:, f, :], w_raw[:, f, :], res.zero[:].broadcast_to([P, GQ_COLS]),
                                   ALU.add).then_inc(pool_hi_done, 1)
                pool.wait_ge(pool_hi_done, n + 1)
                pool.tensor_tensor(w_lo[:, f, :], w_raw[:, f, :], f32(w_hi[:, f, :]), ALU.subtract).then_inc(pool_split, 1)
            pool.wait_ge(sums_read, 2)
            pool.tensor_scalar(rms[:, 0, :], square_sums[:, :, 0], 1.0 / (Q_HEADS * HD), RMS_EPS, ALU.mult, ALU.add).then_inc(rms_step, 1)
            pool.tensor_scalar(rms[:, 1, :], square_sums[:, :, 1], 1.0 / (KV_HEADS * HD), RMS_EPS, ALU.mult, ALU.add).then_inc(rms_step, 1)
            pool.wait_ge(rms_step, 3)
            flat = rms[:].rearrange("p a t -> p (a t)")
            pool.tensor_tensor(flat, flat, power[:], ALU.pow).then_inc(rms_step, 1)
            pool.wait_ge(rms_step, 4)
            pool.tensor_scalar(rms[:, 0, :], rms[:, 0, :], HD ** -0.5, None, ALU.mult).then_inc(rms_done, 1)

        @block.tensor
        def _(pe):
            for one in (scores_ready, o_ready, sum_spread, out_done,):
                pe.sem_inc(one, 1)
            norm.tensor(pe)
            pe.wait_ge(norm.lo_done, NHALF * DC)
            pe.wait_ge(kv_split, 1)
            pe.wait_ge(k_cleared, 1)

            def sum_squares(m):
                b, f = fills[m]
                pe.wait_ge(fill_squared, m + 1)
                for j in range(TB):
                    at = 2 * ((b * TB + j) * 2 + (f == PER_KV))
                    last = pe.matmul(sum_bank[:, at:at + 2], square[:, m % 2, j * P:(j + 1) * P], ones[:],
                                     start=m == 0 and j == 0, stop=f >= PER_KV - 1, skip_group_check=True)
                last.then_inc(fill_summed, 1)

            for m, (b, f) in enumerate(fills):
                if m >= 4:
                    pe.wait_ge(fill_squared, m - 3)
                if 1 <= m <= 2:
                    pe.wait_ge(w_split, m)
                if 3 <= m <= 4:
                    pe.wait_ge(pool_split, m - 2)
                for c in range(DC):
                    at = slice(c * P, (c + 1) * P)
                    w = pair(w_hi, w_lo, f, at) if f < PER_KV else pair(kv_hi, kv_lo, slice((2 * c + 1) * P, (2 * c + 2) * P))
                    last = product(pe, s_bank[m % 4][:], w, pair(res.xh, res.xl, c, batch(b)), c == 0, c == DC - 1)
                last.then_inc(fill_ready, 1)
                if m:
                    sum_squares(m - 1)
            sum_squares(len(fills) - 1)
            for h in range(NT // 2):
                if h == 3:
                    pe.wait_ge(fill_squared, 7)
                for j in range(2):
                    for c in range(DC):
                        at = slice((2 * h + j) * P, (2 * h + j + 1) * P)
                        last = product(pe, v_bank[h][:, j * WHOLE:(j + 1) * WHOLE], pair(res.xh, res.xl, c, at),
                                       pair(kv_hi, kv_lo, slice(c * WHOLE, (c + 1) * WHOLE)),
                                       j == 0 and c == 0, c == DC - 1)
                last.then_inc(v_ready, 1)
            pe.wait_ge(rms_done, 1)
            def spread(b, a, bank):
                if 2 * b + a:
                    pe.wait_ge(rms_applied, 2 * b + a)
                for j in range(TB):
                    last = pe.matmul(bank[:, j * P:(j + 1) * P], rms[:, a, b * TB + j:b * TB + j + 1].broadcast_to([P, P]),
                                     res.ident[:], start=j == 0, stop=True, skip_group_check=True)
                last.then_inc(rms_spread, 1)

            def half(b, f, bank):
                pe.matmul(bank[:], half_turn[:], qk[:, bass.ds(f, 1), batch(b)].rearrange("p a n -> p (a n)"),
                          start=True, stop=True, skip_group_check=True).then_inc(half_turned, 1)

            pe.wait_ge(fill_squared, len(fills))
            for a in range(2):
                spread(0, a, s_bank[a])
            pe.wait_ge(v_done, NT // 2)
            half(0, PER_KV, s_bank[2])
            half(0, 0, s_bank[3])

            def attend(b, G, j):
                pe.wait_ge(exp_done, 16 * G + 4 * (j + 1))
                if j == 0:
                    pe.wait_ge(o_copied, G)
                for g in range(KV_HEADS):
                    slot = slice(g * SLOT, (g + 1) * SLOT)
                    last = pe.matmul(o_bank[slot, :], v[:, b * TB + j, slot], exps[:, j % 2, g, :],
                                     start=j == 0, stop=j == TB - 1, skip_group_check=True)
                last.then_inc(o_ready, 1)

            def finish(G, rotated):
                pe.wait_ge(o_copied, G + 1)
                pe.wait_ge(half_read, rotated)
                pe.matmul(sum_bank[:], sum_sel[:], o_raw[:], start=True, stop=True,
                          skip_group_check=True).then_inc(sum_spread, 1)

            def project_out(c, G):
                pe.wait_ge(o_lo_done, G + 1)
                for j in range(TB):
                    wo = (w_hi[:, c, DC * P:GQ_COLS], w_lo[:, c, DC * P:GQ_COLS])
                    last = product(pe, acc[j // 2][:, j % 2 * D:(j % 2 + 1) * D], pair(o_hi, o_lo, slice(j * P, (j + 1) * P)),
                                   wo, False, True)
                last.then_inc(out_done, 1)

            def scores(b, G, j):
                for g in range(KV_HEADS):
                    pe.wait_ge(exp_done, 16 * G + 4 * j + g - 3 if j else 16 * G)
                    product(pe, s_bank[g][:], pair(k_hi, k_lo, g, slice(b * S + j * P, b * S + (j + 1) * P)),
                            pair(q_hi, q_lo, slice(None)), True, True).then_inc(scores_ready, 1)

            def prepare(b, c, step):
                if not is_last(c):
                    if step == 1:
                        half(b, c + 1, sum_bank)
                elif b + 1 < B:
                    if step <= 2:
                        spread(b + 1, step - 1, sum_bank)
                    if step == 3:
                        pe.wait_ge(rms_applied, 2 * b + 4)
                        half(b + 1, PER_KV, sum_bank)
                    if step == 4:
                        pe.wait_ge(half_read, k_rotation(b + 1) + 1)
                        half(b + 1, 0, sum_bank)

            def unit(b, c, G):
                first = isinstance(c, int) and c == 0
                if first:
                    if b:
                        pe.wait_ge(acc_read, 2 * b)
                    for bank in acc:
                        pe.matmul(bank[:], res.zeros[:, 0:P], res.zeros[:], start=True, stop=False, skip_group_check=True)
                    pe.wait_ge(k_hi_done, (b + 1) * KV_HEADS)
                    pe.wait_ge(k_lo_done, (b + 1) * KV_HEADS)
                pe.wait_ge(q_lo_done, G + 1)
                scores(b, G, 0)
                if not first:
                    finish(G - 1, q_rotation(b, c) + 1)
                scores(b, G, 1)
                attend(b, G, 0)
                if not first:
                    project_out(c - 1, G - 1)
                prepare(b, c, 1)
                for j in range(2, TB):
                    scores(b, G, j)
                    attend(b, G, j - 1)
                    prepare(b, c, j)
                attend(b, G, TB - 1)
                prepare(b, c, TB)
                if is_last(c):
                    finish(G, q_rotation(b + 1, 0) + 1 if b + 1 < B else q_rotation(b, c) + 1)
                    project_out(c, G)

            units(pe, unit)

        @block.scalar
        def _(act):
            norm.scalar(act)
            act.wait_ge(w_loaded, 16 * 2)
            act.activation(kv_hi[:], kv_raw[:], ACT.Copy).then_inc(kv_hi_done, 1)
            for f in range(2):
                act.activation(w_hi[:, f, :], w_raw[:, f, :], ACT.Copy).then_inc(w_hi_done, 1)
            for m, (b, f) in enumerate(fills):
                act.wait_ge(fill_ready, m + 1)
                if m >= 2:
                    act.wait_ge(fill_summed, m - 1)
                act.activation(qk[:, f, batch(b)], s_bank[m % 4][:], ACT.Copy).then_inc(fill_copied, 1)
                act.wait_ge(fill_copied, m + 1)
                act.activation(square[:, m % 2, :], qk[:, f, batch(b)], ACT.Square).then_inc(fill_squared, 1)
            act.wait_ge(k_cleared, 3)
            def high_k(b):
                act.wait_ge(part_done, k_rotation(b) + 1)
                for g in range(KV_HEADS):
                    slot = slice(g * SLOT, (g + 1) * SLOT)
                    act.activation(k_hi[slot, g, batch(b)], qk[slot, PER_KV, batch(b)], ACT.Copy).then_inc(k_hi_done, 1)

            def unit(b, c, G):
                act.wait_ge(part_done, q_rotation(b, c) + 1)
                act.wait_ge(scores_ready, signals(16 * G))
                act.activation(q_hi[:], qk[:, bass.ds(c, 1), batch(b)].rearrange("p a n -> p (a n)"),
                               ACT.Copy).then_inc(q_hi_done, 1)
                for j in range(TB):
                    act.wait_ge(o_ready, signals(4 * G + j - 1 if j else 4 * G))
                    for g in range(KV_HEADS):
                        act.wait_ge(scores_ready, signals(16 * G + 4 * j + g + 1))
                        act.activation(exps[:, j % 2, g, :], s_bank[g][:], ACT.Exp).then_inc(exp_done, 1)
                act.wait_ge(sum_spread, signals(G))
                act.wait_ge(o_done, signals(G))
                act.wait_ge(o_ready, signals(4 * G + 4))
                act.activation(o_raw[:], o_bank[:], ACT.Copy).then_inc(o_copied, 1)

                if is_last(c) and b + 1 < B:
                    high_k(b + 1)

            high_k(0)
            units(act, unit)

        @block.vector
        def _(dve):
            for one in (o_done,):
                dve.sem_inc(one, 1)
            norm.vector(dve)
            dve.wait_ge(kv_hi_done, 1)
            dve.tensor_tensor(kv_lo[:], kv_raw[:], f32(kv_hi[:]), ALU.subtract).then_inc(kv_split, 1)
            for f in range(2):
                dve.wait_ge(w_hi_done, f + 1)
                dve.tensor_tensor(w_lo[:, f, :], w_raw[:, f, :], f32(w_hi[:, f, :]), ALU.subtract).then_inc(w_split, 1)
            dve.wait_ge(loaded, 16 * 5)
            for h in range(NT // 2):
                dve.wait_ge(v_ready, h + 1)
                dve.tensor_tensor(v[:, 2 * h:2 * h + 2, :], v_bank[h][:].rearrange("p (j n) -> p j n", n=WHOLE)[:, :, 0:P],
                                  bv[:].unsqueeze(1).broadcast_to([P, 2, P]), ALU.add).then_inc(v_done, 1)
            dve.wait_ge(fill_summed, len(fills))
            sums = sum_bank[:, 0:4 * NT].rearrange("p (t a two) -> p t a two", t=NT, a=2)[:, :, :, 0]
            dve.tensor_copy(square_sums[:], sums).then_inc(sums_read, 2)

            def apply_rms(b, a, bank):
                dve.wait_ge(rms_spread, 2 * b + a + 1)
                if b:
                    dve.wait_ge(part_done, k_rotation(b))
                dve.tensor_tensor(scaled[:, 2 * a, :], bank[:], cos[:], ALU.mult)
                dve.tensor_tensor(scaled[:, 2 * a + 1, :], bank[:], sin[:], ALU.mult).then_inc(rms_applied, 1)

            def rotate(b, f, bank):
                is_k = isinstance(f, int) and f == PER_KV
                n, a = (k_rotation(b), 2) if is_k else (q_rotation(b, f), 0)
                now = qk[:, bass.ds(f, 1), batch(b)].rearrange("p a n -> p (a n)")
                dve.wait_ge(rms_applied, 2 * b + 2)
                dve.wait_ge(part_done, n)
                dve.wait_ge(half_turned, n + 1)
                dve.tensor_tensor(turned_part[:], bank[:], scaled[:, a + 1, :], ALU.mult).then_inc(half_read, 1)
                dve.tensor_tensor(now, now, scaled[:, a, :], ALU.mult).then_inc(cos_part, 1)
                dve.wait_ge(half_read, n + 1)
                dve.wait_ge(cos_part, n + 1)
                dve.tensor_tensor(now, now, turned_part[:], ALU.add).then_inc(part_done, 1)

            def low_k(b):
                for g in range(KV_HEADS):
                    slot = slice(g * SLOT, (g + 1) * SLOT)
                    dve.wait_ge(k_hi_done, b * KV_HEADS + g + 1)
                    dve.tensor_tensor(k_lo[slot, g, batch(b)], qk[slot, PER_KV, batch(b)], f32(k_hi[slot, g, batch(b)]),
                                      ALU.subtract).then_inc(k_lo_done, 1)

            def split_q(b, c, G):
                dve.wait_ge(q_hi_done, G + 1)
                dve.tensor_tensor(q_lo[:], qk[:, bass.ds(c, 1), batch(b)].rearrange("p a n -> p (a n)"), f32(q_hi[:]),
                                  ALU.subtract).then_inc(q_lo_done, 1)

            def divide(G):
                dve.wait_ge(sum_spread, signals(G + 1))
                dve.reciprocal(o[:], sum_bank[:]).then_inc(inverse_done, 1)
                dve.wait_ge(inverse_done, G + 1)
                dve.tensor_tensor(o[:], o[:], o_raw[:], ALU.mult).then_inc(o_done, 1)
                dve.wait_ge(o_done, signals(G + 1))
                dve.wait_ge(out_done, signals(G))
                dve.tensor_copy(o_hi[:], o[:]).then_inc(o_hi_done, 1)
                dve.wait_ge(o_hi_done, G + 1)
                dve.tensor_tensor(o_lo[:], o[:], f32(o_hi[:]), ALU.subtract).then_inc(o_lo_done, 1)

            def unit(b, c, G):
                split_q(b, c, G)
                if not (isinstance(c, int) and c == 0):
                    divide(G - 1)
                if not is_last(c):
                    rotate(b, c + 1, sum_bank)
                    return
                if b + 1 < B:
                    for a in range(2):
                        apply_rms(b + 1, a, sum_bank)
                    rotate(b + 1, PER_KV, sum_bank)
                    rotate(b + 1, 0, sum_bank)
                divide(G)
                if b + 1 < B:
                    low_k(b + 1)
                dve.wait_ge(out_done, signals((b + 1) * PER_KV))
                for a in range(2):
                    two = res.x[:, b * TB + 2 * a:b * TB + 2 * a + 2, :]
                    dve.tensor_tensor(two, acc[a][:].rearrange("p (t d) -> p t d", d=D), two, ALU.add).then_inc(acc_read, 1)

            for a in range(2):
                apply_rms(0, a, s_bank[a])
            rotate(0, PER_KV, s_bank[2])
            rotate(0, 0, s_bank[3])
            low_k(0)
            units(dve, unit)


SEG = 64
PAIRS = S // (2 * SEG)
SEGS = S // SEG
CHAINS = B * GROUP
RUN = HEADS
RUNS = S // RUN
MZ = DH + 2


def recurrent_stage(nc, name, res, t):
    scale = 1.0 / DH ** 0.5
    with ExitStack() as ctx:
        sem = ctx.enter_context(Semaphores(nc, name))
        sb = lambda what, shape, dt=F32: ctx.enter_context(nc.sbuf_tensor(f"{name}_{what}", shape, dt))
        memory_bank = [ctx.enter_context(nc.psum_tensor(f"{name}_memory{b}", [P, 2, HALF], F32)) for b in range(B)]
        work = [ctx.enter_context(nc.psum_tensor(f"{name}_work{i}", [P, HALF], F32)) for i in range(4)]
        retrieved = [m[:].rearrange("p c (u n) -> p (c u) n", u=2) for m in memory_bank]

        read_nat = sb("read_nat", [P, CHAINS, PAIRS, DH])
        in_order = read_nat[:].rearrange("p m j n -> p m (j n)")
        norm = Norm(nc, ctx, sem, f"{name}_ln", res, [w[:] for w in work],
                    read_nat[:].rearrange("p a b n -> p (a b n)")[:, 0:NT * D].rearrange("p (t d) -> p t d", d=D))
        w_raw = sb("w_raw", [P, 2, DC * WIDE])
        w_hi, w_lo = sb("w_hi", [P, 3, DC * WIDE], F32R), sb("w_lo", [P, 3, DC * WIDE], F32R)
        k, q = sb("k", [P, CHAINS, S]), sb("q", [P, CHAINS, S])
        dot = q
        sigma = sb("sigma", [P, CHAINS, PAIRS, 4, SEG])
        sigma_k = sb("sigma_k", [P, CHAINS, PAIRS, DH])
        v = sb("v", [P, NT, WIDE])
        exp_part, positive = sb("exp_part", [P, 2, S]), sb("positive", [P, S])
        memory, delta = sb("memory", [P, CHAINS, MZ]), sb("delta", [P, CHAINS, MZ])
        inverse = sb("inverse", [P, CHAINS])
        seg_mask = sb("seg_mask", [P, P], BF16)
        probs, probs_t = sb("probs", [P, 2, TB, P]), sb("probs_t", [P, TB, P])
        neg_max, row_sum = sb("neg_max", [P, 2, TB]), sb("row_sum", [P, 2, TB])
        o_hi, o_lo = sb("o_hi", [P, 2, GROUP, CHAINS * RUNS], F32R), sb("o_lo", [P, 2, GROUP, CHAINS * RUNS], F32R)
        gate = sb("gate", [P, HEADS])
        neg_gate, rest_gate = sb("neg_gate", [P, GROUP]), sb("rest_gate", [P, GROUP])

        w_loaded = [sem(f"w_loaded{i}") for i in range(3)]
        w_split = [sem(f"w_split{i}") for i in range(3)]
        x_reloaded, x_stored, x_back = sem("x_reloaded"), sem("x_stored"), sem("x_back")
        w_hi_done, betas_loaded, gate_step, gates_done, mask_step = (
            sem("w_hi_done"), sem("betas_loaded"), sem("gate_step"), sem("gates_done"), sem("mask_step"))
        k_ready, q_ready, kq_read, k_sided, sigma_done = (
            sem("k_ready"), sem("q_ready"), sem("kq_read"), sem("k_sided"), sem("sigma_done"))
        v_ready, v_done, sigma_turned, sigma_k_done = sem("v_ready"), sem("v_done"), sem("sigma_turned"), sem("sigma_k_done")
        delta_set, memory_done, retrieved_ready, inverse_done, delta_done, read_done, update_ready = (
            sem("delta_set"), sem("memory_done"), sem("retrieved_ready"), sem("inverse_done"), sem("delta_done"),
            sem("read_done"), sem("update_ready"))
        scores_ready, max_raw, max_done, exp_done, sum_inverse, probs_done = (
            sem("scores_ready"), sem("max_raw"), sem("max_done"), sem("exp_done"), sem("sum_inverse"), sem("probs_done"))
        turned, probs_t_done, dot_ready, dot_done = sem("turned"), sem("probs_t_done"), sem("dot_ready"), sem("dot_done")
        read_turned, att_done, o_hi_done, o_lo_done, out_done, x_added = (
            sem("read_turned"), sem("att_done"), sem("o_hi_done"), sem("o_lo_done"), sem("out_done"), sem("x_added"))
        o_parts = HEADS // GROUP
        K_PART, Q_PART, V_PART = (t["wa_k"], 2, 0), (t["wa_q"], 0, 0), (t["wa_v"], 1, 0)
        O_SLOT = (0, 1, 2, 0)
        o_part = [(t["wa_o"][i:i + 1], O_SLOT[i], 1 + i // 3) for i in range(o_parts)]
        in_slot = (3, 2, 2)

        def split_before(slot, G, before):
            if slot < 2:
                return in_slot[slot] * G + before
            k_of_0 = isinstance(G, int) and G == 0 and before == 0
            last = isinstance(G, int) and G == GROUPS - 1 and before
            return 0 if k_of_0 else 2 * G - 1 if before == 0 else 2 * G + 2 - bool(last)

        qv_hi_done = sem("qv_hi_done")
        RAW = (0, 1, 1)
        JOBS = [(kind, m) for m in range(CHAINS) for kind in ("v", "q", "turn")]

        def groups(engine, group):
            with engine.Fori(0, GROUPS - 1) as G:
                group(G, True)
            group(GROUPS - 1, False)

        batch = lambda b: slice(b * S, (b + 1) * S)

        def dot_runs(i):
            return dot[:].rearrange("p m (n c) -> p (m n) c", c=RUN)[:, :, i * GROUP:(i + 1) * GROUP]

        def chain_runs(ap):
            return ap.rearrange("p c n -> p n c")

        def key_rows(seg):
            return slice(seg % 2 * SEG, seg % 2 * SEG + SEG)

        def query_rows(seg):
            return key_rows(seg + 1)

        x_in, x_mid = t["x"], t["x_mid"]

        def row_tiles(h):
            return res.x[h * RUNS:(h + 1) * RUNS, :, :]

        def rows_of(stream, b, h):
            at = h * SEG // RUN
            return stream[b].rearrange("(s g n) d -> s g n d", g=GROUPS, n=RUN)[:, :, at:at + SEG // RUN, :]

        block = ctx.enter_context(nc.Block())

        @block.sync
        def _(sp):
            sp.dma_start(gate[:], t["ba_gate"]).then_inc(betas_loaded, 16)
            def load(G, part, after=None):
                weights, slot, before = part
                sp.wait_ge(*after or (w_split[slot], split_before(slot, G, before)))
                which = weights[bass.ds(G, 1), :, :] if weights.shape[0] > 1 else weights
                sp.dma_start(w_raw[:, RAW[slot], :], which.rearrange("a p n -> (a p) n")).then_inc(w_loaded[slot], 16)

            def group(G, more, between):
                load(G, o_part[0])
                if more:
                    load(G + 1, K_PART, (w_split[1], in_slot[1] * G + 1))
                between()
                load(G, o_part[1], (w_split[2], 2 * G + 2) if more else None)
                load(G, o_part[2], (w_split[1], in_slot[1] * G + 2))
                load(G, o_part[3])
                if more:
                    load(G + 1, V_PART, (w_split[2], 2 * G + 3))
                    load(G + 1, Q_PART)

            def store(G):
                sp.wait_ge(x_added, signals(B * (G + 1)))
                for b in range(B):
                    for h in range(GROUP):
                        tile = row_tiles(h)[:, bass.ds(b * GROUPS + G, 1), :].rearrange("p a d -> p (a d)")
                        sp.dma_start(rows_of(x_mid, b, h)[:, bass.ds(G, 1), :, :].rearrange("s a u d -> s (a u) d"), tile
                                     ).then_inc(x_stored, 16)

            def reload():
                sp.wait_ge(norm.normed, NT)
                for b in range(B):
                    for h in range(GROUP):
                        for g in range(GROUPS):
                            sp.dma_start(row_tiles(h)[:, b * GROUPS + g, :], rows_of(x_in, b, h)[:, g, :, :]).then_inc(x_reloaded, 16)

            sp.dma_start(w_raw[:, 1, :], K_PART[0][0, :, :]).then_inc(w_loaded[2], 16)
            sp.dma_start(w_raw[:, 0, :], Q_PART[0][0, :, :]).then_inc(w_loaded[0], 16)
            load(0, V_PART, (w_split[2], 1))
            group(0, True, reload)
            with sp.Fori(1, GROUPS - 1) as G:
                group(G, True, lambda: store(G - 1))
            group(GROUPS - 1, False, lambda: store(GROUPS - 2))
            store(GROUPS - 1)
            sp.wait_ge(x_stored, 16 * B * GROUP * GROUPS)
            sp.dma_start(res.x[:], x_mid.rearrange("b (t p) d -> p (b t) d", p=P)).then_inc(x_back, 16)
            sp.wait_ge(x_back, 16)

        @block.gpsimd
        def _(pool):
            pool.tensor_copy(seg_mask[:], res.causal[:]).then_inc(mask_step, 1)
            pool.wait_ge(mask_step, 1)
            pool.memset(seg_mask[SEG:P, 0:SEG], NEG).then_inc(mask_step, 1)
            pool.wait_ge(mask_step, 2)
            norm.gpsimd(pool)

            def split(G, part, n):
                weights, slot, before = part
                pool.wait_ge(w_loaded[slot], 16 * split_before(slot, G, before) + 16)
                pool.tensor_tensor(w_hi[:, slot, :], w_raw[:, RAW[slot], :], res.zero[:].broadcast_to([P, DC * WIDE]),
                                   ALU.add).then_inc(w_hi_done, 1)
                pool.wait_ge(w_hi_done, n)
                pool.tensor_tensor(w_lo[:, slot, :], w_raw[:, RAW[slot], :], f32(w_hi[:, slot, :]),
                                   ALU.subtract).then_inc(w_split[slot], 1)

            def group(G, more):
                n = (o_parts + 1) * G + 1
                pool.wait_ge(q_ready, CHAINS * G + CHAINS)
                split(G, o_part[0], n + 1)
                if more:
                    pool.wait_ge(k_ready, CHAINS * G + CHAINS)
                    split(G + 1, K_PART, n + 2)
                pool.wait_ge(v_ready, NT * G + NT)
                split(G, o_part[1], n + 2 + more)
                if more:
                    pool.wait_ge(k_ready, CHAINS * G + 2 * CHAINS)
                split(G, o_part[2], n + 3 + more)
                pool.wait_ge(out_done, signals(o_parts * G + 1))
                split(G, o_part[3], n + 4 + more)

            split(0, K_PART, 1)
            groups(pool, group)

        @block.tensor
        def _(pe):
            for one in (turned, dot_ready, out_done,):
                pe.sem_inc(one, 1)
            norm.tensor(pe)
            pe.wait_ge(norm.lo_done, norm.ready(0))
            pe.wait_ge(mask_step, 2)

            def fill(G, m, slot, bank, ready):
                b, h = divmod(m, GROUP)
                for c in range(DC):
                    w = slice(c * WIDE + h * DH, c * WIDE + (h + 1) * DH)
                    last = product(pe, bank[:], (w_hi[:, slot, w], w_lo[:, slot, w]),
                                   (res.xh[:, c, batch(b)], res.xl[:, c, batch(b)]), c == 0, c == DC - 1)
                last.then_inc(ready, 1)

            def k_fill(G, m):
                if m == 0:
                    pe.wait_ge(w_split[2], split_before(2, G, 0) + 1)
                if m >= 2:
                    pe.wait_ge(kq_read, 2 * CHAINS * G + m - 1)
                fill(G, m, 2, work[m % 2], k_ready)

            def v_fill(G, j, bank):
                for c in range(DC):
                    w, at = slice(c * WIDE, (c + 1) * WIDE), slice(j * P, (j + 1) * P)
                    last = product(pe, bank[:], (res.xh[:, c, at], res.xl[:, c, at]),
                                   (w_hi[:, 1, w], w_lo[:, 1, w]), c == 0, c == DC - 1)
                last.then_inc(v_ready, 1)

            def turn_sigma_k(G, m, bank):
                pe.wait_ge(sigma_done, 2 * CHAINS * G + m + 1)
                for j in range(PAIRS):
                    at = slice(j * P, (j + 1) * P)
                    last = pe.transpose(bank[:, at], in_order[:, m, at], res.ident[:])
                last.then_inc(sigma_turned, 1)

            def first_phase(G):
                for x, (kind, m) in enumerate(JOBS):
                    if x >= 4:
                        before, n = JOBS[x - 4]
                        pe.wait_ge(*{"q": (kq_read, 2 * CHAINS * G + CHAINS + n + 1), "v": (v_done, NT * G + n + 1),
                                     "turn": (sigma_k_done, CHAINS * G + n + 1)}[before])
                    bank = work[x % 4]
                    if kind == "q":
                        if m == 0:
                            pe.wait_ge(w_split[0], in_slot[0] * G + 1)
                        fill(G, m, 0, bank, q_ready)
                    elif kind == "v":
                        if m == 0:
                            pe.wait_ge(w_split[1], in_slot[1] * G + 1)
                        v_fill(G, m, bank)
                    else:
                        turn_sigma_k(G, m, bank)

            def retrieve(G, seg, b):
                pe.wait_ge(memory_done, 2 * SEGS * G + max(2 * seg + b + 1, 2))
                for h in range(GROUP):
                    m, side = b * GROUP + h, slice(seg % 2 * 2, seg % 2 * 2 + 2)
                    last = pe.matmul(retrieved[b][:, h, 0:MZ], sigma[:, m, seg // 2, side, :].rearrange("p a n -> p (a n)"),
                                     memory[:, m, :], start=True, stop=True, skip_group_check=True)
                last.then_inc(retrieved_ready, 1)

            def update(G, seg, b):
                pe.wait_ge(delta_done, 2 * SEGS * G + 2 * seg + b + 1)
                pe.wait_ge(read_done, 2 * SEGS * G + 2 * seg + b + 1)
                rows = key_rows(seg)
                for h in range(GROUP):
                    m = b * GROUP + h
                    last = pe.matmul(retrieved[b][:, h, 0:MZ], sigma_k[rows, m, seg // 2, :], delta[rows, m, :],
                                     start=True, stop=True, skip_group_check=True)
                last.then_inc(update_ready, 1)

            def scores(G, m):
                if m >= 2:
                    pe.wait_ge(exp_done, TB * CHAINS * G + TB * (m - 1))
                for j in range(TB):
                    at, to = slice(j * P, (j + 1) * P), work[m % 2][:, j * P:(j + 1) * P]
                    pe.matmul(to, q[:, m, at], k[:, m, at], start=j == 0, stop=False, skip_group_check=True)
                    last = pe.matmul(to, res.ident_bf[:], seg_mask[:], start=False, stop=True, skip_group_check=True)
                last.then_inc(scores_ready, 1)

            def attend(G, m):
                pe.wait_ge(probs_done, CHAINS * G + m + 1)
                pe.wait_ge(probs_t_done, signals(CHAINS * G + m))
                for j in range(TB):
                    last = pe.transpose(work[2][:, j * P:(j + 1) * P], probs[:, m % 2, j, :], res.ident[:])
                last.then_inc(turned, 1)
                b, h = divmod(m, GROUP)
                pe.wait_ge(probs_t_done, signals(CHAINS * G + m + 1))
                pe.wait_ge(dot_done, signals(CHAINS * G + m))
                for j in range(TB):
                    last = pe.matmul(work[3][:, j * P:(j + 1) * P], v[:, b * TB + j, h * DH:(h + 1) * DH], probs_t[:, j, :],
                                     start=j == 0, stop=True, skip_group_check=True)
                last.then_inc(dot_ready, 1)

            def turn_read(G, m):
                if m >= 2:
                    pe.wait_ge(att_done, signals(2 * CHAINS * G + 2 * (m - 1)))
                for j in range(PAIRS):
                    last = pe.transpose(work[2 + m % 2][:, j * P:(j + 1) * P], read_nat[:, m, j, :], res.ident[:])
                last.then_inc(read_turned, 1)

            def project_out(G, i):
                slot = O_SLOT[i]
                pe.wait_ge(w_split[slot], split_before(slot, G, 1 + i // 3) + 1)
                pe.wait_ge(o_lo_done, o_parts * G + i + 1)
                for n in range(GROUP):
                    c, w = i * GROUP + n, slice(n * D, (n + 1) * D)
                    for b in range(B):
                        at = slice(b * P, (b + 1) * P)
                        last = product(pe, memory_bank[b][:, 0, 0:D], (o_hi[:, i % 2, n, at], o_lo[:, i % 2, n, at]),
                                       (w_hi[:, slot, w], w_lo[:, slot, w]), c == 0, c == HEADS - 1)
                last.then_inc(out_done, 1)

            def group(G, more):
                pe.wait_ge(att_done, signals(2 * CHAINS * G))
                pe.wait_ge(kq_read, 2 * CHAINS * G + CHAINS)
                first_phase(G)
                pe.wait_ge(sigma_done, 2 * CHAINS * G + 2 * CHAINS)
                pe.wait_ge(k_sided, CHAINS * (G + 1))
                pe.wait_ge(v_done, NT * (G + 1))
                pe.wait_ge(x_added, signals(B * G))
                pe.wait_ge(sigma_k_done, CHAINS * G + CHAINS)
                for seg in range(SEGS):
                    for b in range(B):
                        retrieve(G, seg, b)
                    scores(G, seg)
                    if seg < SEGS - 1:
                        for b in range(B):
                            update(G, seg, b)
                    if seg:
                        attend(G, seg - 1)
                attend(G, CHAINS - 1)
                pe.wait_ge(read_done, 2 * SEGS * (G + 1))
                pe.wait_ge(delta_done, 2 * SEGS * (G + 1))
                pe.wait_ge(exp_done, TB * CHAINS * (G + 1))
                pe.wait_ge(dot_done, signals(CHAINS * (G + 1)))
                for m in range(CHAINS):
                    turn_read(G, m)
                    if more:
                        k_fill(G + 1, m)
                for i in range(o_parts):
                    project_out(G, i)

            for m in range(CHAINS):
                if m == GROUP:
                    pe.wait_ge(norm.lo_done, norm.ready(1))
                k_fill(0, m)
            groups(pe, group)

        @block.scalar
        def _(act):
            for one in (probs_t_done, dot_done,):
                act.sem_inc(one, 1)
            act.wait_ge(betas_loaded, 16)
            act.activation(gate[:], gate[:], ACT.Exp, scale=-1.0).then_inc(gate_step, 1)
            norm.scalar(act)

            def read_queries(G, seg, b):
                act.wait_ge(inverse_done, 2 * SEGS * G + 2 * seg + b + 1)
                rows = query_rows(seg)
                for h in range(GROUP):
                    m = b * GROUP + h
                    last = act.activation(read_nat[rows, m, seg // 2, :], retrieved[b][rows, h, 0:DH], ACT.Copy,
                                          scale=inverse[rows, m:m + 1])
                last.then_inc(read_done, 1)

            def exponentials(G, m):
                act.wait_ge(max_done, CHAINS * G + m + 1)
                act.wait_ge(turned, signals(CHAINS * G + max(m - 1, 0)))
                for j in range(TB):
                    act.activation(probs[:, m % 2, j, :], work[m % 2][:, j * P:(j + 1) * P], ACT.Exp, scale=scale,
                                   bias=neg_max[:, m % 2, j:j + 1],
                                   accum_out=row_sum[:, m % 2, j:j + 1]).then_inc(exp_done, 1)

            def softmax_part(G, m):
                act.wait_ge(turned, signals(CHAINS * G + m + 1))
                act.wait_ge(dot_ready, signals(CHAINS * G + m))
                act.activation(probs_t[:].rearrange("p j n -> p (j n)"), work[2][:], ACT.Copy).then_inc(probs_t_done, 1)
                act.wait_ge(dot_ready, signals(CHAINS * G + m + 1))
                act.activation(dot[:, m, :], work[3][:], ACT.Copy,
                               scale=rest_gate[:, m % GROUP:m % GROUP + 1]).then_inc(dot_done, 1)

            def evacuate(f, to, m, bank):
                act.activation(to[:, m, :], bank[:], ACT.Copy)
                act.activation(exp_part[:, m % 2, :], bank[:], ACT.Exp)
                act.wait_ge(sigma_done, f)
                act.activation(positive[:], bank[:], ACT.Relu).then_inc(kq_read, 1)

            def high_parts(G):
                for n, slot in enumerate((1, 0)):
                    if not (isinstance(G, int) and G == 0):
                        act.wait_ge(out_done, signals(o_parts * G - 2 + 2 * n))
                    act.wait_ge(w_loaded[slot], 16 * in_slot[slot] * G + 16)
                    act.activation(w_hi[:, slot, :], w_raw[:, RAW[slot], :], ACT.Copy).then_inc(qv_hi_done, 1)

            def evacuate_k(G, m):
                act.wait_ge(k_ready, CHAINS * G + m + 1)
                evacuate(2 * CHAINS * G + m, k, m, work[m % 2])

            def group(G, more):
                for x, (kind, m) in enumerate(JOBS):
                    if kind == "q":
                        act.wait_ge(q_ready, CHAINS * G + m + 1)
                        evacuate(2 * CHAINS * G + CHAINS + m, q, m, work[x % 4])
                    if kind == "turn":
                        act.wait_ge(sigma_turned, CHAINS * G + m + 1)
                        act.activation(sigma_k[:, m, :, :].rearrange("p j n -> p (j n)"), work[x % 4][:],
                                       ACT.Copy).then_inc(sigma_k_done, 1)
                act.wait_ge(gates_done, 2 * G + 2)
                for seg in range(SEGS):
                    for b in range(B):
                        read_queries(G, seg, b)
                    exponentials(G, seg)
                    if seg:
                        softmax_part(G, seg - 1)
                softmax_part(G, CHAINS - 1)
                if more:
                    for m in range(CHAINS):
                        evacuate_k(G + 1, m)
                act.wait_ge(att_done, signals(2 * CHAINS * (G + 1)))
                for i in range(o_parts):
                    if i >= 2:
                        act.wait_ge(out_done, signals(o_parts * G + i - 1))
                    act.activation(chain_runs(o_hi[:, i % 2]), dot_runs(i), ACT.Copy).then_inc(o_hi_done, 1)
                if more:
                    high_parts(G + 1)

            for m in range(CHAINS):
                evacuate_k(0, m)
                if m == 1:
                    high_parts(0)
            groups(act, group)

        @block.vector
        def _(dve):
            for one in (att_done, x_added,):
                dve.sem_inc(one, 1)
            dve.wait_ge(gate_step, 1)
            dve.tensor_scalar(gate[:], gate[:], 1.0, None, ALU.add).then_inc(gate_step, 1)
            dve.wait_ge(gate_step, 2)
            dve.reciprocal(gate[:], gate[:]).then_inc(gate_step, 1)
            dve.memset(delta[:], 0.0).then_inc(delta_set, 1)
            dve.wait_ge(delta_set, 1)
            dve.memset(delta[:, :, DH:DH + 1], -1.0).then_inc(delta_set, 1)
            norm.vector(dve)
            dve.wait_ge(gate_step, 3)

            def feature_map(f, m, sides):
                dve.wait_ge(kq_read, f + 1)
                split = lambda ap: ap.rearrange("p (j s n) -> p j s n", s=2, n=SEG)
                for s, side in enumerate(sides):
                    last = dve.scalar_tensor_tensor(sigma[:, m, :, side, :], split(exp_part[:, m % 2, :])[:, :, s, :], 1.0,
                                                    split(positive[:])[:, :, s, :], ALU.min, ALU.add)
                return last

            def low_parts(G):
                for n, slot in enumerate((1, 0)):
                    dve.wait_ge(qv_hi_done, 2 * G + n + 1)
                    dve.tensor_tensor(w_lo[:, slot, :], w_raw[:, RAW[slot], :], f32(w_hi[:, slot, :]),
                                      ALU.subtract).then_inc(w_split[slot], 1)

            def k_feature_map(G, m):
                f = 2 * CHAINS * G + m
                dve.wait_ge(kq_read, f + 1)
                dve.scalar_tensor_tensor(in_order[:, m, :], exp_part[:, m % 2, :], 1.0, positive[:],
                                         ALU.min, ALU.add).then_inc(sigma_done, 1)

            def k_sides(G, some):
                for m in some:
                    dve.wait_ge(sigma_done, 2 * CHAINS * G + m + 1)
                    for s, side in enumerate((0, 3)):
                        last = dve.tensor_copy(sigma[:, m, :, side, :],
                                               in_order[:, m, :].rearrange("p (j s n) -> p j s n", s=2, n=SEG)[:, :, s, :])
                    last.then_inc(k_sided, 1)

            def deltas(G, seg, b):
                rows, mine = key_rows(seg), slice(b * GROUP, (b + 1) * GROUP)
                dve.wait_ge(retrieved_ready, 2 * SEGS * G + 2 * seg + b + 1)
                dve.reciprocal(inverse[:, mine], retrieved[b][:, :, DH]).then_inc(inverse_done, 1)
                dve.wait_ge(inverse_done, 2 * SEGS * G + 2 * seg + b + 1)
                for h in range(GROUP):
                    m = b * GROUP + h
                    last = dve.scalar_tensor_tensor(delta[rows, m, 0:DH], retrieved[b][rows, h, 0:DH], inverse[rows, m:m + 1],
                                                    v[rows, b * TB + seg // 2, h * DH:(h + 1) * DH], ALU.mult, ALU.add)
                last.then_inc(delta_done, 1)

            def remember(G, seg, b):
                mine = slice(b * GROUP, (b + 1) * GROUP)
                dve.wait_ge(update_ready, 2 * (SEGS - 1) * G + 2 * seg + b + 1)
                dve.tensor_tensor(memory[:, mine, :], memory[:, mine, :], retrieved[b][:, :, 0:MZ],
                                  ALU.add).then_inc(memory_done, 1)

            def maximum(G, m):
                dve.wait_ge(scores_ready, CHAINS * G + m + 1)
                dve.tensor_reduce(neg_max[:, m % 2, :], work[m % 2][:].rearrange("p (j n) -> p j n", n=P), AX.X, ALU.max,
                                  negate=True).then_inc(max_raw, 1)
                dve.wait_ge(max_raw, CHAINS * G + m + 1)
                dve.tensor_scalar(neg_max[:, m % 2, :], neg_max[:, m % 2, :], scale, None, ALU.mult).then_inc(max_done, 1)

            def normalise(G, m):
                dve.wait_ge(exp_done, TB * CHAINS * G + TB * (m + 1))
                dve.reciprocal(row_sum[:, m % 2, :], row_sum[:, m % 2, :]).then_inc(sum_inverse, 1)
                dve.wait_ge(sum_inverse, CHAINS * G + m + 1)
                dve.tensor_tensor(probs[:, m % 2, :, :], probs[:, m % 2, :, :], spread(row_sum[:, m % 2, :], P),
                                  ALU.mult).then_inc(probs_done, 1)

            def mix(G, m):
                dve.wait_ge(read_turned, CHAINS * G + m + 1)
                dve.wait_ge(dot_done, signals(CHAINS * G + m + 1))
                halves = lambda ap: ap.rearrange("p (j s n) -> p j s n", s=2, n=SEG)
                for s in range(2):
                    dve.scalar_tensor_tensor(halves(dot[:, m, :])[:, :, s, :], halves(work[2 + m % 2][:])[:, :, 1 - s, :],
                                             neg_gate[:, m % GROUP:m % GROUP + 1], halves(dot[:, m, :])[:, :, s, :],
                                             ALU.mult, ALU.add).then_inc(att_done, 1)

            def low_part(G, i):
                dve.wait_ge(o_hi_done, o_parts * G + i + 1)
                if i >= 2:
                    dve.wait_ge(out_done, signals(o_parts * G + i - 1))
                dve.tensor_tensor(chain_runs(o_lo[:, i % 2]), dot_runs(i), f32(chain_runs(o_hi[:, i % 2])),
                                  ALU.subtract).then_inc(o_lo_done, 1)

            def group(G, more):
                dve.wait_ge(out_done, signals(o_parts * G))
                dve.tensor_scalar(neg_gate[:], gate[:, bass.ds(G * GROUP, GROUP)], -1.0, None, ALU.mult).then_inc(gates_done, 1)
                dve.tensor_scalar(rest_gate[:], gate[:, bass.ds(G * GROUP, GROUP)], -1.0, 1.0, ALU.mult,
                                  ALU.add).then_inc(gates_done, 1)
                dve.memset(memory[:, :, DH + 1:MZ], 0.0)
                dve.memset(memory[:, :, 0:DH], 0.0).then_inc(memory_done, 1)
                dve.memset(memory[:, :, DH:DH + 1], -1.0 / DH).then_inc(memory_done, 1)
                for x, (kind, m) in enumerate(JOBS):
                    if kind == "q":
                        feature_map(2 * CHAINS * G + CHAINS + m, m, (1, 2)).then_inc(sigma_done, 1)
                    if kind == "v":
                        dve.wait_ge(v_ready, NT * G + m + 1)
                        dve.tensor_copy(v[:, m, :], work[x % 4][:]).then_inc(v_done, 1)
                for seg in range(SEGS):
                    for b in range(B):
                        deltas(G, seg, b)
                    maximum(G, seg)
                    if seg < SEGS - 1:
                        for b in range(B):
                            remember(G, seg, b)
                    normalise(G, seg)
                mix(G, 0)
                for m in range(1, CHAINS):
                    mix(G, m)
                    if more:
                        k_feature_map(G + 1, m - 1)
                low_part(G, 0)
                low_part(G, 1)
                if more:
                    k_feature_map(G + 1, CHAINS - 1)
                    k_sides(G + 1, range(4))
                low_part(G, 2)
                if more:
                    k_sides(G + 1, range(4, CHAINS))
                low_part(G, 3)
                if more:
                    low_parts(G + 1)
                dve.wait_ge(out_done, signals(o_parts * (G + 1)))
                dve.wait_ge(x_reloaded, 16 * B * GROUP * GROUPS)
                for b in range(B):
                    tile = res.x[:, bass.ds(b * GROUPS + G, 1), :].rearrange("p a d -> p (a d)")
                    dve.tensor_tensor(tile, memory_bank[b][:, 0, 0:D], tile, ALU.add).then_inc(x_added, 1)

            for m in range(CHAINS):
                k_feature_map(0, m)
                if m == 1:
                    low_parts(0)
            k_sides(0, range(CHAINS))
            groups(dve, group)


class Residual:

    def __init__(self, nc, ctx):
        sb = lambda what, shape, dt=F32: ctx.enter_context(nc.sbuf_tensor(what, shape, dt))
        self.x = sb("x", [P, NT, D])
        self.xh, self.xl = sb("xn_t_hi", [P, DC, TOK], F32R), sb("xn_t_lo", [P, DC, TOK], F32R)
        self.ident = sb("ident", [P, P])
        self.ident_bf = sb("ident_bf", [P, P], BF16)
        self.causal = sb("causal", [P, P], BF16)
        self.zeros = sb("zeros", [P, HALF], BF16)
        self.zero = sb("zero", [P, 1])
        self.iota = sb("iota", [P, NT, N_EXP])


def load_stage(nc, res, x, consts):
    with ExitStack() as ctx:
        loaded = ctx.enter_context(nc.semaphore("start_loaded"))
        made = ctx.enter_context(nc.semaphore("constants_made"))
        block = ctx.enter_context(nc.Block())

        @block.sync
        def _(sp):
            sp.dma_start(res.ident[:], consts["ident"]).then_inc(loaded, 16)
            sp.dma_start(res.x[:], x.rearrange("b (t p) d -> p (b t) d", p=P)).then_inc(loaded, 16)
            sp.dma_start(res.iota[:], consts["iota"]).then_inc(loaded, 16)
            sp.wait_ge(loaded, 48)

        @block.vector
        def _(dve):
            dve.memset(res.zeros[:], 0.0).then_inc(made, 1)
            dve.wait_ge(loaded, 48)
            dve.tensor_copy(res.ident_bf[:], res.ident[:]).then_inc(made, 1)

        @block.gpsimd
        def _(pool):
            pool.memset(res.causal[:], 0.0).then_inc(made, 1)
            pool.memset(res.zero[:], 0.0).then_inc(made, 1)
            pool.wait_ge(made, 4)
            pool.affine_select(out=res.causal[:], in_=res.causal[:], compare_op=ALU.is_ge, fill=NEG,
                               base=0, pattern=[[-1, P]], channel_multiplier=1).then_inc(made, 1)
            pool.wait_ge(made, 5)


def store_stage(nc, res, out):
    with ExitStack() as ctx:
        stored = ctx.enter_context(nc.semaphore("stored"))
        block = ctx.enter_context(nc.Block())

        @block.sync
        def _(sp):
            sp.dma_start(out.rearrange("b (t p) d -> p (b t) d", p=P), res.x[:]).then_inc(stored, 16)
            sp.wait_ge(stored, 16)


STAGES = ['L0_attn_a', 'L0_ffn', 'L0_attn_b', 'L0_ffn', 'L1_attn_a', 'L1_ffn', 'L1_attn_b', 'L1_ffn']


def build_program(nc, t, out, stages=STAGES):
    with ExitStack() as ctx:
        res = Residual(nc, ctx)
        t = {**t, "x_mid": nc.dram_tensor("x_mid", (B, S, D), F32, kind="Internal").ap()}
        load_stage(nc, res, t["x"], t)
        for n, kind in enumerate(stages):
            name = f"s{n}"
            if kind == "L0_attn_a":
                recurrent_stage(nc, name, res, t)
            if kind == "L0_ffn":
                ffn_stage(nc, name, res, t["ffn0"], t["gate0"], True, False)
            if kind == "L0_attn_b":
                wide_stage(nc, name, res, t)
            if kind == "L1_attn_a":
                causal_gqa_stage(nc, name, res, t)
            if kind == "L1_attn_b":
                rms_gqa_stage(nc, name, res, t)
            if kind == "L1_ffn":
                ffn_stage(nc, name, res, t["ffn1"], t["gate1"], False, True)
        store_stage(nc, res, out)



def ffn_layout(np, gate, up, down, owners):
    n = -(-len(owners) // P)
    whole = np.zeros((n, P, FFN_COLS), np.float32)
    for k in range(n):
        at = slice(k * P, min((k + 1) * P, len(owners)))
        m = at.stop - at.start
        for c in range(DC):
            whole[k, :, W_GATE + c * P:W_GATE + c * P + m] = gate[at, c * P:(c + 1) * P].T
            whole[k, :, W_UP + c * P:W_UP + c * P + m] = up[at, c * P:(c + 1) * P].T
        whole[k, :m, W_DOWN:W_DOWN + D] = down[at]
        whole[k, owners[at], W_SEL + np.arange(m)] = 1.0
    return whole


def router_layout(np, *rows):
    gates = np.zeros((GATES, D), np.float32)
    at = 0
    for r in rows:
        gates[at:at + len(r)] = r
        at += len(r)
    return np.ascontiguousarray(gates.T.reshape(DC, P, GATES).transpose(1, 0, 2))


def slots(np, a):
    whole = np.zeros((*a.shape[:-2], KV_HEADS, SLOT), a.dtype)
    whole[..., :HD] = a
    return whole.reshape(*a.shape[:-2], P)


def gqa_layout(np, wq, wk, wv, wo):
    chunked = lambda w: w.reshape(*w.shape[:-2], DC, P, P).swapaxes(-3, -2).reshape(*w.shape[:-2], P, DC * P)
    q = slots(np, wq.reshape(D, KV_HEADS, PER_KV, HD).transpose(2, 0, 1, 3))
    o = slots(np, wo.T.reshape(D, KV_HEADS, PER_KV, HD).transpose(2, 0, 1, 3)).transpose(0, 2, 1)
    kv = [chunked(slots(np, w.reshape(D, KV_HEADS, HD))).reshape(P, DC, P) for w in (wv, wk)]
    return np.concatenate([chunked(q), o], 2), np.stack(kv, 2).reshape(P, GK_COLS)


def layout(np, i):
    owners = lambda shared: np.concatenate([np.repeat(np.arange(N_EXP), INTER), np.full(shared, N_EXP)])
    w13, gu, w1 = i["L0_ffn_w13"], i["L0_ffn_shared_gate_up_w"], i["L1_ffn_w1"]
    t = {
        "x": i["L0_attn_a_x"],
        "ident": np.eye(P, dtype=np.float32),
        "iota": np.ascontiguousarray(np.broadcast_to(np.arange(N_EXP, dtype=np.float32), (P, NT, N_EXP))),
        "gate0": router_layout(np, i["L0_ffn_gate_w"], i["L0_ffn_shared_gate_w"]),
        "gate1": router_layout(np, i["L1_ffn_gate_w"]),
        "ffn0": ffn_layout(
            np, np.concatenate([w13[:, :INTER].reshape(-1, D), gu[:SHARED0]]),
            np.concatenate([w13[:, INTER:].reshape(-1, D), gu[SHARED0:]]),
            np.concatenate([i["L0_ffn_w2"].transpose(0, 2, 1).reshape(-1, D), i["L0_ffn_shared_down_w"].T]),
            owners(SHARED0)),
        "ffn1": ffn_layout(
            np, np.concatenate([w1[:, :, :INTER].transpose(0, 2, 1).reshape(-1, D), i["L1_ffn_sw1"]]),
            np.concatenate([w1[:, :, INTER:].transpose(0, 2, 1).reshape(-1, D), i["L1_ffn_sw2"]]),
            np.concatenate([i["L1_ffn_w2"].reshape(-1, D), i["L1_ffn_sw3"].T]),
            owners(SHARED1)),
    }
    grouped = lambda w: w.reshape(DC, P, GROUPS, WIDE).transpose(2, 1, 0, 3).reshape(GROUPS, P, DC * WIDE)
    grouped_out = lambda w: w.reshape(GROUPS, GROUP, DH, D).transpose(0, 2, 1, 3).reshape(GROUPS, DH, GROUP * D)
    for n in "kqv":
        t[f"wa_{n}"] = grouped(i[f"L0_attn_a_W{n}"])
    t["wa_o"] = grouped_out(i["L0_attn_a_Wo"])
    t["ba_gate"] = i["L0_attn_a_betas"][0, :, 0, :].T
    t["wb_q"] = i["L0_attn_b_Wq"].reshape(DC, P, HEADS * DH).transpose(1, 0, 2)
    t["wb_k"], t["wb_v"] = grouped(i["L0_attn_b_Wk"]), grouped(i["L0_attn_b_Wv"])
    t["wb_o"] = grouped_out(i["L0_attn_b_Wo"])
    t["bb_q"] = i["L0_attn_b_bq"].reshape(HEADS, DH).T
    t["bb_k"] = i["L0_attn_b_bk"].reshape(GROUPS, GROUP, DH).transpose(0, 2, 1)
    t["bb_v"] = i["L0_attn_b_bv"].reshape(GROUPS, WIDE)
    t["bb_o"] = i["L0_attn_b_bo"]
    wq, wk, wv, wo = (i[f"L1_attn_a_W{n}"].T for n in "qkvo")
    t["wc_q"], t["wc_kv"] = gqa_layout(np, wq, wk, wv, wo)
    t["bc_q"] = slots(np, i["L1_attn_a_bq"].reshape(KV_HEADS, PER_KV, HD).transpose(1, 0, 2)).T
    t["bc_k"] = slots(np, i["L1_attn_a_bk"].reshape(KV_HEADS, HD))[:, None]
    t["bc_v"] = slots(np, i["L1_attn_a_bv"].reshape(KV_HEADS, HD))
    t["bc_o"] = i["L1_attn_a_bo"]
    inverse = np.float32(10000.0) ** (-2.0 * np.arange(HD // 2, dtype=np.float32) / HD).astype(np.float32)
    theta = np.arange(S, dtype=np.float32)[:, None] * inverse[None, :]
    both = np.concatenate([np.cos(theta) + np.sin(theta)] * 2, 1).astype(np.float32)
    by_slot = lambda table: slots(np, np.broadcast_to(table[:, None, :], (S, KV_HEADS, HD))).T
    t["turn_k"] = by_slot(both)
    t["turn_q"] = t["turn_k"] * np.float32(HD ** -0.5)
    wq, wk, wv, wo = (i[f"L1_attn_b_W{n}"] for n in ("q", "k", "v", "out"))
    t["wd_q"], t["wd_kv"] = gqa_layout(np, wq, wk, wv, wo)
    fraction = np.arange(0, HD, 2, dtype=np.float32) / np.float32(HD)
    sinusoid = np.arange(S, dtype=np.float32)[:, None] * (np.float32(1.0) / np.float32(10000.0) ** fraction)[None, :]
    t["cos"], t["sin"] = (by_slot(np.concatenate([f(sinusoid)] * 2, 1).astype(np.float32)) for f in (np.cos, np.sin))
    turn = np.zeros((SLOT, SLOT), np.float32)
    half = HD // 2
    turn[half + np.arange(half), np.arange(half)] = -1.0
    turn[np.arange(half), half + np.arange(half)] = 1.0
    t["half_turn"] = np.kron(np.eye(KV_HEADS, dtype=np.float32), turn)
    t["v_ones"] = np.tile(np.arange(SLOT) == HD, KV_HEADS).astype(np.float32)
    t["sum_sel"] = np.kron(np.eye(KV_HEADS, dtype=np.float32), np.outer(np.arange(SLOT) == HD, np.ones(SLOT)).astype(np.float32))
    return t


def kernel(**inputs):
    import numpy as np
    import concourse.bacc as bacc
    from concourse.bass_utils import run_bass_kernel_spmd

    nc = bacc.Bacc("TRN2", target_bir_lowering=False, num_devices=1)
    arrays, tensors = {}, {}
    for name, a in layout(np, {k: np.asarray(v) for k, v in inputs.items()}).items():
        a = np.ascontiguousarray(a)
        arrays[f"in_{name}"] = a
        tensors[name] = nc.dram_tensor(f"in_{name}", a.shape, mybir.dt.from_np(a.dtype), kind="ExternalInput").ap()
    out = nc.dram_tensor("out_x", (B, S, D), F32, kind="ExternalOutput").ap()
    build_program(nc, tensors, out)
    return run_bass_kernel_spmd(nc, [arrays], core_ids=[0]).results[0]["out_x"]
```
